# Optimizing a Trainium2 kernel written in Bass

```python
import numpy as np
import jax
import jax.numpy as jnp

def _softmax(x, axis=-1):
    return jax.nn.softmax(x, axis=axis)

def _gelu(x):
    return jax.nn.gelu(x, approximate=True)

def _silu(x):
    return jax.nn.silu(x)

def _sigmoid(x):
    return jax.nn.sigmoid(x)

def _layernorm(x, axis=-1, eps=1e-05):
    m = jnp.mean(x, axis=axis, keepdims=True)
    v = jnp.var(x, axis=axis, keepdims=True)
    return (x - m) / jnp.sqrt(v + eps)

def _scatter_add(tgt, idx, src, axis=0):
    return tgt.at[idx].add(src)

def _segment_sum(src, seg, n):
    return jax.ops.segment_sum(src, seg, n)
kernel_name = 'mk_seq_preln_d2_jaxref_r4_9938b0'

def setup_inputs(seed: int=0):
    np.random.seed(seed)
    _w = jnp.asarray

    def _L0_attn_setup():
        import jax, jax.numpy as jnp
        import numpy as np
        import math
        D_MODEL = 256
        N_HEADS = 16
        D_HEAD = D_MODEL // N_HEADS
        WINDOW = 64
        SCALE = 1.0 / math.sqrt(D_HEAD)

        def _window_mask(seq_len: int) -> jnp.ndarray:
            i = jnp.arange(seq_len)[:, None]
            j = jnp.arange(seq_len)[None, :]
            allowed = (j <= i) & (j > i - WINDOW)
            return jnp.where(allowed, 0.0, -jnp.inf).astype(jnp.float32)
        key = jax.random.key(seed)
        kx, kqkv, kout = jax.random.split(key, 3)
        x = jax.random.normal(kx, (2, 512, D_MODEL), dtype=jnp.float32)
        lim_qkv = math.sqrt(6.0 / (D_MODEL + 3 * D_MODEL))
        W_qkv = jax.random.uniform(kqkv, (D_MODEL, 3 * D_MODEL), dtype=jnp.float32, minval=-lim_qkv, maxval=lim_qkv)
        lim_out = math.sqrt(6.0 / (D_MODEL + D_MODEL))
        W_out = jax.random.uniform(kout, (D_MODEL, D_MODEL), dtype=jnp.float32, minval=-lim_out, maxval=lim_out)
        return {'x': x, 'W_qkv': W_qkv, 'W_out': W_out}
    _L0_attn_in = _L0_attn_setup()

    def _L0_ffn_setup():
        import jax, jax.numpy as jnp
        import numpy as np
        B, T, D, H = (4, 512, 256, 512)
        E, S, K = (8, 2, 2)

        def _swiglu_stacked(x, w1, b1, w2, b2, w3, b3):
            p1 = jnp.einsum('btd,ndh->nbth', x, w1) + b1[:, None, None, :]
            p2 = jnp.einsum('btd,ndh->nbth', x, w2) + b2[:, None, None, :]
            glu = jax.nn.silu(p1) * p2
            return jnp.einsum('nbth,nhd->nbtd', glu, w3) + b3[:, None, None, :]
        key = jax.random.key(seed)
        ks = jax.random.split(key, 10)
        s = 0.02
        return {'x': jax.random.normal(ks[0], (B, T, D), jnp.float32), 'gate_w': jax.random.normal(ks[1], (D, E), jnp.float32) * s, 'gate_b': jnp.zeros((E,), jnp.float32), 'rw1': jax.random.normal(ks[2], (E, D, H), jnp.float32) * s, 'rb1': jnp.zeros((E, H), jnp.float32), 'rw2': jax.random.normal(ks[3], (E, D, H), jnp.float32) * s, 'rb2': jnp.zeros((E, H), jnp.float32), 'rw3': jax.random.normal(ks[4], (E, H, D), jnp.float32) * s, 'rb3': jnp.zeros((E, D), jnp.float32), 'sw1': jax.random.normal(ks[5], (S, D, H), jnp.float32) * s, 'sb1': jnp.zeros((S, H), jnp.float32), 'sw2': jax.random.normal(ks[6], (S, D, H), jnp.float32) * s, 'sb2': jnp.zeros((S, H), jnp.float32), 'sw3': jax.random.normal(ks[7], (S, H, D), jnp.float32) * s, 'sb3': jnp.zeros((S, D), jnp.float32)}
    _L0_ffn_in = _L0_ffn_setup()

    def _L1_attn_setup():
        import jax, jax.numpy as jnp
        import numpy as np
        LN_EPS = 1e-05
        NUM_HEAD = 16
        key = jax.random.key(seed)
        ks = jax.random.split(key, 10)
        B, S, E = (2, 512, 256)
        sc = 0.02
        return {'x': jax.random.normal(ks[0], (B, S, E), jnp.float32), 'wq': jax.random.normal(ks[1], (E, E), jnp.float32) * sc, 'bq': jax.random.normal(ks[2], (E,), jnp.float32) * sc, 'wk': jax.random.normal(ks[3], (E, E), jnp.float32) * sc, 'bk': jax.random.normal(ks[4], (E,), jnp.float32) * sc, 'wv': jax.random.normal(ks[5], (E, E), jnp.float32) * sc, 'bv': jax.random.normal(ks[6], (E,), jnp.float32) * sc, 'wo': jax.random.normal(ks[7], (E, E), jnp.float32) * sc, 'bo': jax.random.normal(ks[8], (E,), jnp.float32) * sc, 'gamma': jnp.ones((E,), jnp.float32), 'beta': jnp.zeros((E,), jnp.float32)}
    _L1_attn_in = _L1_attn_setup()

    def _L1_ffn_setup():
        import jax, jax.numpy as jnp
        import numpy as np
        SINKHORN_ITERS = 8
        TEMPERATURE = 1.0
        EPS = 1e-06

        def sinkhorn(t):
            t = jnp.log(jnp.clip(t, EPS)) / TEMPERATURE
            for _ in range(SINKHORN_ITERS):
                t = t - jax.nn.logsumexp(t, axis=-2, keepdims=True)
                t = t - jax.nn.logsumexp(t, axis=-1, keepdims=True)
            return jnp.exp(t)
        key = jax.random.key(seed)
        k1, k2, k3 = jax.random.split(key, 3)
        B, N, D, E = (4, 1024, 256, 8)
        x = jax.random.normal(k1, (B, N, D), dtype=jnp.float32)
        gate_w = jax.random.normal(k2, (D, E), dtype=jnp.float32) * D ** (-0.5)
        experts = jax.random.normal(k3, (E, D, D), dtype=jnp.float32) * D ** (-0.5)
        return {'x': x, 'gate_w': gate_w, 'experts': experts}
    _L1_ffn_in = _L1_ffn_setup()
    _d = {'L0_attn_x': _L0_attn_in['x'], 'L0_attn_W_qkv': _L0_attn_in['W_qkv'], 'L0_attn_W_out': _L0_attn_in['W_out'], 'L0_ffn_gate_w': _L0_ffn_in['gate_w'], 'L0_ffn_gate_b': _L0_ffn_in['gate_b'], 'L0_ffn_rw1': _L0_ffn_in['rw1'], 'L0_ffn_rb1': _L0_ffn_in['rb1'], 'L0_ffn_rw2': _L0_ffn_in['rw2'], 'L0_ffn_rb2': _L0_ffn_in['rb2'], 'L0_ffn_rw3': _L0_ffn_in['rw3'], 'L0_ffn_rb3': _L0_ffn_in['rb3'], 'L0_ffn_sw1': _L0_ffn_in['sw1'], 'L0_ffn_sb1': _L0_ffn_in['sb1'], 'L0_ffn_sw2': _L0_ffn_in['sw2'], 'L0_ffn_sb2': _L0_ffn_in['sb2'], 'L0_ffn_sw3': _L0_ffn_in['sw3'], 'L0_ffn_sb3': _L0_ffn_in['sb3'], 'L1_attn_wq': _L1_attn_in['wq'], 'L1_attn_bq': _L1_attn_in['bq'], 'L1_attn_wk': _L1_attn_in['wk'], 'L1_attn_bk': _L1_attn_in['bk'], 'L1_attn_wv': _L1_attn_in['wv'], 'L1_attn_bv': _L1_attn_in['bv'], 'L1_attn_wo': _L1_attn_in['wo'], 'L1_attn_bo': _L1_attn_in['bo'], 'L1_attn_gamma': _L1_attn_in['gamma'], 'L1_attn_beta': _L1_attn_in['beta'], 'L1_ffn_gate_w': _L1_ffn_in['gate_w'], 'L1_ffn_experts': _L1_ffn_in['experts']}
    _x0 = _d['L0_attn_x']
    _d['L0_attn_x'] = jax.random.normal(jax.random.fold_in(jax.random.key(seed), 1), (4, 1024, 256), dtype=_x0.dtype)
    del _x0
    return _d

def reference(L0_attn_x, L0_attn_W_qkv, L0_attn_W_out, L0_ffn_gate_w, L0_ffn_gate_b, L0_ffn_rw1, L0_ffn_rb1, L0_ffn_rw2, L0_ffn_rb2, L0_ffn_rw3, L0_ffn_rb3, L0_ffn_sw1, L0_ffn_sb1, L0_ffn_sw2, L0_ffn_sb2, L0_ffn_sw3, L0_ffn_sb3, L1_attn_wq, L1_attn_bq, L1_attn_wk, L1_attn_bk, L1_attn_wv, L1_attn_bv, L1_attn_wo, L1_attn_bo, L1_attn_gamma, L1_attn_beta, L1_ffn_gate_w, L1_ffn_experts):

    def _L0_attn_ref(x, W_qkv, W_out):
        import jax, jax.numpy as jnp
        import numpy as np
        import math
        D_MODEL = 256
        N_HEADS = 16
        D_HEAD = D_MODEL // N_HEADS
        WINDOW = 64
        SCALE = 1.0 / math.sqrt(D_HEAD)

        def _window_mask(seq_len: int) -> jnp.ndarray:
            i = jnp.arange(seq_len)[:, None]
            j = jnp.arange(seq_len)[None, :]
            allowed = (j <= i) & (j > i - WINDOW)
            return jnp.where(allowed, 0.0, -jnp.inf).astype(jnp.float32)
        B, S, _ = x.shape
        qkv = x @ W_qkv
        qkv = qkv.reshape(B, S, 3, N_HEADS, D_HEAD)
        qkv = jnp.transpose(qkv, (2, 0, 3, 1, 4))
        q, k, v = (qkv[0], qkv[1], qkv[2])
        scores = jnp.einsum('bhsd,bhtd->bhst', q, k) * SCALE
        scores = scores + _window_mask(S)[None, None]
        weights = jax.nn.softmax(scores, axis=-1)
        out = jnp.einsum('bhst,bhtd->bhsd', weights, v)
        out = jnp.transpose(out, (0, 2, 1, 3)).reshape(B, S, D_MODEL)
        return out @ W_out

    def _L0_ffn_ref(x, gate_w, gate_b, rw1, rb1, rw2, rb2, rw3, rb3, sw1, sb1, sw2, sb2, sw3, sb3):
        import jax, jax.numpy as jnp
        import numpy as np
        B, T, D, H = (4, 512, 256, 512)
        E, S, K = (8, 2, 2)

        def _swiglu_stacked(x, w1, b1, w2, b2, w3, b3):
            p1 = jnp.einsum('btd,ndh->nbth', x, w1) + b1[:, None, None, :]
            p2 = jnp.einsum('btd,ndh->nbth', x, w2) + b2[:, None, None, :]
            glu = jax.nn.silu(p1) * p2
            return jnp.einsum('nbth,nhd->nbtd', glu, w3) + b3[:, None, None, :]
        scores = jax.nn.softmax(x @ gate_w + gate_b, axis=-1)
        weights, indices = jax.lax.top_k(scores, K)
        routed_all = _swiglu_stacked(x, rw1, rb1, rw2, rb2, rw3, rb3)
        out_bted = jnp.transpose(routed_all, (1, 2, 0, 3))
        gathered = jnp.take_along_axis(out_bted, indices[..., None], axis=2)
        routed = jnp.sum(weights[..., None] * gathered, axis=2)
        shared = _swiglu_stacked(x, sw1, sb1, sw2, sb2, sw3, sb3).mean(axis=0)
        return shared + routed

    def _L1_attn_ref(x, wq, bq, wk, bk, wv, bv, wo, bo, gamma, beta):
        import jax, jax.numpy as jnp
        import numpy as np
        LN_EPS = 1e-05
        NUM_HEAD = 16
        B, S, E = x.shape
        H = NUM_HEAD
        D = E // H
        Q = x @ wq + bq
        K = x @ wk + bk
        V = x @ wv + bv
        Q = Q.reshape(B * H, S, D)
        K = K.reshape(B * H, S, D)
        V = V.reshape(B * H, S, D)
        scores = jnp.einsum('bqd,bkd->bqk', Q, K) / jnp.sqrt(jnp.float32(D))
        attn = jax.nn.softmax(scores, axis=-1)
        ctx = jnp.einsum('bqk,bkd->bqd', attn, V)
        ctx = ctx.reshape(B, S, E)
        out = ctx @ wo + bo
        out = out + x
        mu = jnp.mean(out, axis=-1, keepdims=True)
        var = jnp.var(out, axis=-1, keepdims=True)
        out = (out - mu) * jax.lax.rsqrt(var + LN_EPS) * gamma + beta
        return out

    def _L1_ffn_ref(x, gate_w, experts):
        import jax, jax.numpy as jnp
        import numpy as np
        SINKHORN_ITERS = 8
        TEMPERATURE = 1.0
        EPS = 1e-06

        def sinkhorn(t):
            t = jnp.log(jnp.clip(t, EPS)) / TEMPERATURE
            for _ in range(SINKHORN_ITERS):
                t = t - jax.nn.logsumexp(t, axis=-2, keepdims=True)
                t = t - jax.nn.logsumexp(t, axis=-1, keepdims=True)
            return jnp.exp(t)
        B, N, D = x.shape
        E = gate_w.shape[-1]
        M = N // E
        gate_logits = jnp.einsum('bnd,de->bne', x, gate_w)
        competitive_gates = sinkhorn(gate_logits)
        vals, idx = jax.lax.top_k(jnp.swapaxes(competitive_gates, -1, -2), M)
        gate_values = jnp.swapaxes(vals, -1, -2)
        routed_indices = jnp.swapaxes(idx, -1, -2)
        b_idx = jnp.arange(B)[:, None, None]
        routed = x[b_idx, routed_indices]
        routed = jnp.transpose(routed, (2, 0, 1, 3))
        outputs = jnp.einsum('ebmd,edf->ebmf', routed, experts)
        outputs = outputs * jnp.transpose(gate_values, (2, 0, 1))[..., None]
        vals_bmed = jnp.transpose(outputs, (1, 2, 0, 3))
        routed_back = jnp.zeros_like(x).at[b_idx, routed_indices].set(vals_bmed)
        return routed_back
    x = L0_attn_x
    x = x + _L0_attn_ref(_layernorm(x, axis=-1), L0_attn_W_qkv, L0_attn_W_out)
    x = x + _L0_ffn_ref(_layernorm(x, axis=-1), L0_ffn_gate_w, L0_ffn_gate_b, L0_ffn_rw1, L0_ffn_rb1, L0_ffn_rw2, L0_ffn_rb2, L0_ffn_rw3, L0_ffn_rb3, L0_ffn_sw1, L0_ffn_sb1, L0_ffn_sw2, L0_ffn_sb2, L0_ffn_sw3, L0_ffn_sb3)
    x = x + _L1_attn_ref(_layernorm(x, axis=-1), L1_attn_wq, L1_attn_bq, L1_attn_wk, L1_attn_bk, L1_attn_wv, L1_attn_bv, L1_attn_wo, L1_attn_bo, L1_attn_gamma, L1_attn_beta)
    x = x + _L1_ffn_ref(_layernorm(x, axis=-1), L1_ffn_gate_w, L1_ffn_experts)
    return x

_drawn_inputs = setup_inputs


def setup_inputs(seed=0):
    import zlib

    import numpy as np

    out = dict(_drawn_inputs(seed))
    spreads = {'L0_ffn_gate_b': (0.0, 0.1),
     'L0_ffn_rb1': (0.0, 0.371),
     'L0_ffn_rb2': (0.0, 0.444),
     'L0_ffn_rb3': (0.0, 0.1),
     'L0_ffn_sb1': (0.0, 0.1),
     'L0_ffn_sb2': (0.0, 0.27),
     'L0_ffn_sb3': (0.0, 0.1),
     'L1_attn_gamma': (1.0, 0.2),
     'L1_attn_beta': (0.0, 0.1)}
    factors = {'L1_attn_wq': 8.0,
     'L1_attn_bq': 8.0,
     'L1_attn_wk': 8.0,
     'L1_attn_bk': 8.0,
     'L1_attn_wv': 3.063,
     'L1_attn_bv': 7.616,
     'L1_attn_wo': 3.5}
    for name, (base, spread) in spreads.items():
        noise = np.random.default_rng([zlib.crc32(name.encode()), seed]).standard_normal(out[name].shape)
        drawn = base * np.exp(spread * noise) if base else spread * noise
        out[name] = jnp.asarray(drawn.astype(out[name].dtype))
    for name, factor in factors.items():
        out[name] = (out[name] * factor).astype(out[name].dtype)
    return out
```

```python
import concourse.bass as bass
from concourse import mybir
from contextlib import ExitStack, contextmanager

F32 = mybir.dt.float32
F32R = mybir.dt.float32r
BF16 = mybir.dt.bfloat16
F16 = mybir.dt.float16
U32 = mybir.dt.uint32
I32 = mybir.dt.int32
ALU = mybir.AluOpType
ACT = mybir.ActivationFunctionType
AX = mybir.AxisListType

P = 128
B, S, D = 4, 1024, 256
N = B * S
T = N // P
TB = S // P
KD = D // P
NH, DH = 16, 16
SCALE = DH ** -0.5
WIN = 64
LN_EPS = 1e-5
ONE = 1
NEG = -1e30
BN = 6


class Shared:

    def __init__(self, ctx, ins):
        self.ctx, self.ins = ctx, ins


class Chain:

    def __init__(self, eng, sem):
        self.eng, self.sem, self.count = eng, sem, ONE

    def __call__(self, ins):
        ins.then_inc(self.sem, 1)
        self.count += 1
        self.eng.wait_ge(self.sem, self.count)


@contextmanager
def phase(nc):
    sems = []
    with ExitStack() as e:
        def semaphore(name, start=ONE):
            sem = e.enter_context(nc.semaphore(name))
            sems.append((sem, start))
            return sem

        def begin():
            with nc.Block() as block:
                @block.sync
                def _(sp):
                    for sem, _ in sems:
                        sp.sem_clear(sem)
                    for sem, start in sems:
                        if start:
                            sp.sem_inc(sem, start)
            return e.enter_context(nc.Block())

        yield e, semaphore, begin


def setup(nc, g):
    c = g.ctx
    sb = lambda name, shape, dt=F32: c.enter_context(nc.sbuf_tensor(name, shape, dt))
    g.x = sb("x", [P, T, D])
    g.stats = sb("stats", [P, T, BN])
    g.mean = sb("mean", [P, T])
    g.rstd = sb("rstd", [P, T])
    g.ident = sb("ident", [P, P])
    g.bank2 = [c.enter_context(nc.psum_tensor(f"banks{i}", [P, 1024], F32)) for i in range(4)]
    g.bank = [g.bank2[i // 2][:, 512 * (i % 2):512 * (i % 2 + 1)] for i in range(8)]
    with phase(nc) as (e, semaphore, begin):
        x_in = [semaphore(f"x_in{b}") for b in range(B)]
        ident_zero = semaphore("ident_zero")
        ident_set = semaphore("ident_set")
        stats_done = semaphore("stats0_done")
        block = begin()

        @block.sync
        def _(sp):
            for b in range(B):
                src = g.ins["L0_attn_x"][b].rearrange("(t p) d -> p t d", p=P)
                sp.dma_start(g.x[:, b * TB:(b + 1) * TB, :], src).then_inc(x_in[b], 16)

        @block.gpsimd
        def _(pool):
            nc.gpsimd.memset(g.ident[:], 0.0).then_inc(ident_zero, 1)
            pool.wait_ge(ident_zero, ONE + 1)
            nc.gpsimd.affine_select(out=g.ident[:], in_=g.ident[:], compare_op=ALU.not_equal, fill=1.0, base=0,
                                    pattern=[[-1, P]], channel_multiplier=1).then_inc(ident_set, 1)

        @block.vector
        def _(dve):
            for b in range(B):
                dve.wait_ge(x_in[b], ONE + 16)
                with dve.Fori(b * TB, (b + 1) * TB) as t:
                    nc.vector.bn_stats(g.stats[:, bass.ds(t, 1), :], g.x[:, bass.ds(t, 1), :]).then_inc(stats_done, 1)


def finish_stats(nc, g, name):
    with phase(nc) as (e, semaphore, begin):
        sb = lambda n, shape, dt=F32: e.enter_context(nc.sbuf_tensor(f"{name}_{n}", shape, dt))
        diff, var, std = sb("diff", [P, T]), sb("var", [P, T]), sb("std", [P, T])
        eps = sb("eps", [P, 1])
        step = semaphore(f"{name}_step")
        var_ready = semaphore(f"{name}_var_ready")
        std_ready = semaphore(f"{name}_std_ready")
        rstd_ready = semaphore(f"{name}_rstd_ready")
        block = begin()
        half = float(D // 2)

        @block.vector
        def _(dve):
            link = Chain(dve, step)
            even, odd = g.stats[:, :, 1], g.stats[:, :, 4]
            nc.vector.memset(eps[:], LN_EPS)
            nc.vector.tensor_tensor(g.mean[:], even, odd, ALU.add)
            nc.vector.tensor_tensor(var[:], g.stats[:, :, 2], g.stats[:, :, 5], ALU.add)
            link(nc.vector.tensor_tensor(diff[:], even, odd, ALU.subtract))
            link(nc.vector.scalar_tensor_tensor(diff[:], diff[:], half / 2.0, diff[:], ALU.mult, ALU.mult))
            link(nc.vector.tensor_tensor(var[:], var[:], diff[:], ALU.add))
            nc.vector.tensor_scalar(var[:], var[:], 1.0 / D, None, ALU.mult).then_inc(var_ready, 1)
            link(nc.vector.tensor_scalar(g.mean[:], g.mean[:], 0.5, None, ALU.mult))
            dve.wait_ge(std_ready, ONE + 1)
            nc.vector.reciprocal(g.rstd[:], std[:]).then_inc(rstd_ready, 1)

        @block.scalar
        def _(act):
            act.wait_ge(var_ready, ONE + 1)
            nc.scalar.activation(std[:], var[:], ACT.Sqrt, bias=eps[:, 0:1]).then_inc(std_ready, 1)


def window_attention(nc, g):
    NP = T // 2
    HM = P // DH
    HU = 4
    NU = NH // HU
    R = P // HU
    W2 = 2 * WIN
    Q = P // 2
    with phase(nc) as (e, semaphore, begin):
        sb = lambda n, shape, dt=F32: e.enter_context(nc.sbuf_tensor(f"wa_{n}", shape, dt))
        sem = lambda n: semaphore(f"wa_{n}")
        wqkv = sb("wqkv", [P, KD, 3 * D])
        wo = sb("wo", [P, NU, D])
        ident_bf = sb("ident_bf", [P, P], BF16)
        mask0 = sb("mask0", [P, NP, W2], BF16)
        mask1 = sb("mask1", [P, W2], BF16)
        head_rows = sb("head_rows", [P, HM])
        sum_rows = sb("sum_rows", [P, P])
        xn = [sb(f"xn{s}", [P, D]) for s in range(2)]
        xnT = sb("xnT", [P, KD, WIN + 2 * P])
        kT = sb("kT", [P, KD, WIN + 2 * P])
        q_heads = sb("q_heads", [P, KD, HM, 2 * P])
        v = sb("v", [P, 4, NH, R])
        nmax = [sb(f"nmax{k}", [P, HU]) for k in range(2)]
        ex = [sb(f"ex{k}", [P, HU, W2]) for k in range(2)]
        prob = [sb(f"prob{k}", [P, HU, W2]) for k in range(2)]
        probT = [sb(f"probT{k}", [P, HU, P]) for k in range(2)]
        o = [sb(f"o{s}", [P, NU, P]) for s in range(2)]
        rsum = [sb(f"rsum{s}", [P, NU, P]) for s in range(2)]
        on = [sb(f"on{s}", [P, NU, P]) for s in range(2)]
        w_in, wo_zero, const = sem("w_in"), sem("wo_zero"), sem("const")
        consts_set, tails_zero, v_set = sem("consts_set"), sem("tails_zero"), sem("v_set")
        xn_ready, xnT_done, xnT_ready = sem("xn_ready"), sem("xnT_done"), sem("xnT_ready")
        qk_done, k_ready, q_ready, v_done, v_ready = sem("qk_done"), sem("k_ready"), sem("q_ready"), sem("v_done"), sem("v_ready")
        tails_moved = sem("tails_moved")
        s_done, max_ready, ex_ready, prob_ready, probT_done, probT_ready = [
            sem(n) for n in ("s_done", "max_ready", "ex_ready", "prob_ready", "probT_done", "probT_ready")]
        o_done, o_ready, sum_done, rsum_ready, on_ready, y_done, x_ready, stats_ready = [
            sem(n) for n in ("o_done", "o_ready", "sum_done", "rsum_ready", "on_ready", "y_done", "x_ready", "stats_ready")]
        b_pt, b_q, b_k, b_v, b_s = [g.bank[7], g.bank[0]], g.bank[1], g.bank[2], g.bank[3:5], g.bank[5:7]
        b_tp = b_pt
        block = begin()
        half = lambda n: slice(n * Q, (n + 1) * Q)

        @block.sync
        def _(sp):
            sp.dma_start(wqkv[:], g.ins["L0_attn_W_qkv"].rearrange("(k p) n -> p k n", p=P)).then_inc(w_in, 16)
            sp.wait_ge(wo_zero, ONE + 1)
            for j in range(HU):
                src = g.ins["L0_attn_W_out"].rearrange("(m j d) n -> j d m n", j=HU, d=DH)[j]
                sp.dma_start(wo[R * j:R * j + DH], src).then_inc(w_in, 16)

        @block.gpsimd
        def _(pool):
            link = Chain(pool, const)
            nc.gpsimd.memset(wo[:], 0.0).then_inc(wo_zero, 1)
            nc.gpsimd.memset(mask0[:], 0.0)
            nc.gpsimd.memset(mask1[:], 0.0)
            nc.gpsimd.memset(head_rows[:], 1.0)
            nc.gpsimd.memset(xnT[:, :, 0:WIN], 0.0)
            nc.gpsimd.memset(kT[:, :, 0:WIN], 0.0).then_inc(tails_zero, 1)
            link(nc.gpsimd.memset(sum_rows[:], 0.0))
            for h in range(2):
                for m, pat in ((mask0, [[0, NP]]), (mask1, [])):
                    m = m[half(h)]
                    link(nc.gpsimd.affine_select(out=m, in_=m, compare_op=ALU.is_ge, fill=NEG, base=WIN,
                                                 pattern=pat + [[-1, W2]], channel_multiplier=1))
                    link(nc.gpsimd.affine_select(out=m, in_=m, compare_op=ALU.is_ge, fill=NEG, base=-1,
                                                 pattern=pat + [[1, W2]], channel_multiplier=-1))
            m = mask0[half(0)].rearrange("p (b j) w -> p b j w", b=B)[:, :, 0, :]
            nc.gpsimd.affine_select(out=m, in_=m, compare_op=ALU.is_ge, fill=NEG, base=-WIN,
                                    pattern=[[0, B], [1, W2]], channel_multiplier=0)
            link(nc.gpsimd.affine_select(out=head_rows[:], in_=head_rows[:], compare_op=ALU.is_ge, fill=0.0, base=0,
                                         pattern=[[-DH, HM]], channel_multiplier=1))
            link(nc.gpsimd.affine_select(out=head_rows[:], in_=head_rows[:], compare_op=ALU.is_ge, fill=0.0,
                                         base=DH - 1, pattern=[[DH, HM]], channel_multiplier=-1))
            sr = sum_rows[:].rearrange("p (j r) -> p j r", j=HU)
            link(nc.gpsimd.affine_select(out=sr, in_=sr, compare_op=ALU.not_equal, fill=1.0, base=-DH,
                                         pattern=[[-R, HU], [0, R]], channel_multiplier=1))
            nc.gpsimd.tensor_copy(ident_bf[:], g.ident[:]).then_inc(consts_set, 1)

        @block.vector
        def _(dve):
            nc.vector.memset(v[:], 0.0).then_inc(max_ready, 1)
            dve.wait_ge(max_ready, ONE + 1)
            nc.vector.memset(v[:, :, :, DH:DH + 1], 1.0).then_inc(v_set, 1)
            dve.wait_ge(consts_set, ONE + 1)

            with dve.Fori(0, NP) as i:
                def normalise(s):
                    dve.wait_ge(sum_done, ONE + 2 * i + s + 1)
                    nc.vector.reciprocal(rsum[s][:], b_v[s][:].rearrange("p (m q) -> p m q", m=NU)).then_inc(rsum_ready, 1)
                    dve.wait_ge(rsum_ready, ONE + 2 * i + s + 1)
                    nc.vector.tensor_tensor(on[s][:], o[s][:], rsum[s][:], ALU.mult).then_inc(on_ready, 1)

                def residual(s):
                    xt = g.x[:, bass.ds(2 * i + s, 1), :].rearrange("p o d -> p (o d)")
                    dve.wait_ge(y_done, ONE + 2 * i + s + 1)
                    nc.vector.tensor_tensor(xt, (b_q, b_k)[s][:, 0:D], xt, ALU.add).then_inc(x_ready, 1)
                    dve.wait_ge(x_ready, ONE + 2 * i + s + 1)
                    nc.vector.bn_stats(g.stats[:, bass.ds(2 * i + s, 1), :], xt).then_inc(stats_ready, 1)

                for s in range(2):
                    t = 2 * i + s
                    dve.wait_ge(xnT_done, ONE + 2 * i)
                    nc.vector.tensor_scalar(xn[s][:], g.x[:, bass.ds(t, 1), :].rearrange("p o d -> p (o d)"),
                                            g.mean[:, bass.ds(t, 1)], g.rstd[:, bass.ds(t, 1)],
                                            ALU.subtract, ALU.mult).then_inc(xn_ready, 1)
                dve.wait_ge(qk_done, ONE + 2 * i + 1)
                dve.wait_ge(s_done, ONE + 2 * NU * i)
                for k in range(KD):
                    qb = b_q[:, 2 * P * k:2 * P * (k + 1)].unsqueeze(1).broadcast_to([P, HM, 2 * P])
                    hb = head_rows[:].unsqueeze(2).broadcast_to([P, HM, 2 * P])
                    nc.vector.tensor_tensor(q_heads[:, k], qb, hb, ALU.mult).then_inc(q_ready, 1)
                for u in range(2 * NU):
                    n = 2 * NU * i + u + 1
                    k = u % 2
                    sc = b_s[k][:].rearrange("p (h w) -> p h w", h=HU)
                    dve.wait_ge(s_done, ONE + n)
                    if u >= 2:
                        dve.wait_ge(prob_ready, ONE + n - 2)
                    else:
                        dve.wait_ge(prob_ready, ONE + 2 * NU * i)
                    nc.vector.tensor_reduce(nmax[k][:], sc, axis=AX.X, op=ALU.max, negate=True).then_inc(max_ready, 1)
                    dve.wait_ge(max_ready, ONE + n + 1)
                    nc.vector.tensor_tensor(ex[k][:], sc, nmax[k][:].unsqueeze(2).broadcast_to([P, HU, W2]),
                                            ALU.add).then_inc(ex_ready, 1)
                    if u == NU + 2:
                        normalise(0)
                    if u == NU + 3:
                        residual(0)
                normalise(1)
                residual(1)

        @block.scalar
        def _(act):
            act.wait_ge(tails_zero, ONE + 1)
            act.wait_ge(v_set, ONE + 1)
            with act.Fori(0, NP) as i:
                for s in range(2):
                    act.wait_ge(xnT_done, ONE + 2 * i + s + 1)
                    act.wait_ge(tails_moved, ONE + 2 * i)
                    nc.scalar.activation(xnT[:, :, WIN + P * s:WIN + P * (s + 1)],
                                         b_tp[s][:, 0:D].rearrange("p (k q) -> p k q", k=KD),
                                         ACT.Copy).then_inc(xnT_ready, 1)
                act.wait_ge(qk_done, ONE + 2 * i + 2)
                nc.scalar.activation(kT[:, :, WIN:WIN + 2 * P], b_k[:].rearrange("p (k q) -> p k q", k=KD),
                                     ACT.Copy).then_inc(k_ready, 1)
                for s in range(2):
                    act.wait_ge(v_done, ONE + 2 * i + s + 1)
                    act.wait_ge(o_done, ONE + 2 * i)
                    nc.scalar.activation(v[:, 2 * s:2 * s + 2, :, 0:DH],
                                         b_v[s][:].rearrange("p (a h d) -> p a h d", a=2, h=NH),
                                         ACT.Copy).then_inc(v_ready, 1)

                def transposed(u):
                    n = 2 * NU * i + u + 1
                    k = u % 2
                    act.wait_ge(probT_done, ONE + n)
                    nc.scalar.activation(probT[k][:], b_pt[k][:].rearrange("p (h q) -> p h q", h=HU),
                                         ACT.Copy).then_inc(probT_ready, 1)

                for u in range(2 * NU):
                    n = 2 * NU * i + u + 1
                    k = u % 2
                    act.wait_ge(ex_ready, ONE + n)
                    nc.scalar.activation(prob[k][:], ex[k][:], ACT.Exp, scale=SCALE).then_inc(prob_ready, 1)
                    if u >= 1:
                        transposed(u - 1)
                    if u == NU:
                        act.wait_ge(o_done, ONE + 2 * i + 1)
                        nc.scalar.activation(o[0][:], b_q[:].rearrange("p (m q) -> p m q", m=NU), ACT.Copy).then_inc(o_ready, 1)
                transposed(2 * NU - 1)
                act.wait_ge(o_done, ONE + 2 * i + 2)
                nc.scalar.activation(o[1][:], b_k[:].rearrange("p (m q) -> p m q", m=NU), ACT.Copy).then_inc(o_ready, 1)
                act.wait_ge(xnT_ready, ONE + 2 * i + 2)
                act.wait_ge(v_done, ONE + 2 * i + 2)
                nc.scalar.activation(xnT[:, :, 0:WIN], xnT[:, :, 2 * P:2 * P + WIN], ACT.Copy).then_inc(tails_moved, 1)
                act.wait_ge(k_ready, ONE + i + 1)
                act.wait_ge(s_done, ONE + 2 * NU * i + 2 * NU)
                nc.scalar.activation(kT[:, :, 0:WIN], kT[:, :, 2 * P:2 * P + WIN], ACT.Copy).then_inc(tails_moved, 1)

        @block.tensor
        def _(pe):
            pe.wait_ge(w_in, ONE + 16 * (1 + HU))
            pe.wait_ge(consts_set, ONE + 1)
            with pe.Fori(0, NP) as i:
                for s in range(2):
                    pe.wait_ge(xn_ready, ONE + 2 * i + s + 1)
                    pe.wait_ge(probT_ready, ONE + 2 * NU * i)
                    for k in range(KD):
                        last = nc.tensor.transpose(b_tp[s][:, P * k:P * (k + 1)],
                                                   xn[s][:, P * k:P * (k + 1)], g.ident[:])
                    last.then_inc(xnT_done, 1)
                pe.wait_ge(xnT_ready, ONE + 2 * i + 2)
                pe.wait_ge(x_ready, ONE + 2 * i)
                for part, bank in enumerate((b_q, b_k)):
                    for m in range(KD):
                        for k in range(KD):
                            last = nc.tensor.matmul(bank[:, 2 * P * m:2 * P * (m + 1)],
                                                    wqkv[:, k, D * part + P * m:D * part + P * (m + 1)],
                                                    xnT[:, k, WIN:WIN + 2 * P], start=(k == 0), stop=(k == KD - 1))
                    last.then_inc(qk_done, 1)
                pe.wait_ge(rsum_ready, ONE + 2 * i)
                for s in range(2):
                    for h in range(2):
                        at = P * s + Q * h
                        for k in range(KD):
                            last = nc.tensor.matmul(b_v[s][:, D * h:D * (h + 1)], xnT[:, k, at:at + P],
                                                    wqkv[:, k, 2 * D:3 * D], start=(k == 0), stop=(k == KD - 1))
                    last.then_inc(v_done, 1)
                pe.wait_ge(k_ready, ONE + i + 1)
                pe.wait_ge(tails_moved, ONE + 2 * i)

                def scores(u):
                    s, m = u // NU, u % NU
                    n = 2 * NU * i + u + 1
                    bank = b_s[u % 2]
                    if m == 0 and s == 0:
                        pe.wait_ge(q_ready, ONE + 2 * i + 1)
                    if m == 2 and s == 0:
                        pe.wait_ge(q_ready, ONE + 2 * i + 2)
                    if u >= 2:
                        pe.wait_ge(ex_ready, ONE + n - 2)
                    else:
                        pe.wait_ge(ex_ready, ONE + 2 * NU * i)
                    mask = mask1[:].unsqueeze(1) if s else mask0[:, bass.ds(i, 1), :]
                    nc.tensor.matmul(bank[:].rearrange("p (h w) -> p h w", h=HU), ident_bf[:],
                                     mask.broadcast_to([P, HU, W2]), start=True, stop=False, skip_group_check=True)
                    k = m // (HM // HU)
                    for j in range(HU):
                        head = HU * m % HM + j
                        for h in range(2):
                            at = P * s + Q * h
                            last = nc.tensor.matmul(bank[half(h), W2 * j:W2 * (j + 1)],
                                                    q_heads[:, k, head, at:at + Q], kT[:, k, at:at + P],
                                                    start=False, stop=True, skip_group_check=True)
                    last.then_inc(s_done, 1)

                def transposes(u):
                    n = 2 * NU * i + u + 1
                    pe.wait_ge(prob_ready, ONE + n)
                    if u >= 2:
                        pe.wait_ge(probT_ready, ONE + n - 2)
                    else:
                        pe.wait_ge(probT_ready, ONE + 2 * NU * i)
                    for j in range(HU):
                        last = nc.tensor.transpose(b_pt[u % 2][:, P * j:P * (j + 1)], prob[u % 2][:, j, :], g.ident[:])
                    last.then_inc(probT_done, 1)

                def outputs(u):
                    s, m = u // NU, u % NU
                    n = 2 * NU * i + u + 1
                    if m == 0:
                        pe.wait_ge(v_ready, ONE + 2 * i + s + 1)
                    if u == 0:
                        pe.wait_ge(k_ready, ONE + i + 1)
                        pe.wait_ge(q_ready, ONE + 2 * i + 2)
                    pe.wait_ge(probT_ready, ONE + n)
                    for j in range(HU):
                        for h in range(2):
                            last = nc.tensor.matmul((b_q, b_k)[s][R * j:R * (j + 1), P * m + Q * h:P * m + Q * (h + 1)],
                                                    v[:, 2 * s + h, HU * m + j, :], probT[u % 2][:, j, half(h)],
                                                    start=True, stop=True)
                    if m == NU - 1:
                        last.then_inc(o_done, 1)

                def sums(s):
                    pe.wait_ge(o_ready, ONE + 2 * i + s + 1)
                    nc.tensor.matmul(b_v[s][:], sum_rows[:], o[s][:], start=True, stop=True).then_inc(sum_done, 1)

                def project(s):
                    pe.wait_ge(on_ready, ONE + 2 * i + s + 1)
                    for m in range(NU):
                        last = nc.tensor.matmul((b_q, b_k)[s][:, 0:D], on[s][:, m, :], wo[:, m, :],
                                                start=(m == 0), stop=(m == NU - 1))
                    last.then_inc(y_done, 1)

                scores(0)
                for u in range(2 * NU):
                    if u + 1 < 2 * NU:
                        scores(u + 1)
                    transposes(u)
                    if u >= 1:
                        outputs(u - 1)
                    if u == NU + 1:
                        sums(0)
                    if u == NU + 3:
                        project(0)
                outputs(2 * NU - 1)
                sums(1)
                project(1)


def normalised_pairs(nc, g, name, gate, gate_b, xnT_all, logits, rows_out=None):
    E = logits.shape[2]
    with phase(nc) as (e, semaphore, begin):
        sb = lambda n, shape, dt=F32: e.enter_context(nc.sbuf_tensor(f"{name}_{n}", shape, dt))
        sem = lambda n: semaphore(f"{name}_{n}")
        gw = sb("gw", [P, KD, E])
        gb = sb("gb", [P, E])
        xn = [sb(f"xn{s}", [P, D]) for s in range(2)]
        xnT = [sb(f"xnT{s}", [P, KD, P]) for s in range(2)]
        gate_in, gb_zero = sem("gate_in"), sem("gb_zero")
        xn_ready, xnT_done, xnT_ready, kept, l_done, l_ready = [
            sem(n) for n in ("xn_ready", "xnT_done", "xnT_ready", "kept", "l_done", "l_ready")]
        rows_kept = [sem(f"rows_kept{s}") for s in range(2)]
        block = begin()
        b_tp, b_l = g.bank[0:2], g.bank[2:4]

        @block.sync
        def _(sp):
            sp.dma_start(gw[:], gate.rearrange("(k p) e -> p k e", p=P)).then_inc(gate_in, 16)
            if gate_b is not None:
                sp.dma_start(gb[:], gate_b.rearrange("(o e) -> o e", o=1).broadcast_to([P, E])).then_inc(gate_in, 16)
            if rows_out is not None:
                rows = rows_out.rearrange("(t p) d -> t p d", p=P)
                with sp.Fori(0, T // 2) as i:
                    for s in range(2):
                        sp.wait_ge(xn_ready, ONE + 2 * i + s + 1)
                        dst = rows[bass.ds(2 * i + s, 1), :, :].rearrange("t p d -> (t p) d")
                        sp.dma_start(dst, xn[s][:]).then_inc(rows_kept[s], 16)
                for s in range(2):
                    sp.wait_ge(rows_kept[s], ONE + 16 * (T // 2))

        @block.vector
        def _(dve):
            if gate_b is None:
                nc.vector.memset(gb[:], 0.0).then_inc(gb_zero, 1)
                dve.wait_ge(gb_zero, ONE + 1)
            else:
                dve.wait_ge(gate_in, ONE + 32)
            with dve.Fori(0, T // 2) as i:
                for s in range(2):
                    t = 2 * i + s
                    dve.wait_ge(xnT_done, ONE + 2 * i)
                    if rows_out is not None:
                        dve.wait_ge(rows_kept[s], ONE + 16 * i)
                    nc.vector.tensor_scalar(xn[s][:], g.x[:, bass.ds(t, 1), :].rearrange("p o d -> p (o d)"),
                                            g.mean[:, bass.ds(t, 1)], g.rstd[:, bass.ds(t, 1)],
                                            ALU.subtract, ALU.mult).then_inc(xn_ready, 1)
                for s in range(2):
                    dve.wait_ge(l_done, ONE + 2 * i + s + 1)
                    nc.vector.tensor_tensor(logits[:, bass.ds(2 * i + s, 1), :].rearrange("p o e -> p (o e)"),
                                            b_l[s][:, 0:E], gb[:], ALU.add).then_inc(l_ready, 1)

        @block.scalar
        def _(act):
            with act.Fori(0, T // 2) as i:
                for s in range(2):
                    act.wait_ge(xnT_done, ONE + 2 * i + s + 1)
                    act.wait_ge(l_done, ONE + 2 * i)
                    if xnT_all is not None:
                        act.wait_ge(kept, ONE + 2 * i)
                    nc.scalar.activation(xnT[s][:], b_tp[s][:, 0:D].rearrange("p (k q) -> p k q", k=KD),
                                         ACT.Copy).then_inc(xnT_ready, 1)

        @block.gpsimd
        def _(pool):
            if xnT_all is not None:
                with pool.Fori(0, T // 2) as i:
                    for s in range(2):
                        pool.wait_ge(xnT_ready, ONE + 2 * i + s + 1)
                        nc.gpsimd.tensor_copy(xnT_all[:, :, bass.ds((2 * i + s) * P, P)], xnT[s][:]).then_inc(kept, 1)

        @block.tensor
        def _(pe):
            pe.wait_ge(gate_in, ONE + (16 if gate_b is None else 32))
            with pe.Fori(0, T // 2) as i:
                for s in range(2):
                    pe.wait_ge(xn_ready, ONE + 2 * i + s + 1)
                    pe.wait_ge(xnT_ready, ONE + 2 * i)
                    for k in range(KD):
                        last = nc.tensor.transpose(b_tp[s][:, P * k:P * (k + 1)], xn[s][:, P * k:P * (k + 1)], g.ident[:])
                    last.then_inc(xnT_done, 1)
                for s in range(2):
                    pe.wait_ge(xnT_ready, ONE + 2 * i + s + 1)
                    pe.wait_ge(l_ready, ONE + 2 * i)
                    for k in range(KD):
                        last = nc.tensor.matmul(b_l[s][:, 0:E], xnT[s][:, k, :], gw[:, k, :],
                                                start=(k == 0), stop=(k == KD - 1))
                    last.then_inc(l_done, 1)


def top2_weights(nc, g, logits, w, n_shared):
    E = logits.shape[2]
    with phase(nc) as (e, semaphore, begin):
        sb = lambda n, shape, dt=F32: e.enter_context(nc.sbuf_tensor(f"t2_{n}", shape, dt))
        sem = lambda n: semaphore(f"t2_{n}")
        order, row = sb("order", [P, E]), sb("row", [P, T])
        p, left, pick, first = [sb(n, [P, T, E]) for n in ("p", "left", "pick", "first")]
        step, order_set, shifted, exp_ready = sem("step"), sem("order_set"), sem("shifted"), sem("exp_ready")
        block = begin()
        over = lambda a: a[:].unsqueeze(2).broadcast_to([P, T, E])

        @block.gpsimd
        def _(pool):
            nc.gpsimd.iota(order[:], pattern=[[-1, E]], base=E, channel_multiplier=0,
                           allow_small_or_imprecise_dtypes=True).then_inc(order_set, 1)

        @block.scalar
        def _(act):
            act.wait_ge(shifted, ONE + 1)
            nc.scalar.activation(p[:], p[:], ACT.Exp).then_inc(exp_ready, 1)

        @block.vector
        def _(dve):
            link = Chain(dve, step)
            link(nc.vector.tensor_reduce(row[:], logits[:], axis=AX.X, op=ALU.max))
            nc.vector.tensor_tensor(p[:], logits[:], over(row), ALU.subtract).then_inc(shifted, 1)
            dve.wait_ge(exp_ready, ONE + 1)
            link(nc.vector.tensor_reduce(row[:], p[:], axis=AX.X, op=ALU.add))
            link(nc.vector.reciprocal(row[:], row[:]))
            link(nc.vector.tensor_tensor(p[:], p[:], over(row), ALU.mult))
            dve.wait_ge(order_set, ONE + 1)
            link(nc.vector.tensor_copy(left[:], p[:]))
            for n in range(2):
                link(nc.vector.tensor_reduce(row[:], left[:], axis=AX.X, op=ALU.max))
                link(nc.vector.tensor_tensor(pick[:], left[:], over(row), ALU.is_equal))
                link(nc.vector.tensor_tensor(pick[:], pick[:], order[:].unsqueeze(1).broadcast_to([P, T, E]), ALU.mult))
                link(nc.vector.tensor_reduce(row[:], pick[:], axis=AX.X, op=ALU.max))
                link(nc.vector.tensor_tensor(first[:], pick[:], over(row), ALU.is_equal))
                link(nc.vector.scalar_tensor_tensor(left[:], first[:], -4.0, left[:], ALU.mult, ALU.add))
            link(nc.vector.tensor_scalar(first[:], left[:], 0.0, None, ALU.is_lt))
            nc.vector.memset(w[:, :, E:E + n_shared], 1.0 / n_shared)
            link(nc.vector.tensor_tensor(w[:, :, 0:E], first[:], p[:], ALU.mult))


def experts_dense(nc, g, xnT_all, w):
    ins = g.ins
    E, SH = ins["L0_ffn_rw1"].shape[0], ins["L0_ffn_sw1"].shape[0]
    H = ins["L0_ffn_rw1"].shape[2]
    EA, KH, C = E + SH, H // P, 512
    NC, TC = N // C, C // P
    with phase(nc) as (e, semaphore, begin):
        sb = lambda n, shape, dt=F32: e.enter_context(nc.sbuf_tensor(f"ff_{n}", shape, dt))
        sem = lambda n: semaphore(f"ff_{n}")
        w1 = [sb(f"w1_{s}", [P, KD, H]) for s in range(2)]
        w2 = [sb(f"w2_{s}", [P, KD, H]) for s in range(2)]
        w3 = [sb(f"w3_{s}", [P, KH, D]) for s in range(2)]
        b_rows = sb("b_rows", [EA * KH, 2, P])
        b_cols = sb("b_cols", [P, 2, EA, KH])
        b3 = sb("b3", [EA, D])
        w_tile = [sb(f"w_tile{s}", [P, EA]) for s in range(2)]
        wT = [sb(f"wT{s}", [EA, P]) for s in range(2)]
        silu = [sb(f"silu{k}", [P, C]) for k in range(2)]
        glu = [sb(f"glu{k}", [P, KH, C]) for k in range(2)]
        b_in, bT_done, bT_ready = sem("b_in"), sem("bT_done"), sem("bT_ready")
        w_in = [sem(f"w_in{s}") for s in range(2)]
        wt_ready, wT_done, wT_ready, b3_done, b3_added = [
            sem(n) for n in ("wt_ready", "wT_done", "wT_ready", "b3_done", "b3_added")]
        p1_done, p2_done, silu_ready, glu_ready, y_done, y_added, stats_ready = [
            sem(n) for n in ("p1_done", "p2_done", "silu_ready", "glu_ready", "y_done", "y_added", "stats_ready")]
        b_p1, b_p2, b_y = g.bank[0:2], g.bank[2:4], g.bank[4:8]
        block = begin()

        @block.sync
        def _(sp):
            for n, (r, s) in enumerate(((ins["L0_ffn_rb1"], ins["L0_ffn_sb1"]), (ins["L0_ffn_rb2"], ins["L0_ffn_sb2"]))):
                sp.dma_start(b_rows[0:E * KH, n], r.rearrange("e (m p) -> (e m) p", p=P)).then_inc(b_in, 16)
                sp.dma_start(b_rows[E * KH:EA * KH, n], s.rearrange("e (m p) -> (e m) p", p=P)).then_inc(b_in, 16)
            sp.dma_start(b3[0:E], ins["L0_ffn_rb3"]).then_inc(b_in, 16)
            sp.dma_start(b3[E:EA], ins["L0_ffn_sb3"]).then_inc(b_in, 16)
            for n in range(EA):
                s = n % 2
                a1, a2, a3 = [r[n] if n < E else t[n - E] for r, t in (
                    (ins["L0_ffn_rw1"], ins["L0_ffn_sw1"]), (ins["L0_ffn_rw2"], ins["L0_ffn_sw2"]), (ins["L0_ffn_rw3"], ins["L0_ffn_sw3"]))]
                if n >= 2:
                    sp.wait_ge(y_done, ONE + NC * TC * (n - 1))
                sp.dma_start(w1[s][:], a1.rearrange("(k p) h -> p k h", p=P)).then_inc(w_in[s], 16)
                sp.dma_start(w2[s][:], a2.rearrange("(k p) h -> p k h", p=P)).then_inc(w_in[s], 16)
                sp.dma_start(w3[s][:], a3.rearrange("(k p) d -> p k d", p=P)).then_inc(w_in[s], 16)

        @block.vector
        def _(dve):
            with dve.Fori(0, T // 2) as i:
                for s in range(2):
                    dve.wait_ge(wT_done, ONE + 2 * i)
                    nc.vector.tensor_copy(w_tile[s][:], w[:, bass.ds(2 * i + s, 1), :].rearrange("p o e -> p (o e)")).then_inc(wt_ready, 1)
                for s in range(2):
                    xt = g.x[:, bass.ds(2 * i + s, 1), :].rearrange("p o d -> p (o d)")
                    dve.wait_ge(b3_done, ONE + 2 * i + s + 1)
                    nc.vector.tensor_tensor(xt, b_y[s][:, 0:D], xt, ALU.add).then_inc(b3_added, 1)
            dve.wait_ge(bT_ready, ONE + 1)
            dve.wait_ge(b3_added, ONE + T)
            with dve.Fori(0, EA) as n:
                with dve.Fori(0, NC) as c:
                    it = n * NC + c
                    for k in range(2):
                        pass
                    for m in range(KH):
                        dve.wait_ge(silu_ready, ONE + it * KH + m + 1)
                        dve.wait_ge(p2_done, ONE + it * KH + m + 1)
                        dve.wait_ge(y_done, ONE + it * TC)
                        b2 = b_cols[:, 1].rearrange("p e m -> p (e m)")[:, bass.ds(n * KH + m, 1)]
                        nc.vector.scalar_tensor_tensor(glu[0][:, m, :], b_p2[m % 2][:], b2, silu[m % 2][:],
                                                       ALU.add, ALU.mult).then_inc(glu_ready, 1)
                    for q in range(TC):
                        t = c * TC + q
                        xt = g.x[:, bass.ds(t, 1), :].rearrange("p o d -> p (o d)")
                        wt = w[:].rearrange("p t e -> p (t e)")[:, bass.ds(t * EA + n, 1)]
                        dve.wait_ge(y_done, ONE + it * TC + q + 1)
                        dve.wait_ge(y_added, ONE + it * TC)
                        nc.vector.scalar_tensor_tensor(xt, b_y[q][:, 0:D], wt, xt, ALU.mult, ALU.add).then_inc(y_added, 1)
            with dve.Fori(0, T) as t:
                dve.wait_ge(y_added, ONE + EA * T)
                nc.vector.bn_stats(g.stats[:, bass.ds(t, 1), :], g.x[:, bass.ds(t, 1), :]).then_inc(stats_ready, 1)

        @block.scalar
        def _(act):
            act.wait_ge(bT_done, ONE + 1)
            nc.scalar.activation(b_cols[:].rearrange("p n e m -> p n (e m)"),
                                 b_p1[0][:, 0:2 * EA * KH].rearrange("p (n r) -> p n r", n=2), ACT.Copy).then_inc(bT_ready, 1)
            act.wait_ge(bT_ready, ONE + 1)
            with act.Fori(0, T // 2) as i:
                for s in range(2):
                    act.wait_ge(wT_done, ONE + 2 * i + s + 1)
                    act.wait_ge(b3_done, ONE + 2 * i)
                    nc.scalar.activation(wT[s][:], b_p2[s][0:EA, 0:P], ACT.Copy).then_inc(wT_ready, 1)
            with act.Fori(0, EA) as n:
                with act.Fori(0, NC) as c:
                    it = n * NC + c
                    for m in range(KH):
                        act.wait_ge(p1_done, ONE + it * KH + m + 1)
                        if m >= 2:
                            act.wait_ge(glu_ready, ONE + it * KH + m - 1)
                        else:
                            act.wait_ge(glu_ready, ONE + it * KH)
                        b1 = b_cols[:, 0].rearrange("p e m -> p (e m)")[:, bass.ds(n * KH + m, 1)]
                        nc.scalar.activation(silu[m % 2][:], b_p1[m % 2][:], ACT.Silu, bias=b1).then_inc(silu_ready, 1)

        @block.tensor
        def _(pe):
            pe.wait_ge(b_in, ONE + 16 * 6)
            for n in range(2):
                last = nc.tensor.transpose(b_p1[0][:, n * EA * KH:(n + 1) * EA * KH], b_rows[:, n, :], g.ident[0:EA * KH, 0:EA * KH])
            last.then_inc(bT_done, 1)
            with pe.Fori(0, T // 2) as i:
                for s in range(2):
                    pe.wait_ge(wt_ready, ONE + 2 * i + s + 1)
                    pe.wait_ge(wT_ready, ONE + 2 * i)
                    nc.tensor.transpose(b_p2[s][0:EA, 0:P], w_tile[s][:], g.ident[:]).then_inc(wT_done, 1)
                for s in range(2):
                    pe.wait_ge(wT_ready, ONE + 2 * i + s + 1)
                    pe.wait_ge(b3_added, ONE + 2 * i)
                    nc.tensor.matmul(b_y[s][:, 0:D], wT[s][:], b3[:], start=True, stop=True).then_inc(b3_done, 1)
            pe.wait_ge(bT_ready, ONE + 1)
            pe.wait_ge(b3_added, ONE + T)
            with pe.Fori(0, EA // 2) as n2:
                for s in range(2):
                    with pe.Fori(0, NC) as c:
                        it = (2 * n2 + s) * NC + c
                        pe.wait_ge(w_in[s], ONE + 48 * n2 + 48)
                        rhs = lambda k: xnT_all[:, k, bass.ds(c * C, C)]
                        for m in range(KH):
                            if m >= 2:
                                pe.wait_ge(silu_ready, ONE + it * KH + m - 1)
                            else:
                                pe.wait_ge(silu_ready, ONE + it * KH)
                            for k in range(KD):
                                last = nc.tensor.matmul(b_p1[m % 2][:], w1[s][:, k, P * m:P * (m + 1)], rhs(k),
                                                        start=(k == 0), stop=(k == KD - 1))
                            last.then_inc(p1_done, 1)
                            if m >= 2:
                                pe.wait_ge(glu_ready, ONE + it * KH + m - 1)
                            else:
                                pe.wait_ge(glu_ready, ONE + it * KH)
                            for k in range(KD):
                                last = nc.tensor.matmul(b_p2[m % 2][:], w2[s][:, k, P * m:P * (m + 1)], rhs(k),
                                                        start=(k == 0), stop=(k == KD - 1))
                            last.then_inc(p2_done, 1)
                        pe.wait_ge(y_added, ONE + it * TC)
                        for m in range(KH):
                            pe.wait_ge(glu_ready, ONE + it * KH + m + 1)
                            for q in range(TC):
                                last = nc.tensor.matmul(b_y[q][:, 0:D], glu[0][:, m, P * q:P * (q + 1)], w3[s][:, m, :],
                                                        start=(m == 0), stop=(m == KH - 1))
                                if m == KH - 1:
                                    last.then_inc(y_done, 1)


def mixture0(nc, g):
    ins = g.ins
    E, SH = ins["L0_ffn_rw1"].shape[0], ins["L0_ffn_sw1"].shape[0]
    with ExitStack() as e:
        xnT_all = e.enter_context(nc.sbuf_tensor("m0_xnT", [P, KD, N], F32))
        w = e.enter_context(nc.sbuf_tensor("m0_w", [P, T, E + SH], F32))
        logits = e.enter_context(nc.sbuf_tensor("m0_logits", [P, T, E], F32))
        normalised_pairs(nc, g, "np0", ins["L0_ffn_gate_w"], ins["L0_ffn_gate_b"], xnT_all, logits)
        top2_weights(nc, g, logits, w, SH)
        experts_dense(nc, g, xnT_all, w)


def group_attention(nc, g, r_all):
    ins = g.ins
    GT = S * D // NH // D
    NG = 2 * P // GT
    PC = D // DH
    L = GT * PC
    A = P // GT
    QT = L // P
    HC = P // DH
    BL = 32
    ST = 3 * BL
    HALF = 512
    NP = T // 2
    PT_SLOTS = 2 * NG
    U = NG * QT
    with phase(nc) as (e, semaphore, begin):
        sb = lambda n, shape, dt=F32: e.enter_context(nc.sbuf_tensor(f"ga_{n}", shape, dt))
        sem = lambda n: semaphore(f"ga_{n}")
        wq, wk, wv = [sb(n, [P, KD, D]) for n in ("wq", "wk", "wv")]
        wo = sb("wo", [P, A, D])
        b_qk = sb("b_qk", [P, 2, KD])
        bv = sb("bv", [P, QT, DH])
        bo = sb("bo", [P, D])
        pick_f = [sb(f"pick_f{n}", [P, HC, ST]) for n in range(4)]
        pick = [sb(f"pick{n}", [P, HC, ST], F32R) for n in range(4)]
        tile_rows = sb("tile_rows", [P, QT, P])
        xn = [sb(f"xn{s}", [P, D]) for s in range(2)]
        xn_bo = [sb(f"xn_bo{s}", [P, D]) for s in range(2)]
        xnT = sb("xnT", [P, KD, 2 * P])
        part_hi = sb("part_hi", [P, 2, KD, 2 * P], F32R)
        part_lo = sb("part_lo", [P, 2, KD, 2 * P], F32R)
        qs = sb("qs", [P, NG, L], F32R)
        ks = sb("ks", [P, NG, L], F32R)
        v = sb("v", [P, NG, QT, BL])
        nmax = sb("nmax", [P, NG, P])
        probT = [sb(f"probT{k}", [P, L]) for k in range(PT_SLOTS)]
        o = sb("o", [P, L])
        rsum = sb("rsum", [P, QT, NG])
        ctxn = sb("ctxn", [P, NG, QT, DH])
        ctxT = sb("ctxT", [P, 2, A, P])
        w_in, b_in, picks_f, picks, fixed, rows_set, chain = [sem(n) for n in (
            "w_in", "b_in", "picks_f", "picks", "fixed", "rows_set", "chain")]
        xn_ready, xn_bo_ready, xnT_done, xnT_ready, qk_done, hi_ready, lo_ready, v_done, v_ready = [sem(n) for n in (
            "xn_ready", "xn_bo_ready", "xnT_done", "xnT_ready", "qk_done", "hi_ready", "lo_ready", "v_done", "v_ready")]
        q_picked, k_picked, q_ready, k_ready = [sem(n) for n in ("q_picked", "k_picked", "q_ready", "k_ready")]
        s_done, max_ready, maxT_done, fold_ready, sT_done, exp_ready, pv_done, o_ready = [sem(n) for n in (
            "s_done", "max_ready", "maxT_done", "fold_ready", "sT_done", "exp_ready", "pv_done", "o_ready")]
        ctx_done, rsum_ready, ctxn_ready, ctxT_done, ctxT_ready, y_done, r_ready, stats_ready = [sem(n) for n in (
            "ctx_done", "rsum_ready", "ctxn_ready", "ctxT_done", "ctxT_ready", "y_done", "r_ready", "stats_ready")]
        b_s = [g.bank2[0], g.bank2[1]]
        b_o = g.bank2[2]
        b_m = g.bank[6:8]
        block = begin()

        @block.sync
        def _(sp):
            for w, src in ((wq, ins["L1_attn_wq"]), (wk, ins["L1_attn_wk"]), (wv, ins["L1_attn_wv"])):
                sp.dma_start(w[:], src.rearrange("(k p) n -> p k n", p=P)).then_inc(w_in, 16)
            wo_rows = ins["L1_attn_wo"].rearrange("(q a d) n -> q d a n", a=A, d=DH)
            for q in range(QT):
                sp.dma_start(wo[q * DH:(q + 1) * DH], wo_rows[q]).then_inc(w_in, 16)
            for n, src in enumerate((ins["L1_attn_bq"], ins["L1_attn_bk"])):
                for k in range(KD):
                    sp.dma_start(b_qk[:, n, k:k + 1], src[P * k:P * (k + 1)].rearrange("(p o) -> p o", o=1)).then_inc(b_in, 16)
            bv_parts = ins["L1_attn_bv"].rearrange("(o q a d) -> a o q d", o=1, a=A, d=DH)
            for a in range(A):
                sp.dma_start(bv[a * GT:(a + 1) * GT], bv_parts[a].broadcast_to([GT, QT, DH])).then_inc(b_in, 16)
            sp.dma_start(bo[:], ins["L1_attn_bo"].rearrange("(o n) -> o n", o=1).broadcast_to([P, D])).then_inc(b_in, 16)
        W_IN, B_IN = 16 * (3 + QT), 16 * (2 * KD + A + 1)

        @block.gpsimd
        def _(pool):
            link = Chain(pool, chain)
            nc.gpsimd.memset(nmax[:], 0.0)
            nc.gpsimd.memset(v[:], 0.0)
            for n in range(4):
                nc.gpsimd.memset(pick_f[n][:], 0.0)
            link(nc.gpsimd.memset(tile_rows[:], 0.0))
            nc.gpsimd.memset(v[:, :, :, DH:DH + 1], 1.0).then_inc(fixed, 1)
            for n, blocks in enumerate(((0, 1), (2,), (0, 2), (1,))):
                for b in blocks:
                    m = pick_f[n][:, :, BL * b:BL * b + DH]
                    last = nc.gpsimd.affine_select(out=m, in_=m, compare_op=ALU.not_equal, fill=1.0, base=0,
                                                   pattern=[[-DH, HC], [-1, DH]], channel_multiplier=1)
            last.then_inc(picks_f, 1)
            pool.wait_ge(fixed, ONE + 1)
            pool.wait_ge(picks_f, ONE + 1)
            nc.gpsimd.affine_select(out=tile_rows[ST:P], in_=tile_rows[ST:P], compare_op=ALU.not_equal, fill=1.0, base=0,
                                    pattern=[[-1, QT], [0, P]], channel_multiplier=1).then_inc(rows_set, 1)
            pool.wait_ge(rows_set, ONE + 1)
            pool.wait_ge(b_in, ONE + B_IN)
            with pool.Fori(0, NP) as i:
                for s in range(2):
                    pool.wait_ge(xn_ready, ONE + 2 * i + s + 1)
                    pool.wait_ge(r_ready, ONE + 2 * i)
                    nc.gpsimd.tensor_tensor(xn_bo[s][:], xn[s][:], bo[:], ALU.add).then_inc(xn_bo_ready, 1)

        @block.vector
        def _(dve):
            nc.vector.memset(ks[ST:P].bitcast(F32), 1.0).then_inc(picks, 1)
            dve.wait_ge(picks_f, ONE + 1)
            for n in range(4):
                nc.vector.tensor_copy(pick[n][:], pick_f[n][:]).then_inc(picks, 1)
            dve.wait_ge(b_in, ONE + B_IN)
            dve.wait_ge(rows_set, ONE + 1)
            dve.wait_ge(fixed, ONE + 1)
            with dve.Fori(0, NP) as i:
                for s in range(2):
                    t = 2 * i + s
                    dve.wait_ge(xnT_done, ONE + 2 * i)
                    dve.wait_ge(xn_bo_ready, ONE + 2 * i)
                    nc.vector.tensor_scalar(xn[s][:], g.x[:, bass.ds(t, 1), :].rearrange("p o d -> p (o d)"),
                                            g.mean[:, bass.ds(t, 1)], g.rstd[:, bass.ds(t, 1)],
                                            ALU.subtract, ALU.mult).then_inc(xn_ready, 1)
                for n in range(2):
                    for m in range(KD):
                        dve.wait_ge(hi_ready, ONE + 4 * i + 2 * n + 2)
                        dve.wait_ge(k_picked, ONE + QT * i)
                        nc.vector.scalar_tensor_tensor(part_lo[:, n, m], b_m[n][:, 2 * P * m:2 * P * (m + 1)],
                                                       b_qk[:, n, m:m + 1], part_hi[:, n, m].bitcast(F32),
                                                       ALU.add, ALU.subtract).then_inc(lo_ready, 1)
                dve.wait_ge(v_done, ONE + i + 1)
                dve.wait_ge(pv_done, ONE + QT * i)
                nc.vector.tensor_tensor(v[:, :, :, 0:DH], b_o[:, 0:NG * P].rearrange("p (n q d) -> p n q d", n=NG, d=DH),
                                        bv[:].unsqueeze(1).broadcast_to([P, NG, QT, DH]), ALU.add).then_inc(v_ready, 1)
                for c in range(QT):
                    dve.wait_ge(k_picked, ONE + QT * i + c + 1)
                    dve.wait_ge(sT_done, ONE + U * i)
                    nc.vector.tensor_copy(ks[0:ST, :, A * GT * c:A * GT * (c + 1)].rearrange("p n (a t) -> p n a t", a=A),
                                          b_m[1][0:ST, :].rearrange("p (a n t) -> p n a t", a=A, n=NG)).then_inc(k_ready, 1)

                def fold(n):
                    dve.wait_ge(maxT_done, ONE + NG * i + n + 1)
                    nc.vector.tensor_tensor(qs[ST:P, n].rearrange("p (t q) -> p t q", t=QT),
                                            b_m[n % 2][ST:P, 0:P].unsqueeze(1).broadcast_to([P - ST, QT, P]),
                                            tile_rows[ST:P], ALU.mult).then_inc(fold_ready, 1)

                for u in range(U):
                    dve.wait_ge(s_done, ONE + U * i + u + 1)
                    dve.wait_ge(maxT_done, ONE + NG * i)
                    n, q = u // QT, u % QT
                    nc.vector.tensor_reduce(nmax[:, n, ST + q:ST + q + 1], b_s[u % 2][:], axis=AX.X, op=ALU.max,
                                            negate=True).then_inc(max_ready, 1)
                    if n and q == 2:
                        fold(n - 1)
                fold(NG - 1)
                dve.wait_ge(ctx_done, ONE + i + 1)
                for hf in range(2):
                    src = b_m[hf][:].rearrange("p (q n r) -> p q n r", n=NG, r=BL)
                    dst = slice(hf * QT // 2, (hf + 1) * QT // 2)
                    nc.vector.reciprocal(rsum[:, dst], src[:, :, :, DH]).then_inc(rsum_ready, 1)
                    dve.wait_ge(rsum_ready, ONE + 2 * i + hf + 1)
                    nc.vector.tensor_tensor(ctxn[:, :, dst].rearrange("p n q d -> p q n d"), src[:, :, :, 0:DH],
                                            rsum[:, dst].unsqueeze(3).broadcast_to([P, QT // 2, NG, DH]),
                                            ALU.mult).then_inc(ctxn_ready, 1)
                for s in range(2):
                    dve.wait_ge(y_done, ONE + 2 * i + s + 1)
                    dve.wait_ge(xn_bo_ready, ONE + 2 * i + s + 1)
                    rt = r_all[:, bass.ds(2 * i + s, 1), :].rearrange("p o d -> p (o d)")
                    nc.vector.tensor_tensor(rt, (b_m[1], b_o)[s][:, 0:D], xn_bo[s][:], ALU.add).then_inc(r_ready, 1)
                    dve.wait_ge(r_ready, ONE + 2 * i + s + 1)
                    nc.vector.bn_stats(g.stats[:, bass.ds(2 * i + s, 1), :], rt).then_inc(stats_ready, 1)

        @block.scalar
        def _(act):
            act.wait_ge(b_in, ONE + B_IN)
            with act.Fori(0, NP) as i:
                for s in range(2):
                    act.wait_ge(xnT_done, ONE + 2 * i + s + 1)
                    act.wait_ge(v_done, ONE + i)
                    nc.scalar.activation(xnT[:, :, P * s:P * (s + 1)],
                                         b_m[s][:, 0:D].rearrange("p (k q) -> p k q", k=KD), ACT.Copy).then_inc(xnT_ready, 1)
                for n in range(2):
                    act.wait_ge(qk_done, ONE + 2 * i + n + 1)
                    act.wait_ge(k_picked, ONE + QT * i)
                    for m in range(KD):
                        nc.scalar.activation(part_hi[:, n, m], b_m[n][:, 2 * P * m:2 * P * (m + 1)], ACT.Identity,
                                             bias=b_qk[:, n, m:m + 1]).then_inc(hi_ready, 1)
                for c in range(QT):
                    act.wait_ge(q_picked, ONE + QT * i + c + 1)
                    act.wait_ge(sT_done, ONE + U * i)
                    nc.scalar.activation(qs[0:ST, :, A * GT * c:A * GT * (c + 1)].rearrange("p n (a t) -> p n a t", a=A),
                                         b_m[0][0:ST, :].rearrange("p (a n t) -> p n a t", a=A, n=NG),
                                         ACT.Copy).then_inc(q_ready, 1)
                for u in range(U):
                    k = u // NG
                    act.wait_ge(sT_done, ONE + U * i + u + 1)
                    if k >= 2:
                        act.wait_ge(pv_done, ONE + QT * i + k - 1)
                    else:
                        act.wait_ge(pv_done, ONE + QT * i)
                    nc.scalar.activation(probT[u % PT_SLOTS][:], b_s[u % 2][:], ACT.Exp, scale=SCALE).then_inc(exp_ready, 1)
                act.wait_ge(pv_done, ONE + QT * i + QT)
                act.wait_ge(ctx_done, ONE + i)
                nc.scalar.activation(o[:], b_o[:], ACT.Copy).then_inc(o_ready, 1)
                act.wait_ge(ctxT_done, ONE + i + 1)
                for s in range(2):
                    nc.scalar.activation(ctxT[:, s].rearrange("p a (n t) -> p n a t", t=GT),
                                         b_m[0][:, 2 * P * s:2 * P * (s + 1)].rearrange("p (n a t) -> p n a t", a=A, t=GT),
                                         ACT.Copy).then_inc(ctxT_ready, 1)

        @block.tensor
        def _(pe):
            pe.wait_ge(w_in, ONE + W_IN)
            pe.wait_ge(picks, ONE + 5)
            pe.wait_ge(fixed, ONE + 1)
            with pe.Fori(0, NP) as i:
                for s in range(2):
                    pe.wait_ge(xn_ready, ONE + 2 * i + s + 1)
                    pe.wait_ge(r_ready, ONE + 2 * i)
                    for k in range(KD):
                        last = nc.tensor.transpose(b_m[s][:, P * k:P * (k + 1)], xn[s][:, P * k:P * (k + 1)], g.ident[:])
                    last.then_inc(xnT_done, 1)
                pe.wait_ge(xnT_ready, ONE + 2 * i + 2)
                for n, w in enumerate((wq, wk)):
                    for m in range(KD):
                        for k in range(KD):
                            last = nc.tensor.matmul(b_m[n][:, 2 * P * m:2 * P * (m + 1)], w[:, k, P * m:P * (m + 1)],
                                                    xnT[:, k, :], start=(k == 0), stop=(k == KD - 1))
                    last.then_inc(qk_done, 1)
                for n in range(NG):
                    for a in range(A):
                        for k in range(KD):
                            cols = wv[:, k, :].rearrange("p (q a d) -> p a q d", a=A, d=DH)[:, a]
                            last = nc.tensor.matmul(b_o[GT * a:GT * (a + 1), P * n:P * (n + 1)],
                                                    xnT[:, k, GT * n:GT * (n + 1)], cols,
                                                    start=(k == 0), stop=(k == KD - 1))
                last.then_inc(v_done, 1)
                for c in range(QT):
                    for n, (picked, ready) in enumerate(((q_picked, q_ready), (k_picked, k_ready))):
                        if c == 0:
                            pe.wait_ge(lo_ready, ONE + 4 * i + 2 * n + 2)
                        else:
                            pe.wait_ge(ready, ONE + QT * i + c)
                        for a in range(A):
                            m, piece = (A * c + a) // HC, (A * c + a) % HC
                            for j, part in enumerate((part_hi, part_lo)):
                                last = nc.tensor.matmul(b_m[n][0:ST, 2 * P * a:2 * P * (a + 1)],
                                                        pick[2 * n + j][:, piece, :], part[:, n, m, :],
                                                        start=(j == 0), stop=(j == 1))
                        last.then_inc(picked, 1)
                pe.wait_ge(q_ready, ONE + QT * i + QT)
                pe.wait_ge(k_ready, ONE + QT * i + QT)

                def maxT(n):
                    pe.wait_ge(max_ready, ONE + U * i + QT * (n + 1))
                    if n >= 2:
                        pe.wait_ge(fold_ready, ONE + NG * i + n - 1)
                    nc.tensor.transpose(b_m[n % 2][:, 0:P], nmax[:, n, :], g.ident[:]).then_inc(maxT_done, 1)

                for u in range(U):
                    n, q = u // QT, u % QT
                    if u >= 2:
                        pe.wait_ge(max_ready, ONE + U * i + u - 1)
                    else:
                        pe.wait_ge(exp_ready, ONE + U * i)
                    for hf in range(L // HALF):
                        last = nc.tensor.matmul(b_s[u % 2][:, HALF * hf:HALF * (hf + 1)], qs[0:ST, n, P * q:P * (q + 1)],
                                                ks[0:ST, n, HALF * hf:HALF * (hf + 1)], start=True, stop=True)
                    last.then_inc(s_done, 1)
                    if n and q == 1:
                        maxT(n - 1)
                maxT(NG - 1)

                def values(k):
                    pe.wait_ge(exp_ready, ONE + U * i + NG * (k + 1))
                    for hf in range(L // HALF):
                        for n in range(NG):
                            last = nc.tensor.matmul(b_o[BL * n:BL * (n + 1), HALF * hf:HALF * (hf + 1)], v[:, n, k, :],
                                                    probT[NG * k % PT_SLOTS + n][:, HALF * hf:HALF * (hf + 1)],
                                                    start=(k == 0), stop=(k == QT - 1))
                    last.then_inc(pv_done, 1)

                pe.wait_ge(v_ready, ONE + i + 1)
                pe.wait_ge(max_ready, ONE + U * i + U)
                for k in range(QT):
                    for n in range(NG):
                        u = NG * k + n
                        if k == 0:
                            pe.wait_ge(fold_ready, ONE + NG * i + n + 1)
                        if u >= 2:
                            pe.wait_ge(exp_ready, ONE + U * i + u - 1)
                        for hf in range(L // HALF):
                            last = nc.tensor.matmul(b_s[u % 2][:, HALF * hf:HALF * (hf + 1)], ks[:, n, P * k:P * (k + 1)],
                                                    qs[:, n, HALF * hf:HALF * (hf + 1)], start=True, stop=True)
                        last.then_inc(sT_done, 1)
                    if k:
                        values(k - 1)
                values(QT - 1)
                pe.wait_ge(o_ready, ONE + i + 1)
                for q in range(QT):
                    last = nc.tensor.transpose(b_m[q // 4][:, P * (q % 4):P * (q % 4 + 1)], o[:, P * q:P * (q + 1)], g.ident[:])
                last.then_inc(ctx_done, 1)
                pe.wait_ge(ctxn_ready, ONE + 2 * i + 2)
                for n in range(NG):
                    last = nc.tensor.transpose(b_m[0][:, P * n:P * (n + 1)], ctxn[:, n].rearrange("p q d -> p (q d)"), g.ident[:])
                last.then_inc(ctxT_done, 1)
                for s in range(2):
                    pe.wait_ge(ctxT_ready, ONE + 2 * i + s + 1)
                    for a in range(A):
                        last = nc.tensor.matmul((b_m[1], b_o)[s][:, 0:D], ctxT[:, s, a, :], wo[:, a, :],
                                                start=(a == 0), stop=(a == A - 1))
                    last.then_inc(y_done, 1)


def norm_residual(nc, g, r_all):
    C = 4
    with phase(nc) as (e, semaphore, begin):
        sb = lambda n, shape, dt=F32: e.enter_context(nc.sbuf_tensor(f"nr_{n}", shape, dt))
        sem = lambda n: semaphore(f"nr_{n}")
        gamma, beta = sb("gamma", [P, D]), sb("beta", [P, D])
        rn = [sb(f"rn{s}", [P, C, D]) for s in range(2)]
        w_in, xb_ready, rn_ready, scaled, x_ready, stats_ready = [sem(n) for n in (
            "w_in", "xb_ready", "rn_ready", "scaled", "x_ready", "stats_ready")]
        block = begin()
        over = lambda a: a[:].unsqueeze(1).broadcast_to([P, C, D])

        @block.sync
        def _(sp):
            for w, src in ((gamma, g.ins["L1_attn_gamma"]), (beta, g.ins["L1_attn_beta"])):
                sp.dma_start(w[:], src.rearrange("(o n) -> o n", o=1).broadcast_to([P, D])).then_inc(w_in, 16)

        @block.gpsimd
        def _(pool):
            pool.wait_ge(w_in, ONE + 32)
            with pool.Fori(0, T // C) as i:
                xt = g.x[:, bass.ds(C * i, C), :]
                nc.gpsimd.tensor_tensor(xt, xt, over(beta), ALU.add).then_inc(xb_ready, 1)

        @block.vector
        def _(dve):
            dve.wait_ge(w_in, ONE + 32)
            with dve.Fori(0, T // C // 2) as i:
                for s in range(2):
                    n = 2 * i + s
                    dve.wait_ge(x_ready, ONE + 2 * i)
                    for c in range(C):
                        t = C * n + c
                        last = nc.vector.tensor_scalar(rn[s][:, c, :], r_all[:, bass.ds(t, 1), :].rearrange("p o d -> p (o d)"),
                                                       g.mean[:, bass.ds(t, 1)], g.rstd[:, bass.ds(t, 1)],
                                                       ALU.subtract, ALU.mult)
                    last.then_inc(rn_ready, 1)
                    dve.wait_ge(rn_ready, ONE + n + 1)
                    nc.vector.tensor_tensor(rn[s][:], rn[s][:], over(gamma), ALU.mult).then_inc(scaled, 1)
                    dve.wait_ge(scaled, ONE + n + 1)
                    dve.wait_ge(xb_ready, ONE + n + 1)
                    xt = g.x[:, bass.ds(C * n, C), :]
                    nc.vector.tensor_tensor(xt, rn[s][:], xt, ALU.add).then_inc(x_ready, 1)
            dve.wait_ge(x_ready, ONE + T // C)
            with dve.Fori(0, T) as t:
                nc.vector.bn_stats(g.stats[:, bass.ds(t, 1), :], g.x[:, bass.ds(t, 1), :]).then_inc(stats_ready, 1)


SINKHORN_ITERS, CLIP = 8, 1e-6


def sinkhorn(nc, g, logits, gates):
    E = logits.shape[2]
    with phase(nc) as (e, semaphore, begin):
        sb = lambda n, shape, dt=F32: e.enter_context(nc.sbuf_tensor(f"sk_{n}", shape, dt))
        sem = lambda n: semaphore(f"sk_{n}")
        ones = sb("ones", [P, P])
        p = sb("p", [P, B, TB, E])
        token_sum, expert_sum = sb("token_sum", [P, B, E]), sb("expert_sum", [P, B, TB])
        ones_set, step, p_ready, sums_done = sem("ones_set"), sem("step"), sem("p_ready"), sem("sums_done")
        bank = g.bank[0]
        block = begin()

        @block.gpsimd
        def _(pool):
            nc.gpsimd.memset(ones[:], 1.0).then_inc(ones_set, 1)

        @block.tensor
        def _(pe):
            pe.wait_ge(ones_set, ONE + 1)
            for n in range(SINKHORN_ITERS):
                pe.wait_ge(p_ready, ONE + n + 1)
                nc.tensor.matmul(bank[:, 0:T * E], ones[:], p[:].rearrange("p b q e -> p (b q e)"),
                                 start=True, stop=True).then_inc(sums_done, 1)

        @block.vector
        def _(dve):
            link = Chain(dve, step)
            nc.vector.tensor_scalar(p[:].rearrange("p b q e -> p (b q) e"), logits[:], CLIP, None, ALU.max).then_inc(p_ready, 1)
            for n in range(SINKHORN_ITERS):
                dve.wait_ge(sums_done, ONE + n + 1)
                link(nc.vector.tensor_reduce(token_sum[:], bank[:, 0:T * E].rearrange("p (b q e) -> p b e q", b=B, q=TB),
                                             axis=AX.X, op=ALU.add))
                link(nc.vector.reciprocal(token_sum[:], token_sum[:]))
                link(nc.vector.tensor_tensor(p[:], p[:], token_sum[:].unsqueeze(2).broadcast_to([P, B, TB, E]), ALU.mult))
                link(nc.vector.tensor_reduce(expert_sum[:], p[:], axis=AX.X, op=ALU.add))
                link(nc.vector.reciprocal(expert_sum[:], expert_sum[:]))
                last = n == SINKHORN_ITERS - 1
                dst = gates[:].rearrange("p q b e -> p b q e") if last else p[:]
                nc.vector.tensor_tensor(dst, p[:], expert_sum[:].unsqueeze(3).broadcast_to([P, B, TB, E]),
                                        ALU.mult).then_inc(p_ready, 1)


def top_tokens(nc, g, gates, index, value, place):
    E = gates.shape[3]
    BE, M = B * E, S // E
    ROUNDS = M // 8
    with phase(nc) as (e, semaphore, begin):
        sb = lambda n, shape, dt=F32: e.enter_context(nc.sbuf_tensor(f"tt_{n}", shape, dt))
        sem = lambda n: semaphore(f"tt_{n}")
        left = [sb(f"left{k}", [BE, S]) for k in range(2)]
        top, top_at = sb("top", [BE, M]), sb("top_at", [BE, M], U32)
        top_at_f = sb("top_at_f", [BE, M])
        indexT = sb("indexT", [M, BE])
        batch_row = sb("batch_row", [M, B, E])
        token = sb("token", [M, S], F16)
        rank1 = sb("rank1", [M, 1], BF16)
        expert = sb("expert", [P, E])
        tile_base = sb("tile_base", [P, B, TB])
        is_token = [sb(f"is_token{k}", [M, S], BF16) for k in range(2)]
        key = sb("key", [P, B, E, TB])
        best, best_i = sb("best", [P, T]), sb("best_i", [P, T], I32)
        best_e, best_r = sb("best_e", [P, T], I32), sb("best_r", [P, T], I32)
        row, has = sb("row", [P, T]), sb("has", [P, T])
        consts, gT_done, step, top_ready, topT_done, topT_ready = [sem(n) for n in (
            "consts", "gT_done", "step", "top_ready", "topT_done", "topT_ready")]
        is_ready, rank_done = sem("is_ready"), sem("rank_done")
        b_g, b_t, b_r = g.bank2[0], g.bank[2], g.bank[3]
        block = begin()

        @block.gpsimd
        def _(pool):
            io = dict(allow_small_or_imprecise_dtypes=True)
            nc.gpsimd.iota(token[:], pattern=[[1, S]], base=0, channel_multiplier=0, **io)
            nc.gpsimd.iota(rank1[:], pattern=[[0, 1]], base=1, channel_multiplier=1, **io)
            nc.gpsimd.iota(expert[:], pattern=[[1, E]], base=0, channel_multiplier=0, **io)
            nc.gpsimd.iota(batch_row[:], pattern=[[S, B], [0, E]], base=0, channel_multiplier=0, **io)
            nc.gpsimd.iota(tile_base[:], pattern=[[E * M, B], [0, TB]], base=-1, channel_multiplier=0, **io).then_inc(consts, 1)

        @block.tensor
        def _(pe):
            for q in range(TB):
                last = nc.tensor.transpose(b_g[0:BE, P * q:P * (q + 1)], gates[:, q].rearrange("p b e -> p (b e)"), g.ident[:])
            last.then_inc(gT_done, 1)
            pe.wait_ge(top_ready, ONE + 1)
            nc.tensor.transpose(b_t[:, 0:BE], top[:], g.ident[0:BE, 0:BE])
            nc.tensor.transpose(b_t[:, BE:2 * BE], top_at_f[:], g.ident[0:BE, 0:BE]).then_inc(topT_done, 1)
            pe.wait_ge(consts, ONE + 1)
            for n in range(BE):
                pe.wait_ge(is_ready, ONE + n + 1)
                for q in range(TB):
                    last = nc.tensor.matmul(b_r[:, TB * n + q:TB * n + q + 1], is_token[n % 2][:, P * q:P * (q + 1)],
                                            rank1[:], start=True, stop=True)
                last.then_inc(rank_done, 1)

        @block.vector
        def _(dve):
            link = Chain(dve, step)
            dve.wait_ge(gT_done, ONE + 1)
            link(nc.vector.tensor_copy(left[0][:], b_g[0:BE, :]))
            for r in range(ROUNDS):
                eight = slice(8 * r, 8 * r + 8)
                link(nc.vector.max(out=top[:, eight], in_=left[r % 2][:]))
                link(nc.vector.max_index(out=top_at[:, eight], in_max=top[:, eight], in_values=left[r % 2][:]))
                if r < ROUNDS - 1:
                    link(nc.vector.match_replace(out=left[(r + 1) % 2][:], in_to_replace=top[:, eight],
                                                 in_values=left[r % 2][:], imm_value=-1.0))
            nc.vector.tensor_copy(top_at_f[:], top_at[:]).then_inc(top_ready, 1)
            dve.wait_ge(topT_done, ONE + 1)
            nc.vector.tensor_copy(value[:], b_t[:, 0:BE])
            link(nc.vector.tensor_copy(indexT[:], b_t[:, BE:2 * BE]))
            dve.wait_ge(consts, ONE + 1)
            nc.vector.tensor_tensor(index[:], indexT[:], batch_row[:].rearrange("p b e -> p (b e)"), ALU.add)
            for n in range(BE):
                if n >= 2:
                    dve.wait_ge(rank_done, ONE + n - 1)
                nc.vector.tensor_scalar(is_token[n % 2][:], token[:], indexT[:, n:n + 1], None, ALU.is_equal).then_inc(is_ready, 1)
            dve.wait_ge(rank_done, ONE + BE)
            link(nc.vector.tensor_scalar(key[:].rearrange("p b e q -> p (b e q)"), b_r[:, 0:BE * TB], float(E), None, ALU.mult))
            link(nc.vector.tensor_tensor(key[:], key[:], expert[:].unsqueeze(1).unsqueeze(3).broadcast_to([P, B, E, TB]), ALU.add))
            link(nc.vector.tensor_reduce(best[:].rearrange("p (b q) -> p b q", b=B), key[:].rearrange("p b e q -> p b q e"),
                                         axis=AX.X, op=ALU.max))
            link(nc.vector.tensor_copy(best_i[:], best[:]))
            link(nc.vector.tensor_scalar(best_e[:], best_i[:], E - 1, None, ALU.bitwise_and))
            link(nc.vector.tensor_scalar(best_r[:], best_i[:], E.bit_length() - 1, None, ALU.logical_shift_right))
            link(nc.vector.scalar_tensor_tensor(row[:], best_e[:], float(M), best_r[:], ALU.mult, ALU.add))
            link(nc.vector.tensor_tensor(row[:], row[:], tile_base[:].rearrange("p b q -> p (b q)"), ALU.add))
            link(nc.vector.tensor_scalar(has[:], best_r[:], 0.0, None, ALU.is_gt))
            link(nc.vector.scalar_tensor_tensor(row[:], row[:], float(-N), has[:], ALU.add, ALU.mult))
            link(nc.vector.tensor_scalar(place[:], row[:], float(N), None, ALU.add))


def routed_experts(nc, g, rows, outputs, index, value, place, out):
    E = g.ins["L1_ffn_experts"].shape[0]
    BE, M = B * E, S // E
    SL = 4
    with phase(nc) as (e, semaphore, begin):
        sb = lambda n, shape, dt=F32: e.enter_context(nc.sbuf_tensor(f"re_{n}", shape, dt))
        sem = lambda n: semaphore(f"re_{n}")
        w = sb("w", [P, E, KD, D])
        taken = [sb(f"taken{s}", [M, D]) for s in range(SL)]
        takenT = [sb(f"takenT{s}", [P, KD, M]) for s in range(SL)]
        y = [sb(f"y{s}", [M, D]) for s in range(SL)]
        zero = sb("zero", [P, D])
        w_in, zero_set, zero_kept = sem("w_in"), sem("zero_set"), sem("zero_kept")
        taken_in = [semaphore(f"re_taken_in{s}", 0) for s in range(SL)]
        kept = [sem(f"kept{s}") for s in range(SL)]
        t_done, t_ready, y_done, y_ready = [sem(n) for n in ("t_done", "t_ready", "y_done", "y_ready")]
        b_t, b_y = g.bank[0:SL], g.bank[SL:2 * SL]
        block = begin()

        @block.sync
        def _(sp):
            sp.dma_start(w[:], g.ins["L1_ffn_experts"].rearrange("e (k p) n -> p e k n", p=P)).then_inc(w_in, 16)
            sp.wait_ge(zero_set, ONE + 1)
            sp.dma_start(outputs[N:N + P, :], zero[:]).then_inc(zero_kept, 16)
            dst = outputs[0:N, :].rearrange("(b e m) d -> b e m d", b=B, e=E)
            with sp.Fori(0, B) as b:
                for n in range(E):
                    sp.wait_ge(y_ready, ONE + b * E + n + 1)
                    sp.dma_start(dst[bass.ds(b, 1), n, :, :].rearrange("b m d -> (b m) d"), y[n % SL][:]).then_inc(kept[n % SL], 16)
            sp.wait_ge(zero_kept, ONE + 16)
            for s in range(SL):
                sp.wait_ge(kept[s], ONE + 16 * BE // SL)

        @block.gpsimd
        def _(pool):
            nc.gpsimd.memset(zero[:], 0.0).then_inc(zero_set, 1)
            for n in range(BE):
                if n >= SL:
                    pool.wait_ge(t_done, ONE + n - SL + 1)
                nc.gpsimd.indirect_dma_start(out=taken[n % SL][:], out_offset=None, in_=rows,
                                             in_offset=bass.IndirectOffsetOnAxis(ap=index[:, n:n + 1], axis=0)
                                             ).then_inc(taken_in[n % SL], 16)

        @block.tensor
        def _(pe):
            pe.wait_ge(w_in, ONE + 16)
            with pe.Fori(0, B) as b:
                for n in range(E):
                    s, at = n % SL, b * E + n
                    pe.wait_ge(taken_in[s], 16 * (E // SL) * b + 16 * (n // SL + 1))
                    if n >= SL:
                        pe.wait_ge(t_ready, ONE + at - SL + 1)
                    else:
                        pe.wait_ge(t_ready, ONE + b * E)
                    for k in range(KD):
                        last = nc.tensor.transpose(b_t[s][:, M * k:M * (k + 1)], taken[s][:, P * k:P * (k + 1)], g.ident[:])
                    last.then_inc(t_done, 1)
                    pe.wait_ge(t_ready, ONE + at + 1)
                    if n >= SL:
                        pe.wait_ge(y_ready, ONE + at - SL + 1)
                    else:
                        pe.wait_ge(y_ready, ONE + b * E)
                    for k in range(KD):
                        last = nc.tensor.matmul(b_y[s][:, 0:D], takenT[s][:, k, :], w[:, n, k, :],
                                                start=(k == 0), stop=(k == KD - 1))
                    last.then_inc(y_done, 1)

        @block.scalar
        def _(act):
            with act.Fori(0, B) as b:
                for n in range(E):
                    s, at = n % SL, b * E + n
                    act.wait_ge(t_done, ONE + at + 1)
                    if n >= SL:
                        act.wait_ge(y_done, ONE + at - SL + 1)
                    else:
                        act.wait_ge(y_done, ONE + b * E)
                    nc.scalar.activation(takenT[s][:], b_t[s][:, 0:KD * M].rearrange("p (k m) -> p k m", k=KD),
                                         ACT.Copy).then_inc(t_ready, 1)

        @block.vector
        def _(dve):
            with dve.Fori(0, B) as b:
                for n in range(E):
                    s, at = n % SL, b * E + n
                    dve.wait_ge(y_done, ONE + at + 1)
                    if n >= SL:
                        dve.wait_ge(kept[s], ONE + 16 * (E // SL) * b + 16 * (n // SL))
                    else:
                        dve.wait_ge(kept[s], ONE + 16 * (E // SL) * b)
                    nc.vector.tensor_scalar(y[s][:], b_y[s][:, 0:D], value[:, bass.ds(at, 1)], None, ALU.mult).then_inc(y_ready, 1)
    with phase(nc) as (e, semaphore, begin):
        sem = lambda n: semaphore(f"rb_{n}")
        got = [e.enter_context(nc.sbuf_tensor(f"rb_got{s}", [P, D], F32)) for s in range(SL)]
        got_in = [semaphore(f"rb_got_in{s}", 0) for s in range(SL)]
        x_ready, out_done = sem("x_ready"), sem("out_done")
        block = begin()

        @block.gpsimd
        def _(pool):
            for t in range(T):
                if t >= SL:
                    pool.wait_ge(x_ready, ONE + t - SL + 1)
                nc.gpsimd.indirect_dma_start(out=got[t % SL][:], out_offset=None, in_=outputs,
                                             in_offset=bass.IndirectOffsetOnAxis(ap=place[:, t:t + 1], axis=0)
                                             ).then_inc(got_in[t % SL], 16)

        @block.vector
        def _(dve):
            with dve.Fori(0, T // SL) as i:
                for s in range(SL):
                    xt = g.x[:, bass.ds(SL * i + s, 1), :].rearrange("p o d -> p (o d)")
                    dve.wait_ge(got_in[s], 16 * i + 16)
                    nc.vector.tensor_tensor(xt, got[s][:], xt, ALU.add).then_inc(x_ready, 1)

        @block.sync
        def _(sp):
            dst = out.rearrange("b (t p) d -> (b t) p d", p=P)
            with sp.Fori(0, T) as t:
                sp.wait_ge(x_ready, ONE + t + 1)
                sp.dma_start(dst[bass.ds(t, 1), :, :].rearrange("t p d -> (t p) d"),
                             g.x[:, bass.ds(t, 1), :].rearrange("p o d -> p (o d)")).then_inc(out_done, 16)
            sp.wait_ge(out_done, ONE + 16 * T)


def mixture1(nc, g, out):
    E = g.ins["L1_ffn_gate_w"].shape[1]
    BE, M = B * E, S // E
    rows = nc.dram_tensor("routed_rows", [N, D], F32, kind="Internal").ap()
    outputs = nc.dram_tensor("routed_outputs", [N + P, D], F32, kind="Internal").ap()
    with ExitStack() as e:
        sb = lambda n, shape, dt=F32: e.enter_context(nc.sbuf_tensor(f"m1_{n}", shape, dt))
        logits = sb("logits", [P, T, E])
        gates = sb("gates", [P, TB, B, E])
        index, value, place = sb("index", [M, BE], U32), sb("value", [M, BE]), sb("place", [P, T], U32)
        normalised_pairs(nc, g, "np1", g.ins["L1_ffn_gate_w"], None, None, logits, rows_out=rows)
        sinkhorn(nc, g, logits, gates)
        top_tokens(nc, g, gates, index, value, place)
        routed_experts(nc, g, rows, outputs, index, value, place, out)


def program(nc, g, out, stop=""):
    setup(nc, g)
    finish_stats(nc, g, "ln0")
    window_attention(nc, g)
    if stop == "A":
        return
    finish_stats(nc, g, "ln1")
    mixture0(nc, g)
    if stop == "B":
        return
    with nc.sbuf_tensor("r_all", [P, T, D], F32) as r_all:
        finish_stats(nc, g, "ln2")
        group_attention(nc, g, r_all)
        finish_stats(nc, g, "ln3")
        norm_residual(nc, g, r_all)
    if stop == "C":
        return
    finish_stats(nc, g, "ln4")
    mixture1(nc, g, out)


_INS = ['L0_attn_x', 'L0_attn_W_qkv', 'L0_attn_W_out', 'L0_ffn_gate_w', 'L0_ffn_gate_b', 'L0_ffn_rw1', 'L0_ffn_rb1',
        'L0_ffn_rw2', 'L0_ffn_rb2', 'L0_ffn_rw3', 'L0_ffn_rb3', 'L0_ffn_sw1', 'L0_ffn_sb1', 'L0_ffn_sw2', 'L0_ffn_sb2',
        'L0_ffn_sw3', 'L0_ffn_sb3', 'L1_attn_wq', 'L1_attn_bq', 'L1_attn_wk', 'L1_attn_bk', 'L1_attn_wv', 'L1_attn_bv',
        'L1_attn_wo', 'L1_attn_bo', 'L1_attn_gamma', 'L1_attn_beta', 'L1_ffn_gate_w', 'L1_ffn_experts']


def kernel(**inputs):
    import numpy as _np
    import concourse.bacc as _bacc
    from concourse import mybir as _mybir
    from concourse.bass_utils import run_bass_kernel_spmd as _run

    nc = _bacc.Bacc("TRN2", target_bir_lowering=False, num_devices=1)
    arrays, aps = {}, {}
    for name in _INS:
        a = _np.ascontiguousarray(inputs[name])
        arrays[f"in_{name}_dram"] = a
        aps[name] = nc.dram_tensor(f"in_{name}_dram", a.shape, _mybir.dt.from_np(a.dtype), kind="ExternalInput").ap()
    out = nc.dram_tensor("out_0_dram", (B, S, D), F32, kind="ExternalOutput").ap()
    with ExitStack() as ctx:
        program(nc, Shared(ctx, aps), out)
    r = _run(nc, [arrays], core_ids=[0])
    return r.results[0]["out_0_dram"]
```

```python
import concourse.bass as bass
from concourse import mybir
from contextlib import ExitStack, contextmanager

F32 = mybir.dt.float32
F32R = mybir.dt.float32r
BF16 = mybir.dt.bfloat16
F16 = mybir.dt.float16
U32 = mybir.dt.uint32
I32 = mybir.dt.int32
ALU = mybir.AluOpType
ACT = mybir.ActivationFunctionType
AX = mybir.AxisListType

P = 128
B, S, D = 4, 1024, 256
N = B * S
T = N // P
TB = S // P
KD = D // P
NH, DH = 16, 16
SCALE = DH ** -0.5
WIN = 64
LN_EPS = 1e-5
ONE = 1
NEG = -1e30
BN = 6


class Shared:

    def __init__(self, ctx, ins):
        self.ctx, self.ins = ctx, ins


class Chain:

    def __init__(self, eng, sem):
        self.eng, self.sem, self.count = eng, sem, ONE

    def __call__(self, ins):
        ins.then_inc(self.sem, 1)
        self.count += 1
        self.eng.wait_ge(self.sem, self.count)


@contextmanager
def phase(nc):
    sems = []
    with ExitStack() as e:
        def semaphore(name, start=ONE):
            sem = e.enter_context(nc.semaphore(name))
            sems.append((sem, start))
            return sem

        def begin():
            with nc.Block() as block:
                @block.sync
                def _(sp):
                    for sem, _ in sems:
                        sp.sem_clear(sem)
                    for sem, start in sems:
                        if start:
                            sp.sem_inc(sem, start)
            return e.enter_context(nc.Block())

        yield e, semaphore, begin


def setup(nc, g):
    c = g.ctx
    sb = lambda name, shape, dt=F32: c.enter_context(nc.sbuf_tensor(name, shape, dt))
    g.x = sb("x", [P, T, D])
    g.stats = sb("stats", [P, T, BN])
    g.mean = sb("mean", [P, T])
    g.rstd = sb("rstd", [P, T])
    g.ident = sb("ident", [P, P])
    g.bank2 = [c.enter_context(nc.psum_tensor(f"banks{i}", [P, 1024], F32)) for i in range(4)]
    g.bank = [g.bank2[i // 2][:, 512 * (i % 2):512 * (i % 2 + 1)] for i in range(8)]
    with phase(nc) as (e, semaphore, begin):
        x_in = [semaphore(f"x_in{b}") for b in range(B)]
        ident_zero = semaphore("ident_zero")
        ident_set = semaphore("ident_set")
        stats_done = semaphore("stats0_done")
        block = begin()

        @block.sync
        def _(sp):
            for b in range(B):
                src = g.ins["L0_attn_x"][b].rearrange("(t p) d -> p t d", p=P)
                sp.dma_start(g.x[:, b * TB:(b + 1) * TB, :], src).then_inc(x_in[b], 16)

        @block.gpsimd
        def _(pool):
            nc.gpsimd.memset(g.ident[:], 0.0).then_inc(ident_zero, 1)
            pool.wait_ge(ident_zero, ONE + 1)
            nc.gpsimd.affine_select(out=g.ident[:], in_=g.ident[:], compare_op=ALU.not_equal, fill=1.0, base=0,
                                    pattern=[[-1, P]], channel_multiplier=1).then_inc(ident_set, 1)

        @block.vector
        def _(dve):
            for b in range(B):
                dve.wait_ge(x_in[b], ONE + 16)
                with dve.Fori(b * TB, (b + 1) * TB) as t:
                    nc.vector.bn_stats(g.stats[:, bass.ds(t, 1), :], g.x[:, bass.ds(t, 1), :]).then_inc(stats_done, 1)


def finish_stats(nc, g, name):
    with phase(nc) as (e, semaphore, begin):
        sb = lambda n, shape, dt=F32: e.enter_context(nc.sbuf_tensor(f"{name}_{n}", shape, dt))
        diff, var, std = sb("diff", [P, T]), sb("var", [P, T]), sb("std", [P, T])
        eps = sb("eps", [P, 1])
        step = semaphore(f"{name}_step")
        var_ready = semaphore(f"{name}_var_ready")
        std_ready = semaphore(f"{name}_std_ready")
        rstd_ready = semaphore(f"{name}_rstd_ready")
        block = begin()
        half = float(D // 2)

        @block.vector
        def _(dve):
            link = Chain(dve, step)
            even, odd = g.stats[:, :, 1], g.stats[:, :, 4]
            nc.vector.memset(eps[:], LN_EPS)
            nc.vector.tensor_tensor(g.mean[:], even, odd, ALU.add)
            nc.vector.tensor_tensor(var[:], g.stats[:, :, 2], g.stats[:, :, 5], ALU.add)
            link(nc.vector.tensor_tensor(diff[:], even, odd, ALU.subtract))
            link(nc.vector.scalar_tensor_tensor(diff[:], diff[:], half / 2.0, diff[:], ALU.mult, ALU.mult))
            link(nc.vector.tensor_tensor(var[:], var[:], diff[:], ALU.add))
            nc.vector.tensor_scalar(var[:], var[:], 1.0 / D, None, ALU.mult).then_inc(var_ready, 1)
            link(nc.vector.tensor_scalar(g.mean[:], g.mean[:], 0.5, None, ALU.mult))
            dve.wait_ge(std_ready, ONE + 1)
            nc.vector.reciprocal(g.rstd[:], std[:]).then_inc(rstd_ready, 1)

        @block.scalar
        def _(act):
            act.wait_ge(var_ready, ONE + 1)
            nc.scalar.activation(std[:], var[:], ACT.Sqrt, bias=eps[:, 0:1]).then_inc(std_ready, 1)


def window_attention(nc, g, to_clear):
    NP = T // 2
    HM = P // DH
    HU = 4
    NU = NH // HU
    R = P // HU
    W2 = 2 * WIN
    Q = P // 2
    with phase(nc) as (e, semaphore, begin):
        sb = lambda n, shape, dt=F32: e.enter_context(nc.sbuf_tensor(f"wa_{n}", shape, dt))
        sem = lambda n: semaphore(f"wa_{n}")
        wqkv = sb("wqkv", [P, KD, 3 * D])
        wo = sb("wo", [P, NU, D])
        ident_bf = sb("ident_bf", [P, P], BF16)
        mask0 = sb("mask0", [P, NP, W2], BF16)
        mask1 = sb("mask1", [P, W2], BF16)
        head_rows = sb("head_rows", [P, HM])
        sum_rows = sb("sum_rows", [P, P])
        xn = [sb(f"xn{s}", [P, D]) for s in range(2)]
        xnT = sb("xnT", [P, KD, WIN + 2 * P])
        kT = sb("kT", [P, KD, WIN + 2 * P])
        q_heads = sb("q_heads", [P, KD, HM, 2 * P])
        v = sb("v", [P, 4, NH, R])
        nmax = [sb(f"nmax{k}", [P, HU]) for k in range(2)]
        ex = [sb(f"ex{k}", [P, HU, W2]) for k in range(2)]
        prob = [sb(f"prob{k}", [P, HU, W2]) for k in range(2)]
        probT = [sb(f"probT{k}", [P, HU, P]) for k in range(2)]
        o = [sb(f"o{s}", [P, NU, P]) for s in range(2)]
        rsum = [sb(f"rsum{s}", [P, NU, P]) for s in range(2)]
        on = [sb(f"on{s}", [P, NU, P]) for s in range(2)]
        zero = sb("zero", [P, D])
        zero_set, cleared = sem("zero_set"), sem("cleared")
        w_in, wo_zero, const = sem("w_in"), sem("wo_zero"), sem("const")
        consts_set, tails_zero, v_set = sem("consts_set"), sem("tails_zero"), sem("v_set")
        xn_ready, xnT_done, xnT_ready = sem("xn_ready"), sem("xnT_done"), sem("xnT_ready")
        qk_done, k_ready, q_ready, v_done, v_ready = sem("qk_done"), sem("k_ready"), sem("q_ready"), sem("v_done"), sem("v_ready")
        tails_moved = sem("tails_moved")
        s_done, max_ready, ex_ready, prob_ready, probT_done, probT_ready = [
            sem(n) for n in ("s_done", "max_ready", "ex_ready", "prob_ready", "probT_done", "probT_ready")]
        o_done, o_ready, sum_done, rsum_ready, on_ready, y_done, x_ready, stats_ready = [
            sem(n) for n in ("o_done", "o_ready", "sum_done", "rsum_ready", "on_ready", "y_done", "x_ready", "stats_ready")]
        b_pt, b_q, b_k, b_v, b_s = [g.bank[7], g.bank[0]], g.bank[1], g.bank[2], g.bank[3:5], g.bank[5:7]
        b_tp = b_pt
        block = begin()
        half = lambda n: slice(n * Q, (n + 1) * Q)

        @block.sync
        def _(sp):
            sp.dma_start(wqkv[:], g.ins["L0_attn_W_qkv"].rearrange("(k p) n -> p k n", p=P)).then_inc(w_in, 16)
            sp.wait_ge(wo_zero, ONE + 1)
            for j in range(HU):
                src = g.ins["L0_attn_W_out"].rearrange("(m j d) n -> j d m n", j=HU, d=DH)[j]
                sp.dma_start(wo[R * j:R * j + DH], src).then_inc(w_in, 16)
            sp.wait_ge(zero_set, ONE + 1)
            blocks = to_clear.shape[0] // P
            sp.dma_start(to_clear.rearrange("(j p) d -> p j d", p=P),
                         zero[:].unsqueeze(1).broadcast_to([P, blocks, D])).then_inc(cleared, 16)
            sp.wait_ge(cleared, ONE + 16)

        @block.gpsimd
        def _(pool):
            link = Chain(pool, const)
            nc.gpsimd.memset(zero[:], 0.0).then_inc(zero_set, 1)
            nc.gpsimd.memset(wo[:], 0.0).then_inc(wo_zero, 1)
            nc.gpsimd.memset(mask0[:], 0.0)
            nc.gpsimd.memset(mask1[:], 0.0)
            nc.gpsimd.memset(head_rows[:], 1.0)
            nc.gpsimd.memset(xnT[:, :, 0:WIN], 0.0)
            nc.gpsimd.memset(kT[:, :, 0:WIN], 0.0).then_inc(tails_zero, 1)
            link(nc.gpsimd.memset(sum_rows[:], 0.0))
            for h in range(2):
                for m, pat in ((mask0, [[0, NP]]), (mask1, [])):
                    m = m[half(h)]
                    link(nc.gpsimd.affine_select(out=m, in_=m, compare_op=ALU.is_ge, fill=NEG, base=WIN,
                                                 pattern=pat + [[-1, W2]], channel_multiplier=1))
                    link(nc.gpsimd.affine_select(out=m, in_=m, compare_op=ALU.is_ge, fill=NEG, base=-1,
                                                 pattern=pat + [[1, W2]], channel_multiplier=-1))
            m = mask0[half(0)].rearrange("p (b j) w -> p b j w", b=B)[:, :, 0, :]
            nc.gpsimd.affine_select(out=m, in_=m, compare_op=ALU.is_ge, fill=NEG, base=-WIN,
                                    pattern=[[0, B], [1, W2]], channel_multiplier=0)
            link(nc.gpsimd.affine_select(out=head_rows[:], in_=head_rows[:], compare_op=ALU.is_ge, fill=0.0, base=0,
                                         pattern=[[-DH, HM]], channel_multiplier=1))
            link(nc.gpsimd.affine_select(out=head_rows[:], in_=head_rows[:], compare_op=ALU.is_ge, fill=0.0,
                                         base=DH - 1, pattern=[[DH, HM]], channel_multiplier=-1))
            sr = sum_rows[:].rearrange("p (j r) -> p j r", j=HU)
            link(nc.gpsimd.affine_select(out=sr, in_=sr, compare_op=ALU.not_equal, fill=1.0, base=-DH,
                                         pattern=[[-R, HU], [0, R]], channel_multiplier=1))
            nc.gpsimd.tensor_copy(ident_bf[:], g.ident[:]).then_inc(consts_set, 1)

        @block.vector
        def _(dve):
            nc.vector.memset(v[:], 0.0).then_inc(max_ready, 1)
            dve.wait_ge(max_ready, ONE + 1)
            nc.vector.memset(v[:, :, :, DH:DH + 1], 1.0).then_inc(v_set, 1)
            dve.wait_ge(consts_set, ONE + 1)

            with dve.Fori(0, NP) as i:
                def normalise(s):
                    dve.wait_ge(sum_done, ONE + 2 * i + s + 1)
                    nc.vector.reciprocal(rsum[s][:], b_v[s][:].rearrange("p (m q) -> p m q", m=NU)).then_inc(rsum_ready, 1)
                    dve.wait_ge(rsum_ready, ONE + 2 * i + s + 1)
                    nc.vector.tensor_tensor(on[s][:], o[s][:], rsum[s][:], ALU.mult).then_inc(on_ready, 1)

                def residual(s):
                    xt = g.x[:, bass.ds(2 * i + s, 1), :].rearrange("p o d -> p (o d)")
                    dve.wait_ge(y_done, ONE + 2 * i + s + 1)
                    nc.vector.tensor_tensor(xt, (b_q, b_k)[s][:, 0:D], xt, ALU.add).then_inc(x_ready, 1)
                    dve.wait_ge(x_ready, ONE + 2 * i + s + 1)
                    nc.vector.bn_stats(g.stats[:, bass.ds(2 * i + s, 1), :], xt).then_inc(stats_ready, 1)

                for s in range(2):
                    t = 2 * i + s
                    dve.wait_ge(xnT_done, ONE + 2 * i)
                    nc.vector.tensor_scalar(xn[s][:], g.x[:, bass.ds(t, 1), :].rearrange("p o d -> p (o d)"),
                                            g.mean[:, bass.ds(t, 1)], g.rstd[:, bass.ds(t, 1)],
                                            ALU.subtract, ALU.mult).then_inc(xn_ready, 1)
                dve.wait_ge(qk_done, ONE + 2 * i + 1)
                dve.wait_ge(s_done, ONE + 2 * NU * i)
                for k in range(KD):
                    qb = b_q[:, 2 * P * k:2 * P * (k + 1)].unsqueeze(1).broadcast_to([P, HM, 2 * P])
                    hb = head_rows[:].unsqueeze(2).broadcast_to([P, HM, 2 * P])
                    nc.vector.tensor_tensor(q_heads[:, k], qb, hb, ALU.mult).then_inc(q_ready, 1)
                for u in range(2 * NU):
                    n = 2 * NU * i + u + 1
                    k = u % 2
                    sc = b_s[k][:].rearrange("p (h w) -> p h w", h=HU)
                    dve.wait_ge(s_done, ONE + n)
                    if u >= 2:
                        dve.wait_ge(prob_ready, ONE + n - 2)
                    else:
                        dve.wait_ge(prob_ready, ONE + 2 * NU * i)
                    nc.vector.tensor_reduce(nmax[k][:], sc, axis=AX.X, op=ALU.max, negate=True).then_inc(max_ready, 1)
                    dve.wait_ge(max_ready, ONE + n + 1)
                    nc.vector.tensor_tensor(ex[k][:], sc, nmax[k][:].unsqueeze(2).broadcast_to([P, HU, W2]),
                                            ALU.add).then_inc(ex_ready, 1)
                    if u == NU + 2:
                        normalise(0)
                    if u == NU + 3:
                        residual(0)
                normalise(1)
                residual(1)

        @block.scalar
        def _(act):
            act.wait_ge(tails_zero, ONE + 1)
            act.wait_ge(v_set, ONE + 1)
            with act.Fori(0, NP) as i:
                for s in range(2):
                    act.wait_ge(xnT_done, ONE + 2 * i + s + 1)
                    act.wait_ge(tails_moved, ONE + 2 * i)
                    nc.scalar.activation(xnT[:, :, WIN + P * s:WIN + P * (s + 1)],
                                         b_tp[s][:, 0:D].rearrange("p (k q) -> p k q", k=KD),
                                         ACT.Copy).then_inc(xnT_ready, 1)
                act.wait_ge(qk_done, ONE + 2 * i + 2)
                nc.scalar.activation(kT[:, :, WIN:WIN + 2 * P], b_k[:].rearrange("p (k q) -> p k q", k=KD),
                                     ACT.Copy).then_inc(k_ready, 1)
                for s in range(2):
                    act.wait_ge(v_done, ONE + 2 * i + s + 1)
                    act.wait_ge(o_done, ONE + 2 * i)
                    nc.scalar.activation(v[:, 2 * s:2 * s + 2, :, 0:DH],
                                         b_v[s][:].rearrange("p (a h d) -> p a h d", a=2, h=NH),
                                         ACT.Copy).then_inc(v_ready, 1)

                def transposed(u):
                    n = 2 * NU * i + u + 1
                    k = u % 2
                    act.wait_ge(probT_done, ONE + n)
                    nc.scalar.activation(probT[k][:], b_pt[k][:].rearrange("p (h q) -> p h q", h=HU),
                                         ACT.Copy).then_inc(probT_ready, 1)

                for u in range(2 * NU):
                    n = 2 * NU * i + u + 1
                    k = u % 2
                    act.wait_ge(ex_ready, ONE + n)
                    nc.scalar.activation(prob[k][:], ex[k][:], ACT.Exp, scale=SCALE).then_inc(prob_ready, 1)
                    if u >= 1:
                        transposed(u - 1)
                    if u == NU:
                        act.wait_ge(o_done, ONE + 2 * i + 1)
                        nc.scalar.activation(o[0][:], b_q[:].rearrange("p (m q) -> p m q", m=NU), ACT.Copy).then_inc(o_ready, 1)
                transposed(2 * NU - 1)
                act.wait_ge(o_done, ONE + 2 * i + 2)
                nc.scalar.activation(o[1][:], b_k[:].rearrange("p (m q) -> p m q", m=NU), ACT.Copy).then_inc(o_ready, 1)
                act.wait_ge(xnT_ready, ONE + 2 * i + 2)
                act.wait_ge(v_done, ONE + 2 * i + 2)
                nc.scalar.activation(xnT[:, :, 0:WIN], xnT[:, :, 2 * P:2 * P + WIN], ACT.Copy).then_inc(tails_moved, 1)
                act.wait_ge(k_ready, ONE + i + 1)
                act.wait_ge(s_done, ONE + 2 * NU * i + 2 * NU)
                nc.scalar.activation(kT[:, :, 0:WIN], kT[:, :, 2 * P:2 * P + WIN], ACT.Copy).then_inc(tails_moved, 1)

        @block.tensor
        def _(pe):
            pe.wait_ge(w_in, ONE + 16 * (1 + HU))
            pe.wait_ge(consts_set, ONE + 1)
            with pe.Fori(0, NP) as i:
                for s in range(2):
                    pe.wait_ge(xn_ready, ONE + 2 * i + s + 1)
                    pe.wait_ge(probT_ready, ONE + 2 * NU * i)
                    for k in range(KD):
                        last = nc.tensor.transpose(b_tp[s][:, P * k:P * (k + 1)],
                                                   xn[s][:, P * k:P * (k + 1)], g.ident[:])
                    last.then_inc(xnT_done, 1)
                pe.wait_ge(xnT_ready, ONE + 2 * i + 2)
                pe.wait_ge(x_ready, ONE + 2 * i)
                for part, bank in enumerate((b_q, b_k)):
                    for m in range(KD):
                        for k in range(KD):
                            last = nc.tensor.matmul(bank[:, 2 * P * m:2 * P * (m + 1)],
                                                    wqkv[:, k, D * part + P * m:D * part + P * (m + 1)],
                                                    xnT[:, k, WIN:WIN + 2 * P], start=(k == 0), stop=(k == KD - 1))
                    last.then_inc(qk_done, 1)
                pe.wait_ge(rsum_ready, ONE + 2 * i)
                for s in range(2):
                    for h in range(2):
                        at = P * s + Q * h
                        for k in range(KD):
                            last = nc.tensor.matmul(b_v[s][:, D * h:D * (h + 1)], xnT[:, k, at:at + P],
                                                    wqkv[:, k, 2 * D:3 * D], start=(k == 0), stop=(k == KD - 1))
                    last.then_inc(v_done, 1)
                pe.wait_ge(k_ready, ONE + i + 1)
                pe.wait_ge(tails_moved, ONE + 2 * i)

                def scores(u):
                    s, m = u // NU, u % NU
                    n = 2 * NU * i + u + 1
                    bank = b_s[u % 2]
                    if m == 0 and s == 0:
                        pe.wait_ge(q_ready, ONE + 2 * i + 1)
                    if m == 2 and s == 0:
                        pe.wait_ge(q_ready, ONE + 2 * i + 2)
                    if u >= 2:
                        pe.wait_ge(ex_ready, ONE + n - 2)
                    else:
                        pe.wait_ge(ex_ready, ONE + 2 * NU * i)
                    mask = mask1[:].unsqueeze(1) if s else mask0[:, bass.ds(i, 1), :]
                    nc.tensor.matmul(bank[:].rearrange("p (h w) -> p h w", h=HU), ident_bf[:],
                                     mask.broadcast_to([P, HU, W2]), start=True, stop=False, skip_group_check=True)
                    k = m // (HM // HU)
                    for j in range(HU):
                        head = HU * m % HM + j
                        for h in range(2):
                            at = P * s + Q * h
                            last = nc.tensor.matmul(bank[half(h), W2 * j:W2 * (j + 1)],
                                                    q_heads[:, k, head, at:at + Q], kT[:, k, at:at + P],
                                                    start=False, stop=True, skip_group_check=True)
                    last.then_inc(s_done, 1)

                def transposes(u):
                    n = 2 * NU * i + u + 1
                    pe.wait_ge(prob_ready, ONE + n)
                    if u >= 2:
                        pe.wait_ge(probT_ready, ONE + n - 2)
                    else:
                        pe.wait_ge(probT_ready, ONE + 2 * NU * i)
                    for j in range(HU):
                        last = nc.tensor.transpose(b_pt[u % 2][:, P * j:P * (j + 1)], prob[u % 2][:, j, :], g.ident[:])
                    last.then_inc(probT_done, 1)

                def outputs(u):
                    s, m = u // NU, u % NU
                    n = 2 * NU * i + u + 1
                    if m == 0:
                        pe.wait_ge(v_ready, ONE + 2 * i + s + 1)
                    if u == 0:
                        pe.wait_ge(k_ready, ONE + i + 1)
                        pe.wait_ge(q_ready, ONE + 2 * i + 2)
                    pe.wait_ge(probT_ready, ONE + n)
                    for j in range(HU):
                        for h in range(2):
                            last = nc.tensor.matmul((b_q, b_k)[s][R * j:R * (j + 1), P * m + Q * h:P * m + Q * (h + 1)],
                                                    v[:, 2 * s + h, HU * m + j, :], probT[u % 2][:, j, half(h)],
                                                    start=True, stop=True)
                    if m == NU - 1:
                        last.then_inc(o_done, 1)

                def sums(s):
                    pe.wait_ge(o_ready, ONE + 2 * i + s + 1)
                    nc.tensor.matmul(b_v[s][:], sum_rows[:], o[s][:], start=True, stop=True).then_inc(sum_done, 1)

                def project(s):
                    pe.wait_ge(on_ready, ONE + 2 * i + s + 1)
                    for m in range(NU):
                        last = nc.tensor.matmul((b_q, b_k)[s][:, 0:D], on[s][:, m, :], wo[:, m, :],
                                                start=(m == 0), stop=(m == NU - 1))
                    last.then_inc(y_done, 1)

                scores(0)
                for u in range(2 * NU):
                    if u + 1 < 2 * NU:
                        scores(u + 1)
                    transposes(u)
                    if u >= 1:
                        outputs(u - 1)
                    if u == NU + 1:
                        sums(0)
                    if u == NU + 3:
                        project(0)
                outputs(2 * NU - 1)
                sums(1)
                project(1)


def normalised_pairs(nc, g, name, gate, gate_b, xnT_all, logits, rows_out=None):
    E = logits.shape[2]
    with phase(nc) as (e, semaphore, begin):
        sb = lambda n, shape, dt=F32: e.enter_context(nc.sbuf_tensor(f"{name}_{n}", shape, dt))
        sem = lambda n: semaphore(f"{name}_{n}")
        gw = sb("gw", [P, KD, E])
        gb = sb("gb", [P, E])
        xn = [sb(f"xn{s}", [P, D]) for s in range(2)]
        xnT = [sb(f"xnT{s}", [P, KD, P]) for s in range(2)]
        gate_in, gb_zero = sem("gate_in"), sem("gb_zero")
        xn_ready, xnT_done, xnT_ready, kept, l_done, l_ready = [
            sem(n) for n in ("xn_ready", "xnT_done", "xnT_ready", "kept", "l_done", "l_ready")]
        rows_kept = [sem(f"rows_kept{s}") for s in range(2)]
        block = begin()
        b_tp, b_l = g.bank[0:2], g.bank[2:4]

        @block.sync
        def _(sp):
            sp.dma_start(gw[:], gate.rearrange("(k p) e -> p k e", p=P)).then_inc(gate_in, 16)
            if gate_b is not None:
                sp.dma_start(gb[:], gate_b.rearrange("(o e) -> o e", o=1).broadcast_to([P, E])).then_inc(gate_in, 16)
            if rows_out is not None:
                rows = rows_out.rearrange("(t p) d -> t p d", p=P)
                with sp.Fori(0, T // 2) as i:
                    for s in range(2):
                        sp.wait_ge(xn_ready, ONE + 2 * i + s + 1)
                        dst = rows[bass.ds(2 * i + s, 1), :, :].rearrange("t p d -> (t p) d")
                        sp.dma_start(dst, xn[s][:]).then_inc(rows_kept[s], 16)
                for s in range(2):
                    sp.wait_ge(rows_kept[s], ONE + 16 * (T // 2))

        @block.vector
        def _(dve):
            if gate_b is None:
                nc.vector.memset(gb[:], 0.0).then_inc(gb_zero, 1)
                dve.wait_ge(gb_zero, ONE + 1)
            else:
                dve.wait_ge(gate_in, ONE + 32)
            with dve.Fori(0, T // 2) as i:
                for s in range(2):
                    t = 2 * i + s
                    dve.wait_ge(xnT_done, ONE + 2 * i)
                    if rows_out is not None:
                        dve.wait_ge(rows_kept[s], ONE + 16 * i)
                    nc.vector.tensor_scalar(xn[s][:], g.x[:, bass.ds(t, 1), :].rearrange("p o d -> p (o d)"),
                                            g.mean[:, bass.ds(t, 1)], g.rstd[:, bass.ds(t, 1)],
                                            ALU.subtract, ALU.mult).then_inc(xn_ready, 1)
                for s in range(2):
                    dve.wait_ge(l_done, ONE + 2 * i + s + 1)
                    nc.vector.tensor_tensor(logits[:, bass.ds(2 * i + s, 1), :].rearrange("p o e -> p (o e)"),
                                            b_l[s][:, 0:E], gb[:], ALU.add).then_inc(l_ready, 1)

        @block.scalar
        def _(act):
            with act.Fori(0, T // 2) as i:
                for s in range(2):
                    act.wait_ge(xnT_done, ONE + 2 * i + s + 1)
                    act.wait_ge(l_done, ONE + 2 * i)
                    if xnT_all is not None:
                        act.wait_ge(kept, ONE + 2 * i)
                    nc.scalar.activation(xnT[s][:], b_tp[s][:, 0:D].rearrange("p (k q) -> p k q", k=KD),
                                         ACT.Copy).then_inc(xnT_ready, 1)

        @block.gpsimd
        def _(pool):
            if xnT_all is not None:
                with pool.Fori(0, T // 2) as i:
                    for s in range(2):
                        pool.wait_ge(xnT_ready, ONE + 2 * i + s + 1)
                        nc.gpsimd.tensor_copy(xnT_all[:, :, bass.ds((2 * i + s) * P, P)], xnT[s][:]).then_inc(kept, 1)

        @block.tensor
        def _(pe):
            pe.wait_ge(gate_in, ONE + (16 if gate_b is None else 32))
            with pe.Fori(0, T // 2) as i:
                for s in range(2):
                    pe.wait_ge(xn_ready, ONE + 2 * i + s + 1)
                    pe.wait_ge(xnT_ready, ONE + 2 * i)
                    for k in range(KD):
                        last = nc.tensor.transpose(b_tp[s][:, P * k:P * (k + 1)], xn[s][:, P * k:P * (k + 1)], g.ident[:])
                    last.then_inc(xnT_done, 1)
                for s in range(2):
                    pe.wait_ge(xnT_ready, ONE + 2 * i + s + 1)
                    pe.wait_ge(l_ready, ONE + 2 * i)
                    for k in range(KD):
                        last = nc.tensor.matmul(b_l[s][:, 0:E], xnT[s][:, k, :], gw[:, k, :],
                                                start=(k == 0), stop=(k == KD - 1))
                    last.then_inc(l_done, 1)


def top2_weights(nc, g, logits, w, n_shared, taken, weight):
    E = logits.shape[2]
    with phase(nc) as (e, semaphore, begin):
        sb = lambda n, shape, dt=F32: e.enter_context(nc.sbuf_tensor(f"t2_{n}", shape, dt))
        sem = lambda n: semaphore(f"t2_{n}")
        order, row = sb("order", [P, E]), sb("row", [P, T])
        p, left, pick, first = [sb(n, [P, T, E]) for n in ("p", "left", "pick", "first")]
        step, order_set, shifted, exp_ready = sem("step"), sem("order_set"), sem("shifted"), sem("exp_ready")
        block = begin()
        over = lambda a: a[:].unsqueeze(2).broadcast_to([P, T, E])

        @block.gpsimd
        def _(pool):
            nc.gpsimd.iota(order[:], pattern=[[-1, E]], base=E, channel_multiplier=0,
                           allow_small_or_imprecise_dtypes=True).then_inc(order_set, 1)

        @block.scalar
        def _(act):
            act.wait_ge(shifted, ONE + 1)
            nc.scalar.activation(p[:], p[:], ACT.Exp).then_inc(exp_ready, 1)

        @block.vector
        def _(dve):
            link = Chain(dve, step)
            link(nc.vector.tensor_reduce(row[:], logits[:], axis=AX.X, op=ALU.max))
            nc.vector.tensor_tensor(p[:], logits[:], over(row), ALU.subtract).then_inc(shifted, 1)
            dve.wait_ge(exp_ready, ONE + 1)
            link(nc.vector.tensor_reduce(row[:], p[:], axis=AX.X, op=ALU.add))
            link(nc.vector.reciprocal(row[:], row[:]))
            link(nc.vector.tensor_tensor(p[:], p[:], over(row), ALU.mult))
            dve.wait_ge(order_set, ONE + 1)
            link(nc.vector.tensor_copy(left[:], p[:]))
            for n in range(2):
                link(nc.vector.tensor_reduce(row[:], left[:], axis=AX.X, op=ALU.max))
                link(nc.vector.tensor_tensor(pick[:], left[:], over(row), ALU.is_equal))
                link(nc.vector.tensor_tensor(pick[:], pick[:], order[:].unsqueeze(1).broadcast_to([P, T, E]), ALU.mult))
                link(nc.vector.tensor_reduce(row[:], pick[:], axis=AX.X, op=ALU.max))
                link(nc.vector.tensor_tensor(taken[n][:], pick[:], over(row), ALU.is_equal))
                nc.vector.scalar_tensor_tensor(left[:], taken[n][:], -4.0, left[:], ALU.mult, ALU.add)
                link(nc.vector.tensor_tensor(pick[:], taken[n][:], p[:], ALU.mult))
                link(nc.vector.tensor_reduce(weight[n][:], pick[:], axis=AX.X, op=ALU.add))
            link(nc.vector.tensor_scalar(first[:], left[:], 0.0, None, ALU.is_lt))
            nc.vector.memset(w[:, :, E:E + n_shared], 1.0 / n_shared)
            link(nc.vector.tensor_tensor(w[:, :, 0:E], first[:], p[:], ALU.mult))


def block_slots(nc, g, taken, slot, block_e, block_f):
    E, NB = taken[0].shape[2], block_e.shape[1]
    with phase(nc) as (e, semaphore, begin):
        sb = lambda n, shape, dt=F32: e.enter_context(nc.sbuf_tensor(f"bs_{n}", shape, dt))
        sem = lambda n: semaphore(f"bs_{n}")
        ones, earlier = sb("ones", [P, P]), sb("earlier", [P, P])
        number = sb("number", [P, NB])
        mask, tot = sb("mask", [P, T, E]), sb("tot", [P, T, E])
        run = [sb(f"run{k}", [P, T, E]) for k in range(2)]
        count_i, blocks_i = sb("count_i", [P, E], I32), sb("blocks_i", [P, E], I32)
        blocks, first = sb("blocks", [P, E]), sb("first", [P, E])
        ends = [sb(f"ends{k}", [P, E]) for k in range(2)]
        at, part, slot_f = sb("at", [P, T, E]), sb("part", [P, T, E]), sb("slot_f", [P, T])
        past = sb("past", [P, NB, E])
        step, const, consts_set, mask_ready, sums_done = [sem(n) for n in (
            "step", "const", "consts_set", "mask_ready", "sums_done")]
        b_before, b_tot = g.bank[0], g.bank[1]
        flat = lambda a: a[:].rearrange("p t e -> p (t e)")
        block = begin()

        @block.gpsimd
        def _(pool):
            link = Chain(pool, const)
            nc.gpsimd.iota(number[:], pattern=[[1, NB]], base=0, channel_multiplier=0, allow_small_or_imprecise_dtypes=True)
            nc.gpsimd.memset(ones[:], 1.0)
            link(nc.gpsimd.memset(earlier[:], 1.0))
            nc.gpsimd.affine_select(out=earlier[:], in_=earlier[:], compare_op=ALU.is_ge, fill=0.0, base=-1,
                                    pattern=[[1, P]], channel_multiplier=-1).then_inc(consts_set, 1)

        @block.tensor
        def _(pe):
            pe.wait_ge(consts_set, ONE + 1)
            pe.wait_ge(mask_ready, ONE + 1)
            nc.tensor.matmul(b_before[:, 0:T * E], earlier[:], flat(mask), start=True, stop=True)
            nc.tensor.matmul(b_tot[:, 0:T * E], ones[:], flat(mask), start=True, stop=True).then_inc(sums_done, 1)

        @block.vector
        def _(dve):
            link = Chain(dve, step)
            nc.vector.tensor_tensor(mask[:], taken[0][:], taken[1][:], ALU.add).then_inc(mask_ready, 1)
            dve.wait_ge(consts_set, ONE + 1)
            dve.wait_ge(sums_done, ONE + 1)
            nc.vector.tensor_copy(flat(tot), b_tot[:, 0:T * E])
            link(nc.vector.tensor_copy(flat(run[0]), b_tot[:, 0:T * E]))
            d, k = 1, 0
            while d < T:
                nc.vector.tensor_copy(run[1 - k][:, 0:d], run[k][:, 0:d])
                link(nc.vector.tensor_tensor(run[1 - k][:, d:T], run[k][:, d:T], run[k][:, 0:T - d], ALU.add))
                d, k = 2 * d, 1 - k
            link(nc.vector.tensor_scalar(count_i[:], run[k][:, T - 1], float(P - 1), None, ALU.add))
            link(nc.vector.tensor_scalar(blocks_i[:], count_i[:], P.bit_length() - 1, None, ALU.logical_shift_right))
            link(nc.vector.tensor_copy(blocks[:], blocks_i[:]))
            link(nc.vector.tensor_copy(ends[0][:], blocks[:]))
            d, m = 1, 0
            while d < E:
                nc.vector.tensor_copy(ends[1 - m][:, 0:d], ends[m][:, 0:d])
                link(nc.vector.tensor_tensor(ends[1 - m][:, d:E], ends[m][:, d:E], ends[m][:, 0:E - d], ALU.add))
                d, m = 2 * d, 1 - m
            link(nc.vector.tensor_tensor(first[:], ends[m][:], blocks[:], ALU.subtract))
            link(nc.vector.tensor_scalar(first[:], first[:], float(P), None, ALU.mult))
            link(nc.vector.tensor_tensor(at[:], run[k][:], tot[:], ALU.subtract))
            link(nc.vector.tensor_tensor(flat(at), flat(at), b_before[:, 0:T * E], ALU.add))
            link(nc.vector.tensor_tensor(at[:], at[:], first[:].unsqueeze(1).broadcast_to([P, T, E]), ALU.add))
            for n in range(2):
                link(nc.vector.tensor_tensor(part[:], at[:], taken[n][:], ALU.mult))
                link(nc.vector.tensor_reduce(slot_f[:], part[:], axis=AX.X, op=ALU.add))
                link(nc.vector.tensor_copy(slot[n][:], slot_f[:]))
            link(nc.vector.tensor_tensor(past[:], ends[m][:].unsqueeze(1).broadcast_to([P, NB, E]),
                                         number[:].unsqueeze(2).broadcast_to([P, NB, E]), ALU.is_le))
            link(nc.vector.tensor_reduce(block_f[:], past[:], axis=AX.X, op=ALU.add))
            link(nc.vector.tensor_scalar(block_f[:], block_f[:], float(E - 1), None, ALU.min))
            link(nc.vector.tensor_copy(block_e[:], block_f[:]))


def shared_experts(nc, g, xnT_all, w, rows, sorted_rows, slot):
    ins = g.ins
    E, SH = ins["L0_ffn_rw1"].shape[0], ins["L0_ffn_sw1"].shape[0]
    H = ins["L0_ffn_rw1"].shape[2]
    EA, KH, C = E + SH, H // P, 512
    NC, TC = N // C, C // P
    SL = 4
    with phase(nc) as (e, semaphore, begin):
        sb = lambda n, shape, dt=F32: e.enter_context(nc.sbuf_tensor(f"sh_{n}", shape, dt))
        sem = lambda n: semaphore(f"sh_{n}")
        w1, w2 = sb("w1", [P, SH, KD, H]), sb("w2", [P, SH, KD, H])
        w3 = sb("w3", [P, SH, KH, D])
        b_rows = sb("b_rows", [SH * KH, 2, P])
        b_cols = sb("b_cols", [P, 2, SH, KH])
        b3 = sb("b3", [EA, D])
        w_tile = [sb(f"w_tile{s}", [P, EA]) for s in range(2)]
        wT = [sb(f"wT{s}", [EA, P]) for s in range(2)]
        silu = [sb(f"silu{k}", [P, C]) for k in range(2)]
        glu = sb("glu", [P, KH, C])
        row = [sb(f"row{s}", [P, D]) for s in range(SL)]
        row_in = [sem(f"row_in{s}") for s in range(SL)]
        row_out = [semaphore(f"sh_row_out{s}", 0) for s in range(SL)]
        b_in, bT_done, bT_ready = sem("b_in"), sem("bT_done"), sem("bT_ready")
        w_in = [sem(f"w_in{s}") for s in range(SH)]
        wt_ready, wT_done, wT_ready, b3_done, b3_added = [
            sem(n) for n in ("wt_ready", "wT_done", "wT_ready", "b3_done", "b3_added")]
        p1_done, p2_done, silu_ready, glu_ready, y_done, y_added = [
            sem(n) for n in ("p1_done", "p2_done", "silu_ready", "glu_ready", "y_done", "y_added")]
        b_p1, b_p2, b_y = g.bank[0:2], g.bank[2:4], g.bank[4:8]
        block = begin()

        @block.sync
        def _(sp):
            for n, b in enumerate((ins["L0_ffn_sb1"], ins["L0_ffn_sb2"])):
                sp.dma_start(b_rows[:, n], b.rearrange("e (m p) -> (e m) p", p=P)).then_inc(b_in, 16)
            sp.dma_start(b3[0:E], ins["L0_ffn_rb3"]).then_inc(b_in, 16)
            sp.dma_start(b3[E:EA], ins["L0_ffn_sb3"]).then_inc(b_in, 16)
            for n in range(SH):
                sp.dma_start(w1[:, n], ins["L0_ffn_sw1"][n].rearrange("(k p) h -> p k h", p=P)).then_inc(w_in[n], 16)
                sp.dma_start(w2[:, n], ins["L0_ffn_sw2"][n].rearrange("(k p) h -> p k h", p=P)).then_inc(w_in[n], 16)
                sp.dma_start(w3[:, n], ins["L0_ffn_sw3"][n].rearrange("(k p) d -> p k d", p=P)).then_inc(w_in[n], 16)
            for t in range(T):
                s = t % SL
                if t >= SL:
                    sp.wait_ge(row_out[s], 32 * (t // SL))
                sp.dma_start(row[s][:], rows[P * t:P * (t + 1), :]).then_inc(row_in[s], 16)
            for s in range(SL):
                sp.wait_ge(row_out[s], 32 * (T // SL))

        @block.gpsimd
        def _(pool):
            for t in range(T):
                s = t % SL
                pool.wait_ge(row_in[s], ONE + 16 * (t // SL + 1))
                for k in range(2):
                    nc.gpsimd.indirect_dma_start(out=sorted_rows, in_=row[s][:], in_offset=None,
                                                 out_offset=bass.IndirectOffsetOnAxis(ap=slot[k][:, t:t + 1], axis=0)
                                                 ).then_inc(row_out[s], 16)

        @block.vector
        def _(dve):
            with dve.Fori(0, T // 2) as i:
                for s in range(2):
                    dve.wait_ge(wT_done, ONE + 2 * i)
                    nc.vector.tensor_copy(w_tile[s][:], w[:, bass.ds(2 * i + s, 1), :].rearrange("p o e -> p (o e)")).then_inc(wt_ready, 1)
                for s in range(2):
                    xt = g.x[:, bass.ds(2 * i + s, 1), :].rearrange("p o d -> p (o d)")
                    dve.wait_ge(b3_done, ONE + 2 * i + s + 1)
                    nc.vector.tensor_tensor(xt, b_y[s][:, 0:D], xt, ALU.add).then_inc(b3_added, 1)
            dve.wait_ge(bT_ready, ONE + 1)
            dve.wait_ge(b3_added, ONE + T)
            for n in range(SH):
                with dve.Fori(0, NC) as c:
                    it = n * NC + c
                    for m in range(KH):
                        dve.wait_ge(silu_ready, ONE + it * KH + m + 1)
                        dve.wait_ge(p2_done, ONE + it * KH + m + 1)
                        dve.wait_ge(y_done, ONE + it * TC)
                        nc.vector.scalar_tensor_tensor(glu[:, m, :], b_p2[m % 2][:], b_cols[:, 1, n, m:m + 1], silu[m % 2][:],
                                                       ALU.add, ALU.mult).then_inc(glu_ready, 1)
                    for q in range(TC):
                        t = c * TC + q
                        xt = g.x[:, bass.ds(t, 1), :].rearrange("p o d -> p (o d)")
                        wt = w[:].rearrange("p t e -> p (t e)")[:, bass.ds(t * EA + E + n, 1)]
                        dve.wait_ge(y_done, ONE + it * TC + q + 1)
                        dve.wait_ge(y_added, ONE + it * TC)
                        nc.vector.scalar_tensor_tensor(xt, b_y[q][:, 0:D], wt, xt, ALU.mult, ALU.add).then_inc(y_added, 1)

        @block.scalar
        def _(act):
            act.wait_ge(bT_done, ONE + 1)
            nc.scalar.activation(b_cols[:].rearrange("p n e m -> p n (e m)"),
                                 b_p1[0][:, 0:2 * SH * KH].rearrange("p (n r) -> p n r", n=2), ACT.Copy).then_inc(bT_ready, 1)
            act.wait_ge(bT_ready, ONE + 1)
            with act.Fori(0, T // 2) as i:
                for s in range(2):
                    act.wait_ge(wT_done, ONE + 2 * i + s + 1)
                    act.wait_ge(b3_done, ONE + 2 * i)
                    nc.scalar.activation(wT[s][:], b_p2[s][0:EA, 0:P], ACT.Copy).then_inc(wT_ready, 1)
            for n in range(SH):
                with act.Fori(0, NC) as c:
                    it = n * NC + c
                    for m in range(KH):
                        act.wait_ge(p1_done, ONE + it * KH + m + 1)
                        if m >= 2:
                            act.wait_ge(glu_ready, ONE + it * KH + m - 1)
                        else:
                            act.wait_ge(glu_ready, ONE + it * KH)
                        nc.scalar.activation(silu[m % 2][:], b_p1[m % 2][:], ACT.Silu, bias=b_cols[:, 0, n, m:m + 1]).then_inc(silu_ready, 1)

        @block.tensor
        def _(pe):
            pe.wait_ge(b_in, ONE + 16 * 4)
            for n in range(2):
                last = nc.tensor.transpose(b_p1[0][:, n * SH * KH:(n + 1) * SH * KH], b_rows[:, n, :], g.ident[0:SH * KH, 0:SH * KH])
            last.then_inc(bT_done, 1)
            with pe.Fori(0, T // 2) as i:
                for s in range(2):
                    pe.wait_ge(wt_ready, ONE + 2 * i + s + 1)
                    pe.wait_ge(wT_ready, ONE + 2 * i)
                    nc.tensor.transpose(b_p2[s][0:EA, 0:P], w_tile[s][:], g.ident[:]).then_inc(wT_done, 1)
                for s in range(2):
                    pe.wait_ge(wT_ready, ONE + 2 * i + s + 1)
                    pe.wait_ge(b3_added, ONE + 2 * i)
                    nc.tensor.matmul(b_y[s][:, 0:D], wT[s][:], b3[:], start=True, stop=True).then_inc(b3_done, 1)
            pe.wait_ge(bT_ready, ONE + 1)
            pe.wait_ge(b3_added, ONE + T)
            for n in range(SH):
                pe.wait_ge(w_in[n], ONE + 48)
                with pe.Fori(0, NC) as c:
                    it = n * NC + c
                    rhs = lambda k: xnT_all[:, k, bass.ds(c * C, C)]
                    for m in range(KH):
                        for w_, bank, done, free in ((w1, b_p1, p1_done, silu_ready), (w2, b_p2, p2_done, glu_ready)):
                            if m >= 2:
                                pe.wait_ge(free, ONE + it * KH + m - 1)
                            else:
                                pe.wait_ge(free, ONE + it * KH)
                            for k in range(KD):
                                last = nc.tensor.matmul(bank[m % 2][:], w_[:, n, k, P * m:P * (m + 1)], rhs(k),
                                                        start=(k == 0), stop=(k == KD - 1))
                            last.then_inc(done, 1)
                    pe.wait_ge(y_added, ONE + it * TC)
                    for m in range(KH):
                        pe.wait_ge(glu_ready, ONE + it * KH + m + 1)
                        for q in range(TC):
                            last = nc.tensor.matmul(b_y[q][:, 0:D], glu[:, m, P * q:P * (q + 1)], w3[:, n, m, :],
                                                    start=(m == 0), stop=(m == KH - 1))
                            if m == KH - 1:
                                last.then_inc(y_done, 1)


def routed_blocks(nc, g, sorted_rows, sorted_out, block_e, block_f):
    ins = g.ins
    E, _, H = ins["L0_ffn_rw1"].shape
    KH, NB = H // P, block_e.shape[1]
    with phase(nc) as (e, semaphore, begin):
        sb = lambda n, shape, dt=F32: e.enter_context(nc.sbuf_tensor(f"rb_{n}", shape, dt))
        sem = lambda n: semaphore(f"rb_{n}")
        w1, w2 = sb("w1", [P, E, KD, H]), sb("w2", [P, E, KD, H])
        w3 = sb("w3", [P, E, KH, D])
        b_all = sb("b_all", [2 * E, 2, H])
        b_hi = sb("b_hi", [2 * E, 2, H], F32R)
        b_parts = sb("b_parts", [2 * E, 2, H], F32R)
        rest = sb("rest", [2 * E, 1])
        row_e, row_at = sb("row_e", [2 * E, P]), sb("row_at", [2 * E, P])
        own = [sb(f"own{s}", [2 * E, P], F32R) for s in range(2)]
        xb = [sb(f"xb{s}", [P, D]) for s in range(2)]
        xT = [sb(f"xT{s}", [P, KD, P]) for s in range(2)]
        silu = sb("silu", [P, H])
        glu, gluT = sb("glu", [P, H]), sb("gluT", [P, KH, P])
        yb = [sb(f"yb{s}", [P, D]) for s in range(2)]
        w_in, b_in, step, rest_set = sem("w_in"), sem("b_in"), sem("step"), sem("rest_set")
        xb_in, kept = [semaphore(f"rb_xb_in{s}", 0) for s in range(2)], [sem(f"kept{s}") for s in range(2)]
        xT_done, xT_ready, own_ready, p1_done, p2_done = [sem(n) for n in (
            "xT_done", "xT_ready", "own_ready", "p1_done", "p2_done")]
        silu_ready, glu_ready, gluT_done, gluT_ready, y_done, y_ready = [sem(n) for n in (
            "silu_ready", "glu_ready", "gluT_done", "gluT_ready", "y_done", "y_ready")]
        b_x, b_p1, b_p2, b_g, b_y = g.bank[0:5]
        block = begin()

        @block.sync
        def _(sp):
            for h in range(2):
                for n, b in enumerate((ins["L0_ffn_rb1"], ins["L0_ffn_rb2"])):
                    sp.dma_start(b_all[E * h:E * (h + 1), n], b).then_inc(b_in, 16)
            dst = sorted_out.rearrange("(j p) d -> j p d", p=P)
            sp.dma_start(w1[:], ins["L0_ffn_rw1"].rearrange("e (k p) h -> p e k h", p=P)).then_inc(w_in, 16)
            sp.dma_start(w2[:], ins["L0_ffn_rw2"].rearrange("e (k p) h -> p e k h", p=P)).then_inc(w_in, 16)
            sp.dma_start(w3[:], ins["L0_ffn_rw3"].rearrange("e (k p) d -> p e k d", p=P)).then_inc(w_in, 16)
            with sp.Fori(0, NB // 2) as i:
                for s in range(2):
                    j = 2 * i + s
                    sp.wait_ge(y_ready, ONE + j + 1)
                    sp.dma_start(dst[bass.ds(j, 1), :, :].rearrange("j p d -> (j p) d"), yb[s][:]).then_inc(kept[s], 16)
            for s in range(2):
                sp.wait_ge(kept[s], ONE + 16 * (NB // 2))

        @block.gpsimd
        def _(pool):
            io = dict(allow_small_or_imprecise_dtypes=True)
            nc.gpsimd.iota(rest[:], pattern=[[0, 1]], base=0, channel_multiplier=1, **io)
            nc.gpsimd.iota(row_at[:], pattern=[[0, P]], base=0, channel_multiplier=1, **io).then_inc(rest_set, 1)
            src = sorted_rows.rearrange("(j p) d -> j p d", p=P)
            for s in range(2):
                pool.dma_start(xb[s][:], src[s]).then_inc(xb_in[s], 16)
            with pool.Fori(0, NB // 2 - 1) as i:
                for s in range(2):
                    j = 2 * i + s
                    pool.wait_ge(xT_done, ONE + j + 1)
                    pool.dma_start(xb[s][:], src[bass.ds(j + 2, 1), :, :].rearrange("j p d -> (j p) d")).then_inc(xb_in[s], 16)

        @block.vector
        def _(dve):
            link = Chain(dve, step)
            dve.wait_ge(rest_set, ONE + 1)
            link(nc.vector.tensor_scalar(rest[:], rest[:], float(E), -1.0, ALU.is_ge, ALU.mult))
            link(nc.vector.tensor_scalar(row_e[:], row_at[:], float(E), float(-E), ALU.is_ge, ALU.mult))
            link(nc.vector.tensor_tensor(row_e[:], row_e[:], row_at[:], ALU.add))
            dve.wait_ge(b_in, ONE + 64)
            link(nc.vector.tensor_copy(b_hi[:], b_all[:]))
            link(nc.vector.scalar_tensor_tensor(b_parts[:], b_hi[:].bitcast(F32), rest[:, 0:1], b_all[:], ALU.mult, ALU.add))

            def rows_in(s, j):
                dve.wait_ge(xT_done, ONE + j + 1)
                dve.wait_ge(p2_done, ONE + j - 1)
                nc.vector.tensor_copy(xT[s][:], b_x[:, 0:D].rearrange("p (k q) -> p k q", k=KD)).then_inc(xT_ready, 1)
                nc.vector.tensor_scalar(own[s][:], row_e[:], block_f[0:2 * E, bass.ds(j, 1)], None, ALU.is_equal).then_inc(own_ready, 1)

            def gated(j):
                dve.wait_ge(silu_ready, ONE + j + 1)
                dve.wait_ge(p2_done, ONE + j + 1)
                dve.wait_ge(gluT_done, ONE + j)
                nc.vector.tensor_tensor(glu[:], b_p2[:], silu[:], ALU.mult).then_inc(glu_ready, 1)

            def gated_T(j):
                dve.wait_ge(gluT_done, ONE + j + 1)
                dve.wait_ge(y_done, ONE + j)
                nc.vector.tensor_copy(gluT[:], b_g[:].rearrange("p (m q) -> p m q", m=KH)).then_inc(gluT_ready, 1)

            def out_rows(s, j, used):
                dve.wait_ge(y_done, ONE + j + 1)
                dve.wait_ge(kept[s], ONE + 16 * used)
                nc.vector.tensor_copy(yb[s][:], b_y[:, 0:D]).then_inc(y_ready, 1)

            rows_in(0, 0)
            rows_in(1, 1)
            gated(0)
            with dve.Fori(0, NB // 2 - 1) as i:
                for s in range(2):
                    j = 2 * i + s + 1
                    gated_T(j - 1)
                    rows_in(s, j + 1)
                    gated(j)
                    out_rows(s, j - 1, i)
            gated_T(NB - 2)
            gated(NB - 1)
            out_rows(0, NB - 2, NB // 2 - 1)
            gated_T(NB - 1)
            out_rows(1, NB - 1, NB // 2 - 1)

        @block.scalar
        def _(act):
            with act.Fori(0, NB) as j:
                act.wait_ge(p1_done, ONE + j + 1)
                act.wait_ge(glu_ready, ONE + j)
                nc.scalar.activation(silu[:], b_p1[:], ACT.Silu).then_inc(silu_ready, 1)

        @block.tensor
        def _(pe):
            pe.wait_ge(w_in, ONE + 48)

            def expert(j):
                return pe.value_load(block_e[0:1, bass.ds(j, 1)], min_val=0, max_val=E - 1)

            def rows_T(s, j, round_):
                pe.wait_ge(xb_in[s], 16 * (round_ + 1))
                pe.wait_ge(xT_ready, ONE + j)
                for k in range(KD):
                    last = nc.tensor.transpose(b_x[:, P * k:P * (k + 1)], xb[s][:, P * k:P * (k + 1)], g.ident[:])
                last.then_inc(xT_done, 1)

            def hidden(s, n, w, at, bank, done):
                flat = w[:].rearrange("p e k h -> p (e k) h")
                nc.tensor.matmul(bank[:], own[s][:], b_parts[:, at, :], start=True, stop=False)
                for k in range(KD):
                    last = nc.tensor.matmul(bank[:], xT[s][:, k, :], flat[:, bass.ds(n * KD + k, 1), :].rearrange("p o h -> p (o h)"),
                                            start=False, stop=(k == KD - 1))
                last.then_inc(done, 1)

            def first(s, j, n):
                pe.wait_ge(own_ready, ONE + j + 1)
                pe.wait_ge(silu_ready, ONE + j)
                hidden(s, n, w1, 0, b_p1, p1_done)

            def second(s, j, n):
                pe.wait_ge(glu_ready, ONE + j)
                hidden(s, n, w2, 1, b_p2, p2_done)

            def gated_T(j):
                pe.wait_ge(glu_ready, ONE + j + 1)
                pe.wait_ge(gluT_ready, ONE + j)
                for m in range(KH):
                    last = nc.tensor.transpose(b_g[:, P * m:P * (m + 1)], glu[:, P * m:P * (m + 1)], g.ident[:])
                last.then_inc(gluT_done, 1)

            def down(j):
                n = expert(j)
                pe.wait_ge(gluT_ready, ONE + j + 1)
                pe.wait_ge(y_ready, ONE + j)
                flat = w3[:].rearrange("p e m d -> p (e m) d")
                for m in range(KH):
                    last = nc.tensor.matmul(b_y[:, 0:D], gluT[:, m, :], flat[:, bass.ds(n * KH + m, 1), :].rearrange("p o d -> p (o d)"),
                                            start=(m == 0), stop=(m == KH - 1))
                last.then_inc(y_done, 1)

            rows_T(0, 0, 0)
            n = expert(0)
            first(0, 0, n)
            second(0, 0, n)
            rows_T(1, 1, 0)
            with pe.Fori(0, NB // 2 - 1) as i:
                for s in range(2):
                    j = 2 * i + s + 1
                    n = expert(j)
                    first(1 - s, j, n)
                    gated_T(j - 1)
                    second(1 - s, j, n)
                    rows_T(s, j + 1, i + 1)
                    down(j - 1)
            n = expert(NB - 1)
            first(1, NB - 1, n)
            gated_T(NB - 2)
            second(1, NB - 1, n)
            down(NB - 2)
            gated_T(NB - 1)
            down(NB - 1)


def routed_sum(nc, g, sorted_out, slot, weight):
    SL = 8
    with phase(nc) as (e, semaphore, begin):
        sem = lambda n: semaphore(f"rs_{n}")
        got = [e.enter_context(nc.sbuf_tensor(f"rs_got{s}", [P, D], F32)) for s in range(SL)]
        got_in = [semaphore(f"rs_got_in{s}", 0) for s in range(SL)]
        x_ready, stats_ready = sem("x_ready"), sem("stats_ready")
        block = begin()

        @block.gpsimd
        def _(pool):
            for n in range(2 * T):
                t, k = n // 2, n % 2
                if n >= SL:
                    pool.wait_ge(x_ready, ONE + n - SL + 1)
                nc.gpsimd.indirect_dma_start(out=got[n % SL][:], out_offset=None, in_=sorted_out,
                                             in_offset=bass.IndirectOffsetOnAxis(ap=slot[k][:, t:t + 1], axis=0)
                                             ).then_inc(got_in[n % SL], 16)

        @block.vector
        def _(dve):
            with dve.Fori(0, 2 * T // SL) as i:
                for s in range(SL):
                    t, k = i * (SL // 2) + s // 2, s % 2
                    xt = g.x[:, bass.ds(t, 1), :].rearrange("p o d -> p (o d)")
                    dve.wait_ge(got_in[s], 16 * i + 16)
                    dve.wait_ge(x_ready, ONE + SL * i + s)
                    nc.vector.scalar_tensor_tensor(xt, got[s][:], weight[k][:, bass.ds(t, 1)], xt,
                                                   ALU.mult, ALU.add).then_inc(x_ready, 1)
                    if k:
                        dve.wait_ge(x_ready, ONE + SL * i + s + 1)
                        nc.vector.bn_stats(g.stats[:, bass.ds(t, 1), :], g.x[:, bass.ds(t, 1), :]).then_inc(stats_ready, 1)


def mixture0(nc, g, sorted_rows):
    ins = g.ins
    E, SH = ins["L0_ffn_rw1"].shape[0], ins["L0_ffn_sw1"].shape[0]
    NB = sorted_rows.shape[0] // P
    rows = nc.dram_tensor("normalised_rows", [N, D], F32, kind="Internal").ap()
    sorted_out = nc.dram_tensor("sorted_out", [NB * P, D], F32, kind="Internal").ap()
    with ExitStack() as e:
        sb = lambda n, shape, dt=F32: e.enter_context(nc.sbuf_tensor(f"m0_{n}", shape, dt))
        slot, weight = [sb(f"slot{k}", [P, T], U32) for k in range(2)], [sb(f"weight{k}", [P, T]) for k in range(2)]
        block_e, block_f = sb("block_e", [P, NB], I32), sb("block_f", [P, NB])
        with ExitStack() as e:
            xnT_all = sb("xnT", [P, KD, N])
            w, logits = sb("w", [P, T, E + SH]), sb("logits", [P, T, E])
            taken = [sb(f"taken{k}", [P, T, E]) for k in range(2)]
            normalised_pairs(nc, g, "np0", ins["L0_ffn_gate_w"], ins["L0_ffn_gate_b"], xnT_all, logits, rows_out=rows)
            top2_weights(nc, g, logits, w, SH, taken, weight)
            block_slots(nc, g, taken, slot, block_e, block_f)
            shared_experts(nc, g, xnT_all, w, rows, sorted_rows, slot)
        routed_blocks(nc, g, sorted_rows, sorted_out, block_e, block_f)
        routed_sum(nc, g, sorted_out, slot, weight)


GT = S * D // NH // D
NG = 2 * P // GT
PC = D // DH
L = GT * PC
A = P // GT
QT = L // P
BL = 32
ST = 3 * BL
NP = T // 2


def project_groups(nc, g, parts, values, x_kept, qs, ks, nmax, tile_rows):
    ins = g.ins
    with phase(nc) as (e, semaphore, begin):
        sb = lambda n, shape, dt=F32: e.enter_context(nc.sbuf_tensor(f"pg_{n}", shape, dt))
        sem = lambda n: semaphore(f"pg_{n}")
        wq, wk, wv = [sb(n, [P, KD, D]) for n in ("wq", "wk", "wv")]
        b_qk = sb("b_qk", [P, 2, KD])
        bv = sb("bv", [P, QT, DH])
        bo = sb("bo", [P, D])
        xn = [[sb(f"xn{s}{h}", [P, D]) for h in range(2)] for s in range(2)]
        xnT = [sb(f"xnT{s}", [P, KD, 2 * P]) for s in range(2)]
        hi = [[sb(f"hi{s}{n}", [P, KD, 2 * P], F32R) for n in range(2)] for s in range(2)]
        lo = [[sb(f"lo{s}{n}", [P, KD, 2 * P], F32R) for n in range(2)] for s in range(2)]
        v = [sb(f"v{s}", [P, NG, QT, BL]) for s in range(2)]
        w_in, b_in, v_zero, v_one, stack_zero, rows_set = [sem(n) for n in (
            "w_in", "b_in", "v_zero", "v_one", "stack_zero", "rows_set")]
        xn_ready, xnT_done, xnT_ready, qk_done, hi_ready, lo_ready, v_done, v_ready, xn_bo_ready = [sem(n) for n in (
            "xn_ready", "xnT_done", "xnT_ready", "qk_done", "hi_ready", "lo_ready", "v_done", "v_ready", "xn_bo_ready")]
        x_out, parts_out, v_out = [[sem(f"{n}{s}") for s in range(2)] for n in ("x_out", "parts_out", "v_out")]
        b_t, b_q, b_k, b_v = [g.bank[2 * n:2 * n + 2] for n in range(4)]
        block = begin()
        W_IN, B_IN, PARTS = 16 * 3, 16 * (2 * KD + A + 1), 16 * 4 * KD

        @block.sync
        def _(sp):
            for w, src in ((wq, ins["L1_attn_wq"]), (wk, ins["L1_attn_wk"]), (wv, ins["L1_attn_wv"])):
                sp.dma_start(w[:], src.rearrange("(k p) n -> p k n", p=P)).then_inc(w_in, 16)
            for n, src in enumerate((ins["L1_attn_bq"], ins["L1_attn_bk"])):
                for k in range(KD):
                    sp.dma_start(b_qk[:, n, k:k + 1], src[P * k:P * (k + 1)].rearrange("(p o) -> p o", o=1)).then_inc(b_in, 16)
            bv_parts = ins["L1_attn_bv"].rearrange("(o q a d) -> a o q d", o=1, a=A, d=DH)
            for a in range(A):
                sp.dma_start(bv[a * GT:(a + 1) * GT], bv_parts[a].broadcast_to([GT, QT, DH])).then_inc(b_in, 16)
            sp.dma_start(bo[:], ins["L1_attn_bo"].rearrange("(o n) -> o n", o=1).broadcast_to([P, D])).then_inc(b_in, 16)
            x_dst = x_kept.rearrange("(i s p) d -> i p s d", s=2, p=P)
            with sp.Fori(0, NP // 2) as r:
                for s in range(2):
                    i = 2 * r + s
                    sp.wait_ge(xn_bo_ready, ONE + 4 * r)
                    sp.dma_start(x_dst[bass.ds(i, 1)].rearrange("i p s d -> (i p) s d"), g.x[:, bass.ds(2 * i, 2), :]).then_inc(x_out[s], 16)
                for s in range(2):
                    i = 2 * r + s
                    for n in range(2):
                        for part, (tile, ready) in enumerate(((hi, hi_ready), (lo, lo_ready))):
                            sp.wait_ge(ready, ONE + 4 * i + 2 * n + 2)
                            dst = parts[n][part].rearrange("i d n (m c) t -> i m c d n t", m=KD)
                            for m in range(KD):
                                sp.dma_start(dst[bass.ds(i, 1), m].rearrange("i c d n t -> (i c) d n t"),
                                             tile[s][n][:, m].bitcast(F32).rearrange("p (n t) -> p n t", n=NG)
                                             ).then_inc(parts_out[s], 16)
                    sp.wait_ge(v_ready, ONE + i + 1)
                    sp.dma_start(values[bass.ds(i, 1)].rearrange("i p f -> (i p) f"),
                                 v[s][:].rearrange("p n q r -> p (n q r)")).then_inc(v_out[s], 16)
            for s in range(2):
                sp.wait_ge(x_out[s], ONE + 16 * (NP // 2))
                sp.wait_ge(parts_out[s], ONE + PARTS * (NP // 2))
                sp.wait_ge(v_out[s], ONE + 16 * (NP // 2))

        @block.gpsimd
        def _(pool):
            for s in range(2):
                nc.gpsimd.memset(v[s][:], 0.0).then_inc(v_zero, 1)
            pool.wait_ge(v_zero, ONE + 2)
            for s in range(2):
                nc.gpsimd.memset(v[s][:, :, :, DH:DH + 1], 1.0).then_inc(v_one, 1)
            nc.gpsimd.memset(nmax[:], 0.0)
            nc.gpsimd.memset(tile_rows[:], 0.0).then_inc(rows_set, 1)
            pool.wait_ge(rows_set, ONE + 1)
            pool.wait_ge(v_one, ONE + 2)
            nc.gpsimd.affine_select(out=tile_rows[ST:P], in_=tile_rows[ST:P], compare_op=ALU.not_equal, fill=1.0, base=0,
                                    pattern=[[-1, QT], [0, P]], channel_multiplier=1).then_inc(rows_set, 1)
            pool.wait_ge(rows_set, ONE + 2)
            pool.wait_ge(b_in, ONE + B_IN)
            with pool.Fori(0, NP // 2) as r:
                for s in range(2):
                    i = 2 * r + s
                    pool.wait_ge(x_out[s], ONE + 16 * r + 16)
                    for h in range(2):
                        pool.wait_ge(xn_ready, ONE + 2 * i + h + 1)
                        nc.gpsimd.tensor_tensor(g.x[:, bass.ds(2 * i + h, 1), :].rearrange("p o d -> p (o d)"),
                                                xn[s][h][:], bo[:], ALU.add).then_inc(xn_bo_ready, 1)
            for a in range(3):
                nc.gpsimd.memset(qs[a][0:ST].bitcast(F32), 0.0)
                nc.gpsimd.memset(ks[a][0:ST].bitcast(F32), 0.0).then_inc(stack_zero, 1)

        @block.vector
        def _(dve):
            for a in range(3):
                nc.vector.memset(ks[a][ST:P].bitcast(F32), 1.0)
            dve.wait_ge(b_in, ONE + B_IN)
            dve.wait_ge(v_one, ONE + 2)
            with dve.Fori(0, NP // 2) as r:
                for s in range(2):
                    i = 2 * r + s
                    for h in range(2):
                        t = 2 * i + h
                        dve.wait_ge(xnT_done, ONE + 2 * r)
                        dve.wait_ge(xn_bo_ready, ONE + 4 * r)
                        nc.vector.tensor_scalar(xn[s][h][:], g.x[:, bass.ds(t, 1), :].rearrange("p o d -> p (o d)"),
                                                g.mean[:, bass.ds(t, 1)], g.rstd[:, bass.ds(t, 1)],
                                                ALU.subtract, ALU.mult).then_inc(xn_ready, 1)
                for s in range(2):
                    i = 2 * r + s
                    for n in range(2):
                        for m in range(KD):
                            dve.wait_ge(hi_ready, ONE + 4 * i + 2 * n + 2)
                            dve.wait_ge(parts_out[s], ONE + PARTS * r)
                            nc.vector.scalar_tensor_tensor(lo[s][n][:, m], (b_q, b_k)[n][s][:, 2 * P * m:2 * P * (m + 1)],
                                                           b_qk[:, n, m:m + 1], hi[s][n][:, m].bitcast(F32),
                                                           ALU.add, ALU.subtract).then_inc(lo_ready, 1)
                    dve.wait_ge(v_done, ONE + i + 1)
                    dve.wait_ge(v_out[s], ONE + 16 * r)
                    nc.vector.tensor_tensor(v[s][:, :, :, 0:DH], b_v[s][:].rearrange("p (n q d) -> p n q d", n=NG, d=DH),
                                            bv[:].unsqueeze(1).broadcast_to([P, NG, QT, DH]), ALU.add).then_inc(v_ready, 1)

        @block.scalar
        def _(act):
            act.wait_ge(b_in, ONE + B_IN)
            with act.Fori(0, NP // 2) as r:
                for s in range(2):
                    i = 2 * r + s
                    act.wait_ge(xnT_done, ONE + i + 1)
                    act.wait_ge(v_done, ONE + 2 * r)
                    nc.scalar.activation(xnT[s][:].rearrange("p k (h q) -> p h k q", h=2),
                                         b_t[s][:].rearrange("p (h k q) -> p h k q", h=2, k=KD), ACT.Identity).then_inc(xnT_ready, 1)
                for s in range(2):
                    i = 2 * r + s
                    for n in range(2):
                        act.wait_ge(qk_done, ONE + 2 * i + n + 1)
                        act.wait_ge(parts_out[s], ONE + PARTS * r)
                        for m in range(KD):
                            nc.scalar.activation(hi[s][n][:, m], (b_q, b_k)[n][s][:, 2 * P * m:2 * P * (m + 1)], ACT.Identity,
                                                 bias=b_qk[:, n, m:m + 1]).then_inc(hi_ready, 1)

        @block.tensor
        def _(pe):
            pe.wait_ge(w_in, ONE + W_IN)
            with pe.Fori(0, NP // 2) as r:
                for s in range(2):
                    i = 2 * r + s
                    pe.wait_ge(xn_ready, ONE + 2 * i + 2)
                    pe.wait_ge(xnT_ready, ONE + 2 * r)
                    for h in range(2):
                        for k in range(KD):
                            last = nc.tensor.transpose(b_t[s][:, P * (KD * h + k):P * (KD * h + k + 1)],
                                                       xn[s][h][:, P * k:P * (k + 1)], g.ident[:])
                    last.then_inc(xnT_done, 1)
                for s in range(2):
                    i = 2 * r + s
                    pe.wait_ge(xnT_ready, ONE + i + 1)
                    pe.wait_ge(lo_ready, ONE + 8 * r)
                    for n, w in enumerate((wq, wk)):
                        for m in range(KD):
                            for k in range(KD):
                                last = nc.tensor.matmul((b_q, b_k)[n][s][:, 2 * P * m:2 * P * (m + 1)], w[:, k, P * m:P * (m + 1)],
                                                        xnT[s][:, k, :], start=(k == 0), stop=(k == KD - 1))
                        last.then_inc(qk_done, 1)
                    pe.wait_ge(v_ready, ONE + 2 * r)
                    for n in range(NG):
                        for a in range(A):
                            for k in range(KD):
                                cols = wv[:, k, :].rearrange("p (q a d) -> p a q d", a=A, d=DH)[:, a]
                                last = nc.tensor.matmul(b_v[s][GT * a:GT * (a + 1), P * n:P * (n + 1)],
                                                        xnT[s][:, k, GT * n:GT * (n + 1)], cols,
                                                        start=(k == 0), stop=(k == KD - 1))
                    last.then_inc(v_done, 1)


def group_attention(nc, g, parts, values, qs, ks, nmax, tile_rows):
    ins = g.ins
    HALF = 512
    LAG = 2
    U = NG * QT
    HU = 2 * U
    SETS = 3
    NS = HU // NG
    SLOTS = 3

    def step_uses(c):
        uses = []
        for u in range(U):
            if c < NP:
                uses.append(("scores", u, u))
            if u == 0 and 1 <= c <= NP:
                uses.append(("maxima", NG - 1, u))
            if u % QT == 1 and u > QT and c < NP:
                uses.append(("maxima", u // QT - 1, u))
            if c >= 2:
                for at, use in ((6, ("context", 0)), (10, ("contextT", 0)), (14, ("project", 0)), (15, ("project", 1))):
                    if u == at:
                        uses.append((*use, u))
        return uses

    FULL = len(step_uses(2))
    FIRST = [0, len(step_uses(0)), len(step_uses(0)) + len(step_uses(1))]

    def uses_before(c):
        if c <= 2:
            return FIRST[c]
        return FIRST[2] + sum(len(step_uses(n)) for n in range(2, c))

    def use_at(c, kind, arg):
        return uses_before(c) + [(k, a) for k, a, _ in step_uses(c)].index((kind, arg))

    with phase(nc) as (e, semaphore, begin):
        sb = lambda n, shape, dt=F32: e.enter_context(nc.sbuf_tensor(f"ga_{n}", shape, dt))
        sem = lambda n: semaphore(f"ga_{n}")
        wo = sb("wo", [P, A, D])
        v = [sb(f"v{a}", [P, NG, QT, BL]) for a in range(SLOTS)]
        probT = [[sb(f"probT{k}{n}", [P, HALF]) for n in range(NG)] for k in range(SETS)]
        o = sb("o", [P, L])
        rsum = sb("rsum", [P, QT, NG])
        ctxn = sb("ctxn", [P, NG, QT, DH])
        ctxT = sb("ctxT", [P, 2, A, P])
        w_in = sem("w_in")
        qk_in, v_in = [sem(f"qk_in{a}") for a in range(SLOTS)], [sem(f"v_in{a}") for a in range(SLOTS)]
        use_done, use_read, sT_done, exp_ready, pv_done, o_ready = [sem(n) for n in (
            "use_done", "use_read", "sT_done", "exp_ready", "pv_done", "o_ready")]
        rsum_ready, r_ready, stats_ready = sem("rsum_ready"), sem("r_ready"), sem("stats_ready")
        b_s, b_t, b_o = g.bank2[0:2], g.bank[4:6], g.bank2[3]
        block = begin()

        def steps(eng, step):
            for c in range(2):
                step(0, c)
            with eng.Fori(0, (NP - 2) // SLOTS) as r:
                for c in range(2, 2 + SLOTS):
                    step(r, c)
            for c in range(2 + (NP - 2) // SLOTS * SLOTS, NP + 2):
                step(0, c)

        def back_units(c):
            return [(U - LAG + u, c - 2) if u < LAG else (u - LAG, c - 1) for u in range(U)]

        @block.sync
        def _(sp):
            wo_rows = ins["L1_attn_wo"].rearrange("(q a d) n -> q d a n", a=A, d=DH)
            for q in range(QT):
                sp.dma_start(wo[q * DH:(q + 1) * DH], wo_rows[q]).then_inc(w_in, 16)

            def load(r, c):
                i, a = SLOTS * r + c, c % SLOTS
                if c >= SLOTS:
                    sp.wait_ge(sT_done, ONE + HU * (i - SLOTS + 1))
                    sp.wait_ge(pv_done, ONE + NS * (i - SLOTS + 1))
                for tile, n, blocks in ((qs, 0, (0, 0, 1)), (ks, 1, (0, 1, 0))):
                    for b, part in enumerate(blocks):
                        sp.dma_start(tile[a][BL * b:BL * b + DH].bitcast(F32).rearrange("p n l -> p (n l)"),
                                     parts[n][part][bass.ds(i, 1)].rearrange("i d n c t -> (i d) (n c t)")).then_inc(qk_in[a], 16)
                sp.dma_start(v[a][:].rearrange("p n q r -> p (n q r)"),
                             values[bass.ds(i, 1)].rearrange("i p f -> (i p) f")).then_inc(v_in[a], 16)

            for c in range(SLOTS):
                load(0, c)
            with sp.Fori(0, NP // SLOTS - 1) as r:
                for c in range(SLOTS, 2 * SLOTS):
                    load(r, c)
            for c in range(NP // SLOTS * SLOTS, NP):
                load(0, c)

        @block.vector
        def _(dve):
            def step(r, c):
                i = SLOTS * r + c
                before = FULL * SLOTS * r + uses_before(c)
                for n, (kind, arg, _) in enumerate(step_uses(c)):
                    use = before + n
                    slot = b_s[(uses_before(c) + n) % 2]
                    dve.wait_ge(use_done, ONE + use + 1)
                    if kind == "scores":
                        gr, q = arg // QT, arg % QT
                        nc.vector.tensor_reduce(nmax[:, gr, ST + q:ST + q + 1], slot[:], axis=AX.X, op=ALU.max,
                                                negate=True).then_inc(use_read, 1)
                    elif kind == "maxima":
                        a = (c - 1 if arg == NG - 1 else c) % SLOTS
                        nc.vector.tensor_tensor(qs[a][ST:P, arg].rearrange("p (t q) -> p t q", t=QT),
                                                slot[ST:P, 0:P].unsqueeze(1).broadcast_to([P - ST, QT, P]),
                                                tile_rows[ST:P], ALU.mult).then_inc(use_read, 1)
                    elif kind == "context":
                        src = slot[:].rearrange("p (q n r) -> p q n r", n=NG, r=BL)
                        nc.vector.reciprocal(rsum[:], src[:, :, :, DH]).then_inc(rsum_ready, 1)
                        dve.wait_ge(rsum_ready, ONE + i - 1)
                        nc.vector.tensor_tensor(ctxn[:].rearrange("p n q d -> p q n d"), src[:, :, :, 0:DH],
                                                rsum[:].unsqueeze(3).broadcast_to([P, QT, NG, DH]), ALU.mult).then_inc(use_read, 1)
                    elif kind == "contextT":
                        for s in range(2):
                            last = nc.vector.tensor_copy(ctxT[:, s].rearrange("p a (n t) -> p n a t", t=GT),
                                                         slot[:, 2 * P * s:2 * P * (s + 1)].rearrange("p (n a t) -> p n a t", a=A, t=GT))
                        last.then_inc(use_read, 1)
                    else:
                        t = 2 * (i - 2) + arg
                        xt = g.x[:, bass.ds(t, 1), :].rearrange("p o d -> p (o d)")
                        nc.vector.tensor_tensor(xt, slot[:, 0:D], xt, ALU.add).then_inc(use_read, 1)
                        dve.wait_ge(use_read, ONE + use + 1)
                        nc.vector.bn_stats(g.stats[:, bass.ds(t, 1), :], xt).then_inc(stats_ready, 1)

            steps(dve, step)

        @block.scalar
        def _(act):
            def step(r, c):
                for unit, pc in back_units(c):
                    pair = SLOTS * r + pc
                    if 0 <= pc < NP:
                        for h in (2 * unit, 2 * unit + 1):
                            k, n = h // NG, h % NG
                            act.wait_ge(sT_done, ONE + HU * pair + h + 1)
                            if n == 0 and NS * pc + k >= SETS:
                                act.wait_ge(pv_done, ONE + NS * pair + k - SETS + 1)
                            nc.scalar.activation(probT[(NS * pc + k) % SETS][n][:], b_t[h % 2][:], ACT.Exp,
                                                 scale=SCALE).then_inc(exp_ready, 1)
                    if unit == 0 and c >= 2:
                        i = SLOTS * r + c - 2
                        act.wait_ge(pv_done, ONE + NS * i + NS)
                        if c > 2:
                            act.wait_ge(use_read, ONE + FULL * SLOTS * r + use_at(c - 1, "context", 0) + 1)
                        nc.scalar.activation(o[:], b_o[:], ACT.Copy).then_inc(o_ready, 1)

            steps(act, step)

        @block.tensor
        def _(pe):
            def use(r, c, n, kind, arg):
                at = uses_before(c) + n
                before = FULL * SLOTS * r
                slot = b_s[at % 2]
                if at >= 2:
                    pe.wait_ge(use_read, ONE + before + at - 1)
                if kind == "scores":
                    a, gr, q = c % SLOTS, arg // QT, arg % QT
                    if arg == 0:
                        pe.wait_ge(qk_in[a], ONE + 16 * 6 * (r + c // SLOTS + 1))
                    for hf in range(L // HALF):
                        last = nc.tensor.matmul(slot[:, HALF * hf:HALF * (hf + 1)], qs[a][0:ST, gr, P * q:P * (q + 1)],
                                                ks[a][0:ST, gr, HALF * hf:HALF * (hf + 1)], start=True, stop=True)
                elif kind == "maxima":
                    of = c - 1 if arg == NG - 1 else c
                    pe.wait_ge(use_read, ONE + before + use_at(of, "scores", QT * (arg + 1) - 1) + 1)
                    last = nc.tensor.transpose(slot[:, 0:P], nmax[:, arg, :], g.ident[:])
                elif kind == "context":
                    pe.wait_ge(o_ready, ONE + SLOTS * r + c - 1)
                    for q in range(QT):
                        last = nc.tensor.transpose(slot[:, P * q:P * (q + 1)], o[:, P * q:P * (q + 1)], g.ident[:])
                elif kind == "contextT":
                    pe.wait_ge(use_read, ONE + before + use_at(c, "context", 0) + 1)
                    for gr in range(NG):
                        last = nc.tensor.transpose(slot[:, P * gr:P * (gr + 1)], ctxn[:, gr].rearrange("p q d -> p (q d)"), g.ident[:])
                else:
                    pe.wait_ge(use_read, ONE + before + use_at(c, "contextT", 0) + 1)
                    for a in range(A):
                        last = nc.tensor.matmul(slot[:, 0:D], ctxT[:, arg, a, :], wo[:, a, :],
                                                start=(a == 0), stop=(a == A - 1))
                last.then_inc(use_done, 1)

            def scores_T(r, c, unit):
                pair, a = SLOTS * r + c, c % SLOTS
                for h in (2 * unit, 2 * unit + 1):
                    k, hf, n = h // NG // 2, h // NG % 2, h % NG
                    if h < NG:
                        step_of = c + 1 if n == NG - 1 else c
                        pe.wait_ge(use_read, ONE + FULL * SLOTS * r + use_at(step_of, "maxima", n) + 1)
                    if c > 0 or h >= 2:
                        pe.wait_ge(exp_ready, ONE + HU * pair + h - 1)
                    nc.tensor.matmul(b_t[h % 2][:], ks[a][:, n, P * k:P * (k + 1)], qs[a][:, n, HALF * hf:HALF * (hf + 1)],
                                     start=True, stop=True).then_inc(sT_done, 1)

            def weigh(r, c, k):
                pair, a = SLOTS * r + c, c % SLOTS
                kt, hf = k // 2, k % 2
                pe.wait_ge(exp_ready, ONE + HU * pair + NG * (k + 1))
                if k == 0:
                    pe.wait_ge(v_in[a], ONE + 16 * (r + c // SLOTS + 1))
                    if c > 0:
                        pe.wait_ge(o_ready, ONE + pair)
                for n in range(NG):
                    last = nc.tensor.matmul(b_o[BL * n:BL * (n + 1), HALF * hf:HALF * (hf + 1)], v[a][:, n, kt, :],
                                            probT[(NS * c + k) % SETS][n][:], start=(kt == 0), stop=(kt == QT - 1))
                last.then_inc(pv_done, 1)

            def step(r, c):
                uses = list(enumerate(step_uses(c)))
                for u, (unit, pc) in enumerate(back_units(c)):
                    for n, (kind, arg, at) in uses:
                        if at == u:
                            use(r, c, n, kind, arg)
                    if 0 <= pc < NP:
                        scores_T(r, pc, unit)
                    if unit == 0 and c >= 2:
                        weigh(r, c - 2, NS - 1)
                    elif unit and unit % 2 == 0 and 0 <= pc < NP:
                        weigh(r, pc, unit // 2 - 1)

            pe.wait_ge(w_in, ONE + 16 * QT)
            steps(pe, step)


def norm_residual(nc, g, x_kept):
    C = 4
    with phase(nc) as (e, semaphore, begin):
        sb = lambda n, shape, dt=F32: e.enter_context(nc.sbuf_tensor(f"nr_{n}", shape, dt))
        sem = lambda n: semaphore(f"nr_{n}")
        gamma, beta = sb("gamma", [P, D]), sb("beta", [P, D])
        rn = [sb(f"rn{s}", [P, C, D]) for s in range(2)]
        xb = [sb(f"xb{s}", [P, C, D]) for s in range(2)]
        w_in, xb_ready, rn_ready, scaled, x_ready, stats_ready = [sem(n) for n in (
            "w_in", "xb_ready", "rn_ready", "scaled", "x_ready", "stats_ready")]
        xb_in = [sem(f"xb_in{s}") for s in range(2)]
        block = begin()
        over = lambda a: a[:].unsqueeze(1).broadcast_to([P, C, D])

        @block.sync
        def _(sp):
            for w, src in ((gamma, g.ins["L1_attn_gamma"]), (beta, g.ins["L1_attn_beta"])):
                sp.dma_start(w[:], src.rearrange("(o n) -> o n", o=1).broadcast_to([P, D])).then_inc(w_in, 16)
            src = x_kept.rearrange("(i c p) d -> i p c d", c=C, p=P)
            with sp.Fori(0, T // C // 2) as i:
                for s in range(2):
                    sp.wait_ge(x_ready, ONE + 2 * i)
                    sp.dma_start(xb[s][:], src[bass.ds(2 * i + s, 1)].rearrange("i p c d -> (i p) c d")).then_inc(xb_in[s], 16)

        @block.gpsimd
        def _(pool):
            pool.wait_ge(w_in, ONE + 32)
            with pool.Fori(0, T // C // 2) as i:
                for s in range(2):
                    pool.wait_ge(xb_in[s], ONE + 16 * i + 16)
                    nc.gpsimd.tensor_tensor(xb[s][:], xb[s][:], over(beta), ALU.add).then_inc(xb_ready, 1)

        @block.vector
        def _(dve):
            dve.wait_ge(w_in, ONE + 32)
            with dve.Fori(0, T // C // 2) as i:
                for s in range(2):
                    n = 2 * i + s
                    dve.wait_ge(x_ready, ONE + 2 * i)
                    for c in range(C):
                        t = C * n + c
                        last = nc.vector.tensor_scalar(rn[s][:, c, :], g.x[:, bass.ds(t, 1), :].rearrange("p o d -> p (o d)"),
                                                       g.mean[:, bass.ds(t, 1)], g.rstd[:, bass.ds(t, 1)],
                                                       ALU.subtract, ALU.mult)
                    last.then_inc(rn_ready, 1)
                    dve.wait_ge(rn_ready, ONE + n + 1)
                    nc.vector.tensor_tensor(rn[s][:], rn[s][:], over(gamma), ALU.mult).then_inc(scaled, 1)
                    dve.wait_ge(scaled, ONE + n + 1)
                    dve.wait_ge(xb_ready, ONE + n + 1)
                    nc.vector.tensor_tensor(g.x[:, bass.ds(C * n, C), :], rn[s][:], xb[s][:], ALU.add).then_inc(x_ready, 1)
            dve.wait_ge(x_ready, ONE + T // C)
            with dve.Fori(0, T) as t:
                nc.vector.bn_stats(g.stats[:, bass.ds(t, 1), :], g.x[:, bass.ds(t, 1), :]).then_inc(stats_ready, 1)


def attention1(nc, g):
    dram = lambda n, shape: nc.dram_tensor(n, shape, F32, kind="Internal").ap()
    parts = [[dram(f"{n}_{part}", [NP, DH, NG, PC, GT]) for part in ("rounded", "rest")] for n in ("queries", "keys")]
    values, x_kept = dram("values", [NP, P, NG * QT * BL]), dram("x_kept", [N, D])
    with ExitStack() as e:
        sb = lambda n, shape, dt=F32: e.enter_context(nc.sbuf_tensor(f"a1_{n}", shape, dt))
        qs, ks = [[sb(f"{n}{a}", [P, NG, L], F32R) for a in range(3)] for n in ("qs", "ks")]
        nmax = sb("nmax", [P, NG, P])
        tile_rows = sb("tile_rows", [P, QT, P])
        project_groups(nc, g, parts, values, x_kept, qs, ks, nmax, tile_rows)
        group_attention(nc, g, parts, values, qs, ks, nmax, tile_rows)
    finish_stats(nc, g, "ln3")
    norm_residual(nc, g, x_kept)


SINKHORN_ITERS, CLIP = 8, 1e-6


def sinkhorn(nc, g, logits, gates):
    E = logits.shape[2]
    with phase(nc) as (e, semaphore, begin):
        sb = lambda n, shape, dt=F32: e.enter_context(nc.sbuf_tensor(f"sk_{n}", shape, dt))
        sem = lambda n: semaphore(f"sk_{n}")
        ones = sb("ones", [P, P])
        p = sb("p", [P, B, TB, E])
        token_sum, expert_sum = sb("token_sum", [P, B, E]), sb("expert_sum", [P, B, TB])
        ones_set, step, p_ready, sums_done = sem("ones_set"), sem("step"), sem("p_ready"), sem("sums_done")
        bank = g.bank[0]
        block = begin()

        @block.gpsimd
        def _(pool):
            nc.gpsimd.memset(ones[:], 1.0).then_inc(ones_set, 1)

        @block.tensor
        def _(pe):
            pe.wait_ge(ones_set, ONE + 1)
            for n in range(SINKHORN_ITERS):
                pe.wait_ge(p_ready, ONE + n + 1)
                nc.tensor.matmul(bank[:, 0:T * E], ones[:], p[:].rearrange("p b q e -> p (b q e)"),
                                 start=True, stop=True).then_inc(sums_done, 1)

        @block.vector
        def _(dve):
            link = Chain(dve, step)
            nc.vector.tensor_scalar(p[:].rearrange("p b q e -> p (b q) e"), logits[:], CLIP, None, ALU.max).then_inc(p_ready, 1)
            for n in range(SINKHORN_ITERS):
                dve.wait_ge(sums_done, ONE + n + 1)
                link(nc.vector.tensor_reduce(token_sum[:], bank[:, 0:T * E].rearrange("p (b q e) -> p b e q", b=B, q=TB),
                                             axis=AX.X, op=ALU.add))
                link(nc.vector.reciprocal(token_sum[:], token_sum[:]))
                link(nc.vector.tensor_tensor(p[:], p[:], token_sum[:].unsqueeze(2).broadcast_to([P, B, TB, E]), ALU.mult))
                link(nc.vector.tensor_reduce(expert_sum[:], p[:], axis=AX.X, op=ALU.add))
                link(nc.vector.reciprocal(expert_sum[:], expert_sum[:]))
                last = n == SINKHORN_ITERS - 1
                dst = gates[:].rearrange("p q b e -> p b q e") if last else p[:]
                nc.vector.tensor_tensor(dst, p[:], expert_sum[:].unsqueeze(3).broadcast_to([P, B, TB, E]),
                                        ALU.mult).then_inc(p_ready, 1)


def top_tokens(nc, g, gates, index, value, place):
    E = gates.shape[3]
    BE, M = B * E, S // E
    ROUNDS = M // 8
    with phase(nc) as (e, semaphore, begin):
        sb = lambda n, shape, dt=F32: e.enter_context(nc.sbuf_tensor(f"tt_{n}", shape, dt))
        sem = lambda n: semaphore(f"tt_{n}")
        left = [sb(f"left{k}", [BE, S]) for k in range(2)]
        top, top_at = sb("top", [BE, M]), sb("top_at", [BE, M], U32)
        top_at_f = sb("top_at_f", [BE, M])
        indexT = sb("indexT", [M, BE])
        batch_row = sb("batch_row", [M, B, E])
        token = sb("token", [M, S], F16)
        rank1 = sb("rank1", [M, 1], BF16)
        expert = sb("expert", [P, E])
        tile_base = sb("tile_base", [P, B, TB])
        is_token = [sb(f"is_token{k}", [M, S], BF16) for k in range(2)]
        key = sb("key", [P, B, E, TB])
        best, best_i = sb("best", [P, T]), sb("best_i", [P, T], I32)
        best_e, best_r = sb("best_e", [P, T], I32), sb("best_r", [P, T], I32)
        row, has = sb("row", [P, T]), sb("has", [P, T])
        consts, gT_done, step, top_ready, topT_done, topT_ready = [sem(n) for n in (
            "consts", "gT_done", "step", "top_ready", "topT_done", "topT_ready")]
        is_ready, rank_done = sem("is_ready"), sem("rank_done")
        b_g, b_t, b_r = g.bank2[0], g.bank[2], g.bank[3]
        block = begin()

        @block.gpsimd
        def _(pool):
            io = dict(allow_small_or_imprecise_dtypes=True)
            nc.gpsimd.iota(token[:], pattern=[[1, S]], base=0, channel_multiplier=0, **io)
            nc.gpsimd.iota(rank1[:], pattern=[[0, 1]], base=1, channel_multiplier=1, **io)
            nc.gpsimd.iota(expert[:], pattern=[[1, E]], base=0, channel_multiplier=0, **io)
            nc.gpsimd.iota(batch_row[:], pattern=[[S, B], [0, E]], base=0, channel_multiplier=0, **io)
            nc.gpsimd.iota(tile_base[:], pattern=[[E * M, B], [0, TB]], base=-1, channel_multiplier=0, **io).then_inc(consts, 1)

        @block.tensor
        def _(pe):
            for q in range(TB):
                last = nc.tensor.transpose(b_g[0:BE, P * q:P * (q + 1)], gates[:, q].rearrange("p b e -> p (b e)"), g.ident[:])
            last.then_inc(gT_done, 1)
            pe.wait_ge(top_ready, ONE + 1)
            nc.tensor.transpose(b_t[:, 0:BE], top[:], g.ident[0:BE, 0:BE])
            nc.tensor.transpose(b_t[:, BE:2 * BE], top_at_f[:], g.ident[0:BE, 0:BE]).then_inc(topT_done, 1)
            pe.wait_ge(consts, ONE + 1)
            for n in range(BE):
                pe.wait_ge(is_ready, ONE + n + 1)
                for q in range(TB):
                    last = nc.tensor.matmul(b_r[:, TB * n + q:TB * n + q + 1], is_token[n % 2][:, P * q:P * (q + 1)],
                                            rank1[:], start=True, stop=True)
                last.then_inc(rank_done, 1)

        @block.vector
        def _(dve):
            link = Chain(dve, step)
            dve.wait_ge(gT_done, ONE + 1)
            link(nc.vector.tensor_copy(left[0][:], b_g[0:BE, :]))
            for r in range(ROUNDS):
                eight = slice(8 * r, 8 * r + 8)
                link(nc.vector.max(out=top[:, eight], in_=left[r % 2][:]))
                link(nc.vector.max_index(out=top_at[:, eight], in_max=top[:, eight], in_values=left[r % 2][:]))
                if r < ROUNDS - 1:
                    link(nc.vector.match_replace(out=left[(r + 1) % 2][:], in_to_replace=top[:, eight],
                                                 in_values=left[r % 2][:], imm_value=-1.0))
            nc.vector.tensor_copy(top_at_f[:], top_at[:]).then_inc(top_ready, 1)
            dve.wait_ge(topT_done, ONE + 1)
            nc.vector.tensor_copy(value[:], b_t[:, 0:BE])
            link(nc.vector.tensor_copy(indexT[:], b_t[:, BE:2 * BE]))
            dve.wait_ge(consts, ONE + 1)
            nc.vector.tensor_tensor(index[:], indexT[:], batch_row[:].rearrange("p b e -> p (b e)"), ALU.add)
            for n in range(BE):
                if n >= 2:
                    dve.wait_ge(rank_done, ONE + n - 1)
                nc.vector.tensor_scalar(is_token[n % 2][:], token[:], indexT[:, n:n + 1], None, ALU.is_equal).then_inc(is_ready, 1)
            dve.wait_ge(rank_done, ONE + BE)
            link(nc.vector.tensor_scalar(key[:].rearrange("p b e q -> p (b e q)"), b_r[:, 0:BE * TB], float(E), None, ALU.mult))
            link(nc.vector.tensor_tensor(key[:], key[:], expert[:].unsqueeze(1).unsqueeze(3).broadcast_to([P, B, E, TB]), ALU.add))
            link(nc.vector.tensor_reduce(best[:].rearrange("p (b q) -> p b q", b=B), key[:].rearrange("p b e q -> p b q e"),
                                         axis=AX.X, op=ALU.max))
            link(nc.vector.tensor_copy(best_i[:], best[:]))
            link(nc.vector.tensor_scalar(best_e[:], best_i[:], E - 1, None, ALU.bitwise_and))
            link(nc.vector.tensor_scalar(best_r[:], best_i[:], E.bit_length() - 1, None, ALU.logical_shift_right))
            link(nc.vector.scalar_tensor_tensor(row[:], best_e[:], float(M), best_r[:], ALU.mult, ALU.add))
            link(nc.vector.tensor_tensor(row[:], row[:], tile_base[:].rearrange("p b q -> p (b q)"), ALU.add))
            link(nc.vector.tensor_scalar(has[:], best_r[:], 0.0, None, ALU.is_gt))
            link(nc.vector.scalar_tensor_tensor(row[:], row[:], float(-N), has[:], ALU.add, ALU.mult))
            link(nc.vector.tensor_scalar(place[:], row[:], float(N), None, ALU.add))


def routed_experts(nc, g, rows, outputs, index, value, place, out):
    E = g.ins["L1_ffn_experts"].shape[0]
    BE, M = B * E, S // E
    SL = 4
    with phase(nc) as (e, semaphore, begin):
        sb = lambda n, shape, dt=F32: e.enter_context(nc.sbuf_tensor(f"re_{n}", shape, dt))
        sem = lambda n: semaphore(f"re_{n}")
        w = sb("w", [P, E, KD, D])
        taken = [sb(f"taken{s}", [M, D]) for s in range(SL)]
        takenT = [sb(f"takenT{s}", [P, KD, M]) for s in range(SL)]
        y = [sb(f"y{s}", [M, D]) for s in range(SL)]
        zero = sb("zero", [P, D])
        w_in, zero_set, zero_kept = sem("w_in"), sem("zero_set"), sem("zero_kept")
        taken_in = [semaphore(f"re_taken_in{s}", 0) for s in range(SL)]
        kept = [sem(f"kept{s}") for s in range(SL)]
        t_done, t_ready, y_done, y_ready = [sem(n) for n in ("t_done", "t_ready", "y_done", "y_ready")]
        b_t, b_y = g.bank[0:SL], g.bank[SL:2 * SL]
        block = begin()

        @block.sync
        def _(sp):
            sp.dma_start(w[:], g.ins["L1_ffn_experts"].rearrange("e (k p) n -> p e k n", p=P)).then_inc(w_in, 16)
            sp.wait_ge(zero_set, ONE + 1)
            sp.dma_start(outputs[N:N + P, :], zero[:]).then_inc(zero_kept, 16)
            dst = outputs[0:N, :].rearrange("(b e m) d -> b e m d", b=B, e=E)
            with sp.Fori(0, B) as b:
                for n in range(E):
                    sp.wait_ge(y_ready, ONE + b * E + n + 1)
                    sp.dma_start(dst[bass.ds(b, 1), n, :, :].rearrange("b m d -> (b m) d"), y[n % SL][:]).then_inc(kept[n % SL], 16)
            sp.wait_ge(zero_kept, ONE + 16)
            for s in range(SL):
                sp.wait_ge(kept[s], ONE + 16 * BE // SL)

        @block.gpsimd
        def _(pool):
            nc.gpsimd.memset(zero[:], 0.0).then_inc(zero_set, 1)
            for n in range(BE):
                if n >= SL:
                    pool.wait_ge(t_done, ONE + n - SL + 1)
                nc.gpsimd.indirect_dma_start(out=taken[n % SL][:], out_offset=None, in_=rows,
                                             in_offset=bass.IndirectOffsetOnAxis(ap=index[:, n:n + 1], axis=0)
                                             ).then_inc(taken_in[n % SL], 16)

        @block.tensor
        def _(pe):
            pe.wait_ge(w_in, ONE + 16)
            with pe.Fori(0, B) as b:
                for n in range(E):
                    s, at = n % SL, b * E + n
                    pe.wait_ge(taken_in[s], 16 * (E // SL) * b + 16 * (n // SL + 1))
                    if n >= SL:
                        pe.wait_ge(t_ready, ONE + at - SL + 1)
                    else:
                        pe.wait_ge(t_ready, ONE + b * E)
                    for k in range(KD):
                        last = nc.tensor.transpose(b_t[s][:, M * k:M * (k + 1)], taken[s][:, P * k:P * (k + 1)], g.ident[:])
                    last.then_inc(t_done, 1)
                    pe.wait_ge(t_ready, ONE + at + 1)
                    if n >= SL:
                        pe.wait_ge(y_ready, ONE + at - SL + 1)
                    else:
                        pe.wait_ge(y_ready, ONE + b * E)
                    for k in range(KD):
                        last = nc.tensor.matmul(b_y[s][:, 0:D], takenT[s][:, k, :], w[:, n, k, :],
                                                start=(k == 0), stop=(k == KD - 1))
                    last.then_inc(y_done, 1)

        @block.scalar
        def _(act):
            with act.Fori(0, B) as b:
                for n in range(E):
                    s, at = n % SL, b * E + n
                    act.wait_ge(t_done, ONE + at + 1)
                    if n >= SL:
                        act.wait_ge(y_done, ONE + at - SL + 1)
                    else:
                        act.wait_ge(y_done, ONE + b * E)
                    nc.scalar.activation(takenT[s][:], b_t[s][:, 0:KD * M].rearrange("p (k m) -> p k m", k=KD),
                                         ACT.Copy).then_inc(t_ready, 1)

        @block.vector
        def _(dve):
            with dve.Fori(0, B) as b:
                for n in range(E):
                    s, at = n % SL, b * E + n
                    dve.wait_ge(y_done, ONE + at + 1)
                    if n >= SL:
                        dve.wait_ge(kept[s], ONE + 16 * (E // SL) * b + 16 * (n // SL))
                    else:
                        dve.wait_ge(kept[s], ONE + 16 * (E // SL) * b)
                    nc.vector.tensor_scalar(y[s][:], b_y[s][:, 0:D], value[:, bass.ds(at, 1)], None, ALU.mult).then_inc(y_ready, 1)
    with phase(nc) as (e, semaphore, begin):
        sem = lambda n: semaphore(f"rb_{n}")
        got = [e.enter_context(nc.sbuf_tensor(f"rb_got{s}", [P, D], F32)) for s in range(SL)]
        got_in = [semaphore(f"rb_got_in{s}", 0) for s in range(SL)]
        x_ready, out_done = sem("x_ready"), sem("out_done")
        block = begin()

        @block.gpsimd
        def _(pool):
            for t in range(T):
                if t >= SL:
                    pool.wait_ge(x_ready, ONE + t - SL + 1)
                nc.gpsimd.indirect_dma_start(out=got[t % SL][:], out_offset=None, in_=outputs,
                                             in_offset=bass.IndirectOffsetOnAxis(ap=place[:, t:t + 1], axis=0)
                                             ).then_inc(got_in[t % SL], 16)

        @block.vector
        def _(dve):
            with dve.Fori(0, T // SL) as i:
                for s in range(SL):
                    xt = g.x[:, bass.ds(SL * i + s, 1), :].rearrange("p o d -> p (o d)")
                    dve.wait_ge(got_in[s], 16 * i + 16)
                    nc.vector.tensor_tensor(xt, got[s][:], xt, ALU.add).then_inc(x_ready, 1)

        @block.sync
        def _(sp):
            dst = out.rearrange("b (t p) d -> (b t) p d", p=P)
            with sp.Fori(0, T) as t:
                sp.wait_ge(x_ready, ONE + t + 1)
                sp.dma_start(dst[bass.ds(t, 1), :, :].rearrange("t p d -> (t p) d"),
                             g.x[:, bass.ds(t, 1), :].rearrange("p o d -> p (o d)")).then_inc(out_done, 16)
            sp.wait_ge(out_done, ONE + 16 * T)


def mixture1(nc, g, out):
    E = g.ins["L1_ffn_gate_w"].shape[1]
    BE, M = B * E, S // E
    rows = nc.dram_tensor("routed_rows", [N, D], F32, kind="Internal").ap()
    outputs = nc.dram_tensor("routed_outputs", [N + P, D], F32, kind="Internal").ap()
    with ExitStack() as e:
        sb = lambda n, shape, dt=F32: e.enter_context(nc.sbuf_tensor(f"m1_{n}", shape, dt))
        logits = sb("logits", [P, T, E])
        gates = sb("gates", [P, TB, B, E])
        index, value, place = sb("index", [M, BE], U32), sb("value", [M, BE]), sb("place", [P, T], U32)
        normalised_pairs(nc, g, "np1", g.ins["L1_ffn_gate_w"], None, None, logits, rows_out=rows)
        sinkhorn(nc, g, logits, gates)
        top_tokens(nc, g, gates, index, value, place)
        routed_experts(nc, g, rows, outputs, index, value, place, out)


def program(nc, g, out, stop=""):
    setup(nc, g)
    finish_stats(nc, g, "ln0")
    E = g.ins["L0_ffn_rw1"].shape[0]
    sorted_rows = nc.dram_tensor("sorted_rows", [(2 * T + E) * P, D], F32, kind="Internal").ap()
    window_attention(nc, g, sorted_rows)
    if stop == "A":
        return
    finish_stats(nc, g, "ln1")
    mixture0(nc, g, sorted_rows)
    if stop == "B":
        return
    finish_stats(nc, g, "ln2")
    attention1(nc, g)
    if stop == "C":
        return
    finish_stats(nc, g, "ln4")
    mixture1(nc, g, out)


_INS = ['L0_attn_x', 'L0_attn_W_qkv', 'L0_attn_W_out', 'L0_ffn_gate_w', 'L0_ffn_gate_b', 'L0_ffn_rw1', 'L0_ffn_rb1',
        'L0_ffn_rw2', 'L0_ffn_rb2', 'L0_ffn_rw3', 'L0_ffn_rb3', 'L0_ffn_sw1', 'L0_ffn_sb1', 'L0_ffn_sw2', 'L0_ffn_sb2',
        'L0_ffn_sw3', 'L0_ffn_sb3', 'L1_attn_wq', 'L1_attn_bq', 'L1_attn_wk', 'L1_attn_bk', 'L1_attn_wv', 'L1_attn_bv',
        'L1_attn_wo', 'L1_attn_bo', 'L1_attn_gamma', 'L1_attn_beta', 'L1_ffn_gate_w', 'L1_ffn_experts']


def kernel(**inputs):
    import numpy as _np
    import concourse.bacc as _bacc
    from concourse import mybir as _mybir
    from concourse.bass_utils import run_bass_kernel_spmd as _run

    nc = _bacc.Bacc("TRN2", target_bir_lowering=False, num_devices=1)
    arrays, aps = {}, {}
    for name in _INS:
        a = _np.ascontiguousarray(inputs[name])
        arrays[f"in_{name}_dram"] = a
        aps[name] = nc.dram_tensor(f"in_{name}_dram", a.shape, _mybir.dt.from_np(a.dtype), kind="ExternalInput").ap()
    out = nc.dram_tensor("out_0_dram", (B, S, D), F32, kind="ExternalOutput").ap()
    with ExitStack() as ctx:
        program(nc, Shared(ctx, aps), out)
    r = _run(nc, [arrays], core_ids=[0])
    return r.results[0]["out_0_dram"]
```

```python
import concourse.bass as bass
from concourse import mybir
from contextlib import ExitStack, contextmanager

F32 = mybir.dt.float32
F32R = mybir.dt.float32r
BF16 = mybir.dt.bfloat16
F16 = mybir.dt.float16
U32 = mybir.dt.uint32
I32 = mybir.dt.int32
ALU = mybir.AluOpType
ACT = mybir.ActivationFunctionType
AX = mybir.AxisListType

P = 128
B, S, D = 4, 1024, 256
N = B * S
T = N // P
TB = S // P
KD = D // P
NH, DH = 16, 16
SCALE = DH ** -0.5
WIN = 64
LN_EPS = 1e-5
ONE = 1
NEG = -1e30
BN = 6


class Shared:

    def __init__(self, ctx, ins):
        self.ctx, self.ins = ctx, ins


class Chain:

    def __init__(self, eng, sem):
        self.eng, self.sem, self.count = eng, sem, ONE

    def __call__(self, ins):
        ins.then_inc(self.sem, 1)
        self.count += 1
        self.eng.wait_ge(self.sem, self.count)


@contextmanager
def phase(nc):
    sems = []
    with ExitStack() as e:
        def semaphore(name, start=ONE):
            sem = e.enter_context(nc.semaphore(name))
            sems.append((sem, start))
            return sem

        def begin():
            with nc.Block() as block:
                @block.sync
                def _(sp):
                    for sem, _ in sems:
                        sp.sem_clear(sem)
                    for sem, start in sems:
                        if start:
                            sp.sem_inc(sem, start)
            return e.enter_context(nc.Block())

        yield e, semaphore, begin


def setup(nc, g):
    c = g.ctx
    sb = lambda name, shape, dt=F32: c.enter_context(nc.sbuf_tensor(name, shape, dt))
    g.x = sb("x", [P, T, D])
    g.stats = sb("stats", [P, T, BN])
    g.mean = sb("mean", [P, T])
    g.rstd = sb("rstd", [P, T])
    g.ident = sb("ident", [P, P])
    g.bank2 = [c.enter_context(nc.psum_tensor(f"banks{i}", [P, 1024], F32)) for i in range(4)]
    g.bank = [g.bank2[i // 2][:, 512 * (i % 2):512 * (i % 2 + 1)] for i in range(8)]
    with phase(nc) as (e, semaphore, begin):
        x_in = [semaphore(f"x_in{b}") for b in range(B)]
        ident_zero = semaphore("ident_zero")
        ident_set = semaphore("ident_set")
        stats_done = semaphore("stats0_done")
        block = begin()

        @block.sync
        def _(sp):
            for b in range(B):
                src = g.ins["L0_attn_x"][b].rearrange("(t p) d -> p t d", p=P)
                sp.dma_start(g.x[:, b * TB:(b + 1) * TB, :], src).then_inc(x_in[b], 16)

        @block.gpsimd
        def _(pool):
            nc.gpsimd.memset(g.ident[:], 0.0).then_inc(ident_zero, 1)
            pool.wait_ge(ident_zero, ONE + 1)
            nc.gpsimd.affine_select(out=g.ident[:], in_=g.ident[:], compare_op=ALU.not_equal, fill=1.0, base=0,
                                    pattern=[[-1, P]], channel_multiplier=1).then_inc(ident_set, 1)

        @block.vector
        def _(dve):
            for b in range(B):
                dve.wait_ge(x_in[b], ONE + 16)
                with dve.Fori(b * TB, (b + 1) * TB) as t:
                    nc.vector.bn_stats(g.stats[:, bass.ds(t, 1), :], g.x[:, bass.ds(t, 1), :]).then_inc(stats_done, 1)


def finish_stats(nc, g, name):
    with phase(nc) as (e, semaphore, begin):
        sb = lambda n, shape, dt=F32: e.enter_context(nc.sbuf_tensor(f"{name}_{n}", shape, dt))
        diff, var, std = sb("diff", [P, T]), sb("var", [P, T]), sb("std", [P, T])
        eps = sb("eps", [P, 1])
        step = semaphore(f"{name}_step")
        var_ready = semaphore(f"{name}_var_ready")
        std_ready = semaphore(f"{name}_std_ready")
        rstd_ready = semaphore(f"{name}_rstd_ready")
        block = begin()
        half = float(D // 2)

        @block.vector
        def _(dve):
            link = Chain(dve, step)
            even, odd = g.stats[:, :, 1], g.stats[:, :, 4]
            nc.vector.memset(eps[:], LN_EPS)
            nc.vector.tensor_tensor(g.mean[:], even, odd, ALU.add)
            nc.vector.tensor_tensor(var[:], g.stats[:, :, 2], g.stats[:, :, 5], ALU.add)
            link(nc.vector.tensor_tensor(diff[:], even, odd, ALU.subtract))
            link(nc.vector.scalar_tensor_tensor(diff[:], diff[:], half / 2.0, diff[:], ALU.mult, ALU.mult))
            link(nc.vector.tensor_tensor(var[:], var[:], diff[:], ALU.add))
            nc.vector.tensor_scalar(var[:], var[:], 1.0 / D, None, ALU.mult).then_inc(var_ready, 1)
            link(nc.vector.tensor_scalar(g.mean[:], g.mean[:], 0.5, None, ALU.mult))
            dve.wait_ge(std_ready, ONE + 1)
            nc.vector.reciprocal(g.rstd[:], std[:]).then_inc(rstd_ready, 1)

        @block.scalar
        def _(act):
            act.wait_ge(var_ready, ONE + 1)
            nc.scalar.activation(std[:], var[:], ACT.Sqrt, bias=eps[:, 0:1]).then_inc(std_ready, 1)


def window_attention(nc, g, to_clear):
    NP = T // 2
    HM = P // DH
    HU = 4
    NU = NH // HU
    R = P // HU
    W2 = 2 * WIN
    Q = P // 2
    with phase(nc) as (e, semaphore, begin):
        sb = lambda n, shape, dt=F32: e.enter_context(nc.sbuf_tensor(f"wa_{n}", shape, dt))
        sem = lambda n: semaphore(f"wa_{n}")
        wqkv = sb("wqkv", [P, KD, 3 * D])
        wo = sb("wo", [P, NU, D])
        ident_bf = sb("ident_bf", [P, P], BF16)
        mask0 = sb("mask0", [P, NP, W2], BF16)
        mask1 = sb("mask1", [P, W2], BF16)
        head_rows = sb("head_rows", [P, HM])
        sum_rows = sb("sum_rows", [P, P])
        xn = [sb(f"xn{s}", [P, D]) for s in range(2)]
        xnT = sb("xnT", [P, KD, WIN + 2 * P])
        kT = [sb(f"kT{a}", [P, KD, WIN + 2 * P]) for a in range(2)]
        q = sb("q", [P, KD, 2 * P])
        q_heads = [sb(f"q_heads{a}", [P, KD, HM, 2 * P]) for a in range(2)]
        v = [sb(f"v{a}", [P, 4, NH, R]) for a in range(2)]
        nmax = [sb(f"nmax{k}", [P, HU]) for k in range(2)]
        ex = [sb(f"ex{k}", [P, HU, W2]) for k in range(2)]
        prob = [sb(f"prob{k}", [P, HU, W2]) for k in range(2)]
        probT = [sb(f"probT{k}", [P, HU, P]) for k in range(2)]
        o = [sb(f"o{s}", [P, NU, P]) for s in range(2)]
        rsum = sb("rsum", [P, NU, P])
        on = [sb(f"on{s}", [P, NU, P]) for s in range(2)]
        zero = sb("zero", [P, D])
        zero_set, cleared = sem("zero_set"), sem("cleared")
        w_in, wo_zero, const = sem("w_in"), sem("wo_zero"), sem("const")
        consts_set, tails_zero, v_zero, v_set = sem("consts_set"), sem("tails_zero"), sem("v_zero"), sem("v_set")
        xn_ready, xnT_done, xnT_ready, x_tail, k_tail = [sem(n) for n in (
            "xn_ready", "xnT_done", "xnT_ready", "x_tail", "k_tail")]
        q_copied = sem("q_copied")
        q_done, q_ready, k_done, k_ready, v_done, v_ready = [sem(n) for n in (
            "q_done", "q_ready", "k_done", "k_ready", "v_done", "v_ready")]
        s_done, max_ready, ex_ready, prob_ready, probT_done, probT_ready, out_done = [sem(n) for n in (
            "s_done", "max_ready", "ex_ready", "prob_ready", "probT_done", "probT_ready", "out_done")]
        o_ready, sum_done, rsum_ready, on_ready, y_done, x_ready, stats_ready = [sem(n) for n in (
            "o_ready", "sum_done", "rsum_ready", "on_ready", "y_done", "x_ready", "stats_ready")]
        b_s, b_pt, b_o, b_m = [g.bank[2 * n:2 * n + 2] for n in range(4)]
        block = begin()
        half = lambda n: slice(n * Q, (n + 1) * Q)

        @block.sync
        def _(sp):
            sp.dma_start(wqkv[:], g.ins["L0_attn_W_qkv"].rearrange("(k p) n -> p k n", p=P)).then_inc(w_in, 16)
            sp.wait_ge(wo_zero, ONE + 1)
            for j in range(HU):
                src = g.ins["L0_attn_W_out"].rearrange("(m j d) n -> j d m n", j=HU, d=DH)[j]
                sp.dma_start(wo[R * j:R * j + DH], src).then_inc(w_in, 16)
            sp.wait_ge(zero_set, ONE + 1)
            blocks = to_clear.shape[0] // P
            sp.dma_start(to_clear.rearrange("(j p) d -> p j d", p=P),
                         zero[:].unsqueeze(1).broadcast_to([P, blocks, D])).then_inc(cleared, 16)
            sp.wait_ge(cleared, ONE + 16)

        @block.gpsimd
        def _(pool):
            link = Chain(pool, const)
            nc.gpsimd.memset(zero[:], 0.0).then_inc(zero_set, 1)
            nc.gpsimd.memset(wo[:], 0.0).then_inc(wo_zero, 1)
            nc.gpsimd.memset(mask0[:], 0.0)
            nc.gpsimd.memset(mask1[:], 0.0)
            nc.gpsimd.memset(head_rows[:], 1.0)
            nc.gpsimd.memset(xnT[:, :, 0:WIN], 0.0)
            nc.gpsimd.memset(kT[0][:, :, 0:WIN], 0.0).then_inc(tails_zero, 1)
            link(nc.gpsimd.memset(sum_rows[:], 0.0))
            for h in range(2):
                for m, pat in ((mask0, [[0, NP]]), (mask1, [])):
                    m = m[half(h)]
                    link(nc.gpsimd.affine_select(out=m, in_=m, compare_op=ALU.is_ge, fill=NEG, base=WIN,
                                                 pattern=pat + [[-1, W2]], channel_multiplier=1))
                    link(nc.gpsimd.affine_select(out=m, in_=m, compare_op=ALU.is_ge, fill=NEG, base=-1,
                                                 pattern=pat + [[1, W2]], channel_multiplier=-1))
            m = mask0[half(0)].rearrange("p (b j) w -> p b j w", b=B)[:, :, 0, :]
            nc.gpsimd.affine_select(out=m, in_=m, compare_op=ALU.is_ge, fill=NEG, base=-WIN,
                                    pattern=[[0, B], [1, W2]], channel_multiplier=0)
            link(nc.gpsimd.affine_select(out=head_rows[:], in_=head_rows[:], compare_op=ALU.is_ge, fill=0.0, base=0,
                                         pattern=[[-DH, HM]], channel_multiplier=1))
            link(nc.gpsimd.affine_select(out=head_rows[:], in_=head_rows[:], compare_op=ALU.is_ge, fill=0.0,
                                         base=DH - 1, pattern=[[DH, HM]], channel_multiplier=-1))
            sr = sum_rows[:].rearrange("p (j r) -> p j r", j=HU)
            link(nc.gpsimd.affine_select(out=sr, in_=sr, compare_op=ALU.not_equal, fill=1.0, base=-DH,
                                         pattern=[[-R, HU], [0, R]], channel_multiplier=1))
            nc.gpsimd.tensor_copy(ident_bf[:], g.ident[:]).then_inc(consts_set, 1)
            pool.wait_ge(consts_set, ONE + 1)

            def heads(r, c):
                i = 2 * r + c
                pool.wait_ge(q_copied, ONE + i + 1)
                if c >= 2:
                    pool.wait_ge(s_done, ONE + 2 * NU * (i - 1))
                for k in range(KD):
                    nc.gpsimd.tensor_tensor(q_heads[c % 2][:, k], q[:, k, :].unsqueeze(1).broadcast_to([P, HM, 2 * P]),
                                            head_rows[:].unsqueeze(2).broadcast_to([P, HM, 2 * P]), ALU.mult).then_inc(q_ready, 1)

            for c in range(2):
                heads(0, c)
            with pool.Fori(0, NP // 2 - 1) as r:
                for c in (2, 3):
                    heads(r, c)

        UP = 2 * NU

        def between(c):
            uses = []
            if c >= 1:
                uses += [(1, "project", -1, 0), (3, "sum", -1, 1), (5, "project", -1, 1)]
            if c < NP - 1:
                uses += [(1, "x", 1, 0), (2, "q", 1, 0), (4, "k", 1, 0), (5, "v", 1, 0), (6, "v", 1, 1)]
            if 0 <= c < NP:
                uses.append((7, "sum", 0, 0))
            return sorted(uses, key=lambda use: use[0])

        def turn(c, n):
            first = [0, len(between(-1)), len(between(-1)) + len(between(0))]
            return n + (first[c + 1] if c <= 1 else first[2] + len(between(1)) * (c - 1))

        def steps(eng, step):
            for c in (-1, 0):
                step(0, c)
            with eng.Fori(0, NP // 2 - 1) as r:
                for c in (1, 2):
                    step(r, c)
            for c in (NP - 1, NP):
                step(0, c)

        def unit_at(c, place):
            return (place, c) if place >= 0 else (UP + place, c - 1)

        @block.vector
        def _(dve):
            for a in range(2):
                nc.vector.memset(v[a][:], 0.0).then_inc(v_zero, 1)
            dve.wait_ge(v_zero, ONE + 2)
            for a in range(2):
                nc.vector.memset(v[a][:, :, :, DH:DH + 1], 1.0).then_inc(v_set, 1)
            dve.wait_ge(consts_set, ONE + 1)

            def normalise(r, c):
                p = 2 * r + c
                for s in range(2):
                    t = 2 * p + s
                    if c > 0:
                        dve.wait_ge(xnT_done, ONE + p)
                    nc.vector.tensor_scalar(xn[s][:], g.x[:, bass.ds(t, 1), :].rearrange("p o d -> p (o d)"),
                                            g.mean[:, bass.ds(t, 1)], g.rstd[:, bass.ds(t, 1)],
                                            ALU.subtract, ALU.mult).then_inc(xn_ready, 1)

            def shifted(r, c, u):
                n, k = UP * (2 * r + c) + u, u % 2
                sc = b_s[k][:].rearrange("p (h w) -> p h w", h=HU)
                dve.wait_ge(s_done, ONE + n + 1)
                if c > 0 or u >= 2:
                    dve.wait_ge(prob_ready, ONE + n - 1)
                nc.vector.tensor_reduce(nmax[k][:], sc, axis=AX.X, op=ALU.max, negate=True).then_inc(max_ready, 1)
                dve.wait_ge(max_ready, ONE + n + 1)
                nc.vector.tensor_tensor(ex[k][:], sc, nmax[k][:].unsqueeze(2).broadcast_to([P, HU, W2]),
                                        ALU.add).then_inc(ex_ready, 1)

            def inverse(bank, n):
                some = slice(n * NU // 2, (n + 1) * NU // 2)
                nc.vector.reciprocal(rsum[:, some], bank[:].rearrange("p (m q) -> p m q", m=NU)[:, some]).then_inc(rsum_ready, 1)

            def over_sums(r, c, n, shift, s):
                i = 2 * r + c + shift
                inverse(b_m[turn(c, n) % 2], 1)
                dve.wait_ge(rsum_ready, ONE + 4 * i + 2 * s + 2)
                nc.vector.tensor_tensor(on[s][:], o[s][:], rsum[:], ALU.mult).then_inc(on_ready, 1)

            def step(r, c):
                uses = list(enumerate(between(c)))
                for place in range(UP):
                    if 0 <= c < NP:
                        shifted(r, c, place)
                    for n, (at, kind, shift, s) in uses:
                        if kind == "sum" and at == place - 1:
                            over_sums(r, c, n, shift, s)
                    if place == 0 and c >= 1:
                        over_sums(r, c - 1, len(between(c - 1)) - 1, 0, 0)
                    if place == 0 and c < NP - 1:
                        normalise(r, c + 1)
                    for n, (at, kind, shift, s) in uses:
                        if at != place:
                            continue
                        bank, i = b_m[turn(c, n) % 2], 2 * r + c + shift
                        if kind == "sum":
                            dve.wait_ge(sum_done, ONE + 2 * i + s + 1)
                            inverse(bank, 0)
                        elif kind == "project":
                            xt = g.x[:, bass.ds(2 * i + s, 1), :].rearrange("p o d -> p (o d)")
                            dve.wait_ge(y_done, ONE + 2 * i + s + 1)
                            nc.vector.tensor_tensor(xt, bank[:, 0:D], xt, ALU.add).then_inc(x_ready, 1)
                            dve.wait_ge(x_ready, ONE + 2 * i + s + 1)
                            nc.vector.bn_stats(g.stats[:, bass.ds(2 * i + s, 1), :], xt).then_inc(stats_ready, 1)

            steps(dve, step)

        @block.scalar
        def _(act):
            act.wait_ge(tails_zero, ONE + 1)
            act.wait_ge(v_set, ONE + 2)

            def weights(r, c, u):
                n, k = UP * (2 * r + c) + u, u % 2
                act.wait_ge(ex_ready, ONE + n + 1)
                if c > 0 or u >= 2:
                    act.wait_ge(probT_done, ONE + n - 1)
                nc.scalar.activation(prob[k][:], ex[k][:], ACT.Exp, scale=SCALE).then_inc(prob_ready, 1)

            def transposed(r, c, u):
                n, k = UP * (2 * r + c) + u, u % 2
                act.wait_ge(probT_done, ONE + n + 1)
                if c > 0 or u >= 2:
                    act.wait_ge(out_done, ONE + n - 1)
                nc.scalar.activation(probT[k][:], b_pt[k][:].rearrange("p (h q) -> p h q", h=HU),
                                     ACT.Copy).then_inc(probT_ready, 1)

            def outputs(r, c, s):
                i = 2 * r + c
                act.wait_ge(out_done, ONE + UP * i + NU * (s + 1))
                if c > 0:
                    act.wait_ge(on_ready, ONE + 2 * i + s - 1)
                nc.scalar.activation(o[s][:], b_o[s][:].rearrange("p (m q) -> p m q", m=NU), ACT.Copy).then_inc(o_ready, 1)

            def step(r, c):
                uses = list(enumerate(between(c)))
                for place in range(UP):
                    u, uc = unit_at(c, place - 1)
                    if 0 <= uc < NP:
                        transposed(r, uc, u)
                    if 0 <= c < NP:
                        weights(r, c, place)
                    if place == 2 and c >= 1:
                        outputs(r, c - 1, 1)
                    if place == NU + 2 and 0 <= c < NP:
                        outputs(r, c, 0)
                    for n, (at, kind, shift, s) in uses:
                        if at != place:
                            continue
                        bank, i, a = b_m[turn(c, n) % 2], 2 * r + c + shift, (c + shift) % 2
                        first = c + shift == 0
                        if kind == "x":
                            act.wait_ge(xnT_done, ONE + i + 1)
                            if not first:
                                act.wait_ge(v_done, ONE + 2 * i)
                                act.wait_ge(xnT_ready, ONE + i)
                                nc.scalar.activation(xnT[:, :, 0:WIN], xnT[:, :, 2 * P:2 * P + WIN], ACT.Copy).then_inc(x_tail, 1)
                                act.wait_ge(x_tail, ONE + i)
                            nc.scalar.activation(xnT[:, :, WIN:WIN + 2 * P].rearrange("p k (h q) -> p h k q", h=2),
                                                 bank[:].rearrange("p (h k q) -> p h k q", h=2, k=KD),
                                                 ACT.Copy).then_inc(xnT_ready, 1)
                        elif kind == "q":
                            act.wait_ge(q_done, ONE + i + 1)
                            if not first:
                                act.wait_ge(q_ready, ONE + KD * i)
                            nc.scalar.activation(q[:], bank[:].rearrange("p (k q) -> p k q", k=KD), ACT.Copy).then_inc(q_copied, 1)
                        elif kind == "k":
                            act.wait_ge(k_done, ONE + i + 1)
                            if not first:
                                if c + shift >= 2:
                                    act.wait_ge(s_done, ONE + UP * (i - 1))
                                act.wait_ge(k_ready, ONE + i)
                                nc.scalar.activation(kT[a][:, :, 0:WIN], kT[1 - a][:, :, 2 * P:2 * P + WIN], ACT.Copy).then_inc(k_tail, 1)
                            nc.scalar.activation(kT[a][:, :, WIN:WIN + 2 * P], bank[:].rearrange("p (k q) -> p k q", k=KD),
                                                 ACT.Copy).then_inc(k_ready, 1)
                        elif kind == "v":
                            act.wait_ge(v_done, ONE + 2 * i + s + 1)
                            if c + shift >= 2:
                                act.wait_ge(out_done, ONE + UP * (i - 1))
                            nc.scalar.activation(v[a][:, 2 * s:2 * s + 2, :, 0:DH],
                                                 bank[:].rearrange("p (a h d) -> p a h d", a=2, h=NH),
                                                 ACT.Copy).then_inc(v_ready, 1)

            steps(act, step)

        @block.tensor
        def _(pe):
            pe.wait_ge(w_in, ONE + 16 * (1 + HU))
            pe.wait_ge(consts_set, ONE + 1)

            def bank_read(r, c, kind, shift, s):
                i = 2 * r + c + shift
                {"x": lambda: pe.wait_ge(xnT_ready, ONE + i + 1),
                 "q": lambda: pe.wait_ge(q_copied, ONE + i + 1),
                 "k": lambda: pe.wait_ge(k_ready, ONE + i + 1),
                 "v": lambda: pe.wait_ge(v_ready, ONE + 2 * i + s + 1),
                 "sum": lambda: pe.wait_ge(on_ready, ONE + 2 * i + s + 1),
                 "project": lambda: pe.wait_ge(x_ready, ONE + 2 * i + s + 1)}[kind]()

            def use(r, c, n, kind, shift, s):
                bank, i = b_m[turn(c, n) % 2], 2 * r + c + shift
                if turn(c, n) >= 2:
                    if n >= 2:
                        bank_read(r, c, *between(c)[n - 2][1:])
                    else:
                        bank_read(r, c - 1, *between(c - 1)[n - 2][1:])
                if kind == "x":
                    pe.wait_ge(xn_ready, ONE + 2 * i + 2)
                    for h in range(2):
                        for k in range(KD):
                            last = nc.tensor.transpose(bank[:, P * (KD * h + k):P * (KD * h + k + 1)],
                                                       xn[h][:, P * k:P * (k + 1)], g.ident[:])
                    last.then_inc(xnT_done, 1)
                elif kind in ("q", "k"):
                    pe.wait_ge(xnT_ready, ONE + i + 1)
                    part = ("q", "k").index(kind)
                    for m in range(KD):
                        for k in range(KD):
                            last = nc.tensor.matmul(bank[:, 2 * P * m:2 * P * (m + 1)],
                                                    wqkv[:, k, D * part + P * m:D * part + P * (m + 1)],
                                                    xnT[:, k, WIN:WIN + 2 * P], start=(k == 0), stop=(k == KD - 1))
                    last.then_inc((q_done, k_done)[part], 1)
                elif kind == "v":
                    if c + shift > 0:
                        pe.wait_ge(x_tail, ONE + i)
                    for h in range(2):
                        at = P * s + Q * h
                        for k in range(KD):
                            last = nc.tensor.matmul(bank[:, D * h:D * (h + 1)], xnT[:, k, at:at + P],
                                                    wqkv[:, k, 2 * D:3 * D], start=(k == 0), stop=(k == KD - 1))
                    last.then_inc(v_done, 1)
                elif kind == "sum":
                    pe.wait_ge(o_ready, ONE + 2 * i + s + 1)
                    nc.tensor.matmul(bank[:], sum_rows[:], o[s][:], start=True, stop=True).then_inc(sum_done, 1)
                else:
                    pe.wait_ge(on_ready, ONE + 2 * i + s + 1)
                    for m in range(NU):
                        last = nc.tensor.matmul(bank[:, 0:D], on[s][:, m, :], wo[:, m, :],
                                                start=(m == 0), stop=(m == NU - 1))
                    last.then_inc(y_done, 1)

            def scores(r, c, u):
                i, s, m, a = 2 * r + c, u // NU, u % NU, c % 2
                n = UP * i + u
                bank = b_s[u % 2]
                if u == 0:
                    pe.wait_ge(q_ready, ONE + KD * i + KD)
                    pe.wait_ge(k_ready, ONE + i + 1)
                    if c > 0:
                        pe.wait_ge(k_tail, ONE + i)
                if c > 0 or u >= 2:
                    pe.wait_ge(ex_ready, ONE + n - 1)
                mask = mask1[:].unsqueeze(1) if s else mask0[:, bass.ds(i, 1), :]
                nc.tensor.matmul(bank[:].rearrange("p (h w) -> p h w", h=HU), ident_bf[:],
                                 mask.broadcast_to([P, HU, W2]), start=True, stop=False, skip_group_check=True)
                k = m // (HM // HU)
                for j in range(HU):
                    head = HU * m % HM + j
                    for h in range(2):
                        at = P * s + Q * h
                        last = nc.tensor.matmul(bank[half(h), W2 * j:W2 * (j + 1)],
                                                q_heads[a][:, k, head, at:at + Q], kT[a][:, k, at:at + P],
                                                start=False, stop=True, skip_group_check=True)
                last.then_inc(s_done, 1)

            def transposes(r, c, u):
                n, k = UP * (2 * r + c) + u, u % 2
                pe.wait_ge(prob_ready, ONE + n + 1)
                if c > 0 or u >= 2:
                    pe.wait_ge(probT_ready, ONE + n - 1)
                for j in range(HU):
                    last = nc.tensor.transpose(b_pt[k][:, P * j:P * (j + 1)], prob[k][:, j, :], g.ident[:])
                last.then_inc(probT_done, 1)

            def outputs(r, c, u):
                i, s, m = 2 * r + c, u // NU, u % NU
                n = UP * i + u
                if m == 0:
                    pe.wait_ge(v_ready, ONE + 2 * i + s + 1)
                    if c > 0:
                        pe.wait_ge(o_ready, ONE + 2 * i + s - 1)
                pe.wait_ge(probT_ready, ONE + n + 1)
                for j in range(HU):
                    for h in range(2):
                        last = nc.tensor.matmul(b_o[s][R * j:R * (j + 1), P * m + Q * h:P * m + Q * (h + 1)],
                                                v[c % 2][:, 2 * s + h, HU * m + j, :], probT[u % 2][:, j, half(h)],
                                                start=True, stop=True)
                last.then_inc(out_done, 1)

            def step(r, c):
                uses = list(enumerate(between(c)))
                for place in range(UP):
                    if 0 <= c < NP:
                        scores(r, c, place)
                    u, uc = unit_at(c, place - 1)
                    if 0 <= uc < NP:
                        transposes(r, uc, u)
                    for n, (at, kind, shift, s) in uses:
                        if at == place:
                            use(r, c, n, kind, shift, s)
                    u, uc = unit_at(c, place - 2)
                    if 0 <= uc < NP:
                        outputs(r, uc, u)

            steps(pe, step)


def normalised_tiles(nc, g, name, gate, gate_b, logits, rows_out, xnT_parts=None):
    E = logits.shape[2]
    C = 4
    with phase(nc) as (e, semaphore, begin):
        sb = lambda n, shape, dt=F32: e.enter_context(nc.sbuf_tensor(f"{name}_{n}", shape, dt))
        sem = lambda n: semaphore(f"{name}_{n}")
        gw = sb("gw", [P, KD, E])
        gb = sb("gb", [1, E])
        ones = sb("ones", [1, P])
        xn = [sb(f"xn{s}", [P, D]) for s in range(C)]
        xnT = [sb(f"xnT{s}", [P, KD, P]) for s in range(C)]
        gate_in, gb_set = sem("gate_in"), sem("gb_set")
        xn_ready, xnT_done, xnT_ready, hi_ready, lo_ready, l_done, l_ready = [
            sem(n) for n in ("xn_ready", "xnT_done", "xnT_ready", "hi_ready", "lo_ready", "l_done", "l_ready")]
        rows_kept = [sem(f"rows_kept{s}") for s in range(C)]
        block = begin()
        b_tp, b_l = g.bank[0:C], g.bank[C]
        at = lambda t: bass.ds(t * P, P)

        @block.sync
        def _(sp):
            sp.dma_start(gw[:], gate.rearrange("(k p) e -> p k e", p=P)).then_inc(gate_in, 16)
            if gate_b is not None:
                sp.dma_start(gb[:], gate_b.rearrange("(o e) -> o e", o=1)).then_inc(gate_in, 16)
            rows = rows_out.rearrange("(t p) d -> t p d", p=P)
            with sp.Fori(0, T // C) as i:
                for s in range(C):
                    t = C * i + s
                    sp.wait_ge(xn_ready, ONE + t + 1)
                    sp.dma_start(rows[bass.ds(t, 1), :, :].rearrange("t p d -> (t p) d"), xn[s][:]).then_inc(rows_kept[s], 16)
            for s in range(C):
                sp.wait_ge(rows_kept[s], ONE + 16 * (T // C))

        @block.vector
        def _(dve):
            if gate_b is None:
                nc.vector.memset(gb[:], 0.0)
            nc.vector.memset(ones[:], 1.0).then_inc(gb_set, 1)
            with dve.Fori(0, T // C) as i:
                for s in range(C):
                    t = C * i + s
                    dve.wait_ge(xnT_done, ONE + C * i)
                    dve.wait_ge(rows_kept[s], ONE + 16 * i)
                    nc.vector.tensor_scalar(xn[s][:], g.x[:, bass.ds(t, 1), :].rearrange("p o d -> p (o d)"),
                                            g.mean[:, bass.ds(t, 1)], g.rstd[:, bass.ds(t, 1)],
                                            ALU.subtract, ALU.mult).then_inc(xn_ready, 1)
                if xnT_parts is not None:
                    for s in range(C):
                        t = C * i + s
                        dve.wait_ge(hi_ready, ONE + t + 1)
                        nc.vector.tensor_tensor(xnT_parts[1][:, :, at(t)], xnT[s][:], xnT_parts[0][:, :, at(t)].bitcast(F32),
                                                ALU.subtract).then_inc(lo_ready, 1)

        @block.scalar
        def _(act):
            with act.Fori(0, T // C) as i:
                for s in range(C):
                    act.wait_ge(xnT_done, ONE + C * i + s + 1)
                    act.wait_ge(l_done, ONE + i)
                    if xnT_parts is not None:
                        act.wait_ge(lo_ready, ONE + C * i)
                    nc.scalar.activation(xnT[s][:], b_tp[s][:, 0:D].rearrange("p (k q) -> p k q", k=KD),
                                         ACT.Copy).then_inc(xnT_ready, 1)
                act.wait_ge(l_done, ONE + i + 1)
                nc.scalar.activation(logits[:, bass.ds(C * i, C), :], b_l[:, 0:C * E].rearrange("p (c e) -> p c e", c=C),
                                     ACT.Copy).then_inc(l_ready, 1)

        @block.gpsimd
        def _(pool):
            if xnT_parts is not None:
                with pool.Fori(0, T // C) as i:
                    for s in range(C):
                        t = C * i + s
                        pool.wait_ge(xnT_ready, ONE + t + 1)
                        nc.gpsimd.tensor_copy(xnT_parts[0][:, :, at(t)], xnT[s][:]).then_inc(hi_ready, 1)

        @block.tensor
        def _(pe):
            pe.wait_ge(gate_in, ONE + (16 if gate_b is None else 32))
            pe.wait_ge(gb_set, ONE + 1)
            with pe.Fori(0, T // C) as i:
                for s in range(C):
                    pe.wait_ge(xn_ready, ONE + C * i + s + 1)
                    pe.wait_ge(xnT_ready, ONE + C * i)
                    for k in range(KD):
                        last = nc.tensor.transpose(b_tp[s][:, P * k:P * (k + 1)], xn[s][:, P * k:P * (k + 1)], g.ident[:])
                    last.then_inc(xnT_done, 1)
                pe.wait_ge(l_ready, ONE + i)
                for s in range(C):
                    pe.wait_ge(xnT_ready, ONE + C * i + s + 1)
                    dst = b_l[:, E * s:E * (s + 1)]
                    nc.tensor.matmul(dst, ones[:], gb[:], start=True, stop=False)
                    for k in range(KD):
                        last = nc.tensor.matmul(dst, xnT[s][:, k, :], gw[:, k, :], start=False, stop=(k == KD - 1))
                last.then_inc(l_done, 1)


def top2_weights(nc, g, logits, taken, weight):
    E = logits.shape[2]
    with phase(nc) as (e, semaphore, begin):
        sb = lambda n, shape, dt=F32: e.enter_context(nc.sbuf_tensor(f"t2_{n}", shape, dt))
        sem = lambda n: semaphore(f"t2_{n}")
        order, row = sb("order", [P, E]), sb("row", [P, T])
        p, left, pick = [sb(n, [P, T, E]) for n in ("p", "left", "pick")]
        step, order_set, shifted, exp_ready = sem("step"), sem("order_set"), sem("shifted"), sem("exp_ready")
        block = begin()
        over = lambda a: a[:].unsqueeze(2).broadcast_to([P, T, E])

        @block.gpsimd
        def _(pool):
            nc.gpsimd.iota(order[:], pattern=[[-1, E]], base=E, channel_multiplier=0,
                           allow_small_or_imprecise_dtypes=True).then_inc(order_set, 1)

        @block.scalar
        def _(act):
            act.wait_ge(shifted, ONE + 1)
            nc.scalar.activation(p[:], p[:], ACT.Exp).then_inc(exp_ready, 1)

        @block.vector
        def _(dve):
            link = Chain(dve, step)
            link(nc.vector.tensor_reduce(row[:], logits[:], axis=AX.X, op=ALU.max))
            nc.vector.tensor_tensor(p[:], logits[:], over(row), ALU.subtract).then_inc(shifted, 1)
            dve.wait_ge(exp_ready, ONE + 1)
            link(nc.vector.tensor_reduce(row[:], p[:], axis=AX.X, op=ALU.add))
            link(nc.vector.reciprocal(row[:], row[:]))
            link(nc.vector.tensor_tensor(p[:], p[:], over(row), ALU.mult))
            dve.wait_ge(order_set, ONE + 1)
            link(nc.vector.tensor_copy(left[:], p[:]))
            for n in range(2):
                link(nc.vector.tensor_reduce(row[:], left[:], axis=AX.X, op=ALU.max))
                link(nc.vector.tensor_tensor(pick[:], left[:], over(row), ALU.is_equal))
                link(nc.vector.tensor_tensor(pick[:], pick[:], order[:].unsqueeze(1).broadcast_to([P, T, E]), ALU.mult))
                link(nc.vector.tensor_reduce(row[:], pick[:], axis=AX.X, op=ALU.max))
                link(nc.vector.tensor_tensor(taken[n][:], pick[:], over(row), ALU.is_equal))
                nc.vector.scalar_tensor_tensor(left[:], taken[n][:], -4.0, left[:], ALU.mult, ALU.add)
                link(nc.vector.tensor_tensor(pick[:], taken[n][:], p[:], ALU.mult))
                link(nc.vector.tensor_reduce(weight[n][:], pick[:], axis=AX.X, op=ALU.add))


def block_slots(nc, g, taken, slot, block_e, block_f):
    E, NB = taken[0].shape[2], block_e.shape[1]
    with phase(nc) as (e, semaphore, begin):
        sb = lambda n, shape, dt=F32: e.enter_context(nc.sbuf_tensor(f"bs_{n}", shape, dt))
        sem = lambda n: semaphore(f"bs_{n}")
        ones, earlier = sb("ones", [P, P]), sb("earlier", [P, P])
        number = sb("number", [P, NB])
        mask, tot = sb("mask", [P, T, E]), sb("tot", [P, T, E])
        run = [sb(f"run{k}", [P, T, E]) for k in range(2)]
        count_i, blocks_i = sb("count_i", [P, E], I32), sb("blocks_i", [P, E], I32)
        blocks, first = sb("blocks", [P, E]), sb("first", [P, E])
        ends = [sb(f"ends{k}", [P, E]) for k in range(2)]
        at, part, slot_f = sb("at", [P, T, E]), sb("part", [P, T, E]), sb("slot_f", [P, T])
        past = sb("past", [P, NB, E])
        step, const, consts_set, mask_ready, sums_done = [sem(n) for n in (
            "step", "const", "consts_set", "mask_ready", "sums_done")]
        b_before, b_tot = g.bank[0], g.bank[1]
        flat = lambda a: a[:].rearrange("p t e -> p (t e)")
        block = begin()

        @block.gpsimd
        def _(pool):
            link = Chain(pool, const)
            nc.gpsimd.iota(number[:], pattern=[[1, NB]], base=0, channel_multiplier=0, allow_small_or_imprecise_dtypes=True)
            nc.gpsimd.memset(ones[:], 1.0)
            link(nc.gpsimd.memset(earlier[:], 1.0))
            nc.gpsimd.affine_select(out=earlier[:], in_=earlier[:], compare_op=ALU.is_ge, fill=0.0, base=-1,
                                    pattern=[[1, P]], channel_multiplier=-1).then_inc(consts_set, 1)

        @block.tensor
        def _(pe):
            pe.wait_ge(consts_set, ONE + 1)
            pe.wait_ge(mask_ready, ONE + 1)
            nc.tensor.matmul(b_before[:, 0:T * E], earlier[:], flat(mask), start=True, stop=True)
            nc.tensor.matmul(b_tot[:, 0:T * E], ones[:], flat(mask), start=True, stop=True).then_inc(sums_done, 1)

        @block.vector
        def _(dve):
            link = Chain(dve, step)
            nc.vector.tensor_tensor(mask[:], taken[0][:], taken[1][:], ALU.add).then_inc(mask_ready, 1)
            dve.wait_ge(consts_set, ONE + 1)
            dve.wait_ge(sums_done, ONE + 1)
            nc.vector.tensor_copy(flat(tot), b_tot[:, 0:T * E])
            link(nc.vector.tensor_copy(flat(run[0]), b_tot[:, 0:T * E]))
            d, k = 1, 0
            while d < T:
                nc.vector.tensor_copy(run[1 - k][:, 0:d], run[k][:, 0:d])
                link(nc.vector.tensor_tensor(run[1 - k][:, d:T], run[k][:, d:T], run[k][:, 0:T - d], ALU.add))
                d, k = 2 * d, 1 - k
            link(nc.vector.tensor_scalar(count_i[:], run[k][:, T - 1], float(P - 1), None, ALU.add))
            link(nc.vector.tensor_scalar(blocks_i[:], count_i[:], P.bit_length() - 1, None, ALU.logical_shift_right))
            link(nc.vector.tensor_copy(blocks[:], blocks_i[:]))
            link(nc.vector.tensor_copy(ends[0][:], blocks[:]))
            d, m = 1, 0
            while d < E:
                nc.vector.tensor_copy(ends[1 - m][:, 0:d], ends[m][:, 0:d])
                link(nc.vector.tensor_tensor(ends[1 - m][:, d:E], ends[m][:, d:E], ends[m][:, 0:E - d], ALU.add))
                d, m = 2 * d, 1 - m
            link(nc.vector.tensor_tensor(first[:], ends[m][:], blocks[:], ALU.subtract))
            link(nc.vector.tensor_scalar(first[:], first[:], float(P), None, ALU.mult))
            link(nc.vector.tensor_tensor(at[:], run[k][:], tot[:], ALU.subtract))
            link(nc.vector.tensor_tensor(flat(at), flat(at), b_before[:, 0:T * E], ALU.add))
            link(nc.vector.tensor_tensor(at[:], at[:], first[:].unsqueeze(1).broadcast_to([P, T, E]), ALU.add))
            for n in range(2):
                link(nc.vector.tensor_tensor(part[:], at[:], taken[n][:], ALU.mult))
                link(nc.vector.tensor_reduce(slot_f[:], part[:], axis=AX.X, op=ALU.add))
                link(nc.vector.tensor_copy(slot[n][:], slot_f[:]))
            link(nc.vector.tensor_tensor(past[:], ends[m][:].unsqueeze(1).broadcast_to([P, NB, E]),
                                         number[:].unsqueeze(2).broadcast_to([P, NB, E]), ALU.is_le))
            link(nc.vector.tensor_reduce(block_f[:], past[:], axis=AX.X, op=ALU.add))
            link(nc.vector.tensor_scalar(block_f[:], block_f[:], float(E - 1), None, ALU.min))
            link(nc.vector.tensor_copy(block_e[:], block_f[:]))


def shared_experts(nc, g, xnT_parts, rows, sorted_rows, slot):
    ins = g.ins
    SH, _, H = ins["L0_ffn_sw1"].shape
    KH, C = H // P, 512
    NC, TC = N // C, C // P
    SL = 4
    PASSES = ((0, 0), (0, 1), (1, 0))
    with phase(nc) as (e, semaphore, begin):
        sb = lambda n, shape, dt=F32: e.enter_context(nc.sbuf_tensor(f"sh_{n}", shape, dt))
        sem = lambda n: semaphore(f"sh_{n}")
        F = KD * H
        w_f = [sb(f"w_f{s}", [P, F]) for s in range(2)]
        w1, w2 = [[sb(f"{n}_{p}", [P, SH, KD, H], F32R) for p in range(2)] for n in ("w1", "w2")]
        w3 = [sb(f"w3_{p}", [P, SH, KH, D], F32R) for p in range(2)]
        b_rows = sb("b_rows", [SH * KH, 2, P])
        b_cols = sb("b_cols", [P, 2, SH, KH])
        b3_f = sb("b3_f", [2, SH, D])
        b3_hi = sb("b3_hi", [2, SH, D], F32R)
        b3 = sb("b3", [2, SH, D], F32R)
        minus_row = sb("minus_row", [2, 1])
        ones_f, ones = sb("ones_f", [2, P]), sb("ones", [2, P], F32R)
        silu = [sb(f"silu{k}", [P, C]) for k in range(2)]
        glu_f = [sb(f"glu_f{k}", [P, C]) for k in range(2)]
        glu = [sb(f"glu_{p}", [P, KH, C], F32R) for p in range(2)]
        row = [sb(f"row{s}", [P, D]) for s in range(SL)]
        row_in = [sem(f"row_in{s}") for s in range(SL)]
        row_out = [semaphore(f"sh_row_out{s}", 0) for s in range(SL)]
        b_in, b3_in, bT_done, bT_ready, step, consts_set = [sem(n) for n in (
            "b_in", "b3_in", "bT_done", "bT_ready", "step", "consts_set")]
        w_in = [sem(f"w_in{s}") for s in range(2)]
        w_hi, w_ready = sem("w_hi"), sem("w_ready")
        p1_done, p2_done, silu_ready, glu_ready, hi_ready, lo_ready, y_done, y_added = [sem(n) for n in (
            "p1_done", "p2_done", "silu_ready", "glu_ready", "hi_ready", "lo_ready", "y_done", "y_added")]
        b_p1, b_p2, b_y = g.bank[0:2], g.bank[2:4], g.bank[4:8]
        block = begin()
        order = [(w, n) for n in range(SH) for w in (w1, w2, w3)]
        flat = lambda w, p, n: w[p][:, n].rearrange("p a b -> p (a b)")

        @block.sync
        def _(sp):
            sources = [(ins[f"L0_ffn_s{m}"][n], m) for n in range(SH) for m in ("w1", "w2", "w3")]

            def load(k):
                src, m = sources[k]
                rows_of = "(k p) h -> p k h"
                width = D if m == "w3" else H
                sp.dma_start(w_f[k % 2][:].rearrange("p (k h) -> p k h", h=width), src.rearrange(rows_of, p=P)).then_inc(w_in[k % 2], 16)

            load(0)
            load(1)
            for n, b in enumerate((ins["L0_ffn_sb1"], ins["L0_ffn_sb2"])):
                sp.dma_start(b_rows[:, n], b.rearrange("e (m p) -> (e m) p", p=P)).then_inc(b_in, 16)
            for h in range(2):
                sp.dma_start(b3_f[h:h + 1], ins["L0_ffn_sb3"].rearrange("(o n) d -> o n d", o=1)).then_inc(b3_in, 16)
            for k in range(2, len(sources)):
                sp.wait_ge(w_ready, ONE + k - 1)
                load(k)
            for t in range(T):
                s = t % SL
                if t >= SL:
                    sp.wait_ge(row_out[s], 32 * (t // SL))
                sp.dma_start(row[s][:], rows[P * t:P * (t + 1), :]).then_inc(row_in[s], 16)
            for s in range(SL):
                sp.wait_ge(row_out[s], 32 * (T // SL))

        @block.gpsimd
        def _(pool):
            nc.gpsimd.iota(minus_row[:], pattern=[[0, 1]], base=0, channel_multiplier=-1, allow_small_or_imprecise_dtypes=True)
            nc.gpsimd.memset(ones_f[:], 1.0).then_inc(consts_set, 1)
            for k, (w, n) in enumerate(order):
                pool.wait_ge(w_hi, ONE + k + 1)
                nc.gpsimd.tensor_tensor(flat(w, 1, n), w_f[k % 2][:], flat(w, 0, n).bitcast(F32), ALU.subtract).then_inc(w_ready, 1)
            for t in range(T):
                s = t % SL
                pool.wait_ge(row_in[s], ONE + 16 * (t // SL + 1))
                for k in range(2):
                    nc.gpsimd.indirect_dma_start(out=sorted_rows, in_=row[s][:], in_offset=None,
                                                 out_offset=bass.IndirectOffsetOnAxis(ap=slot[k][:, t:t + 1], axis=0)
                                                 ).then_inc(row_out[s], 16)

        @block.vector
        def _(dve):
            link = Chain(dve, step)
            dve.wait_ge(consts_set, ONE + 1)
            dve.wait_ge(b3_in, ONE + 32)
            nc.vector.tensor_copy(ones[:], ones_f[:])
            link(nc.vector.tensor_copy(b3_hi[:], b3_f[:]))
            link(nc.vector.scalar_tensor_tensor(b3[:], b3_hi[:].bitcast(F32), minus_row[:, 0:1], b3_f[:], ALU.mult, ALU.add))
            dve.wait_ge(bT_ready, ONE + 1)
            for n in range(SH):
                with dve.Fori(0, NC) as c:
                    it = n * NC + c
                    for m in range(KH):
                        dve.wait_ge(silu_ready, ONE + it * KH + m + 1)
                        dve.wait_ge(p2_done, ONE + it * KH + m + 1)
                        nc.vector.scalar_tensor_tensor(glu_f[m % 2][:], b_p2[m % 2][:], b_cols[:, 1, n, m:m + 1], silu[m % 2][:],
                                                       ALU.add, ALU.mult).then_inc(glu_ready, 1)
                        dve.wait_ge(hi_ready, ONE + it * KH + m + 1)
                        dve.wait_ge(y_done, ONE + it * TC)
                        nc.vector.tensor_tensor(glu[1][:, m, :], glu_f[m % 2][:], glu[0][:, m, :].bitcast(F32),
                                                ALU.subtract).then_inc(lo_ready, 1)
                    for q in range(TC):
                        t = c * TC + q
                        xt = g.x[:, bass.ds(t, 1), :].rearrange("p o d -> p (o d)")
                        dve.wait_ge(y_done, ONE + it * TC + q + 1)
                        dve.wait_ge(y_added, ONE + it * TC)
                        nc.vector.scalar_tensor_tensor(xt, b_y[q][:, 0:D], 1.0 / SH, xt, ALU.mult, ALU.add).then_inc(y_added, 1)

        @block.scalar
        def _(act):
            act.wait_ge(bT_done, ONE + 1)
            nc.scalar.activation(b_cols[:].rearrange("p n e m -> p n (e m)"),
                                 b_p1[0][:, 0:2 * SH * KH].rearrange("p (n r) -> p n r", n=2), ACT.Copy).then_inc(bT_ready, 1)
            for k, (w, n) in enumerate(order):
                act.wait_ge(w_in[k % 2], ONE + 16 * (k // 2 + 1))
                nc.scalar.activation(flat(w, 0, n), w_f[k % 2][:], ACT.Copy).then_inc(w_hi, 1)
            act.wait_ge(bT_ready, ONE + 1)
            for n in range(SH):
                with act.Fori(0, NC) as c:
                    it = n * NC + c

                    def rounded(m):
                        act.wait_ge(glu_ready, ONE + it * KH + m + 1)
                        act.wait_ge(y_done, ONE + it * TC)
                        nc.scalar.activation(glu[0][:, m, :], glu_f[m % 2][:], ACT.Copy).then_inc(hi_ready, 1)

                    for m in range(KH):
                        act.wait_ge(p1_done, ONE + it * KH + m + 1)
                        if m >= 2:
                            act.wait_ge(glu_ready, ONE + it * KH + m - 1)
                        else:
                            act.wait_ge(glu_ready, ONE + it * KH)
                        nc.scalar.activation(silu[m % 2][:], b_p1[m % 2][:], ACT.Silu, bias=b_cols[:, 0, n, m:m + 1]).then_inc(silu_ready, 1)
                        rounded(m)

        @block.tensor
        def _(pe):
            pe.wait_ge(b_in, ONE + 16 * 2)
            for n in range(2):
                last = nc.tensor.transpose(b_p1[0][:, n * SH * KH:(n + 1) * SH * KH], b_rows[:, n, :], g.ident[0:SH * KH, 0:SH * KH])
            last.then_inc(bT_done, 1)
            pe.wait_ge(bT_ready, ONE + 1)
            pe.wait_ge(step, ONE + 2)
            for n in range(SH):
                pe.wait_ge(w_ready, ONE + 3 * (n + 1))
                with pe.Fori(0, NC) as c:
                    it = n * NC + c
                    for m in range(KH):
                        for w, bank, done, free in ((w1, b_p1, p1_done, silu_ready), (w2, b_p2, p2_done, glu_ready)):
                            if m >= 2:
                                pe.wait_ge(free, ONE + it * KH + m - 1)
                            else:
                                pe.wait_ge(free, ONE + it * KH)
                            for k in range(KD):
                                for a, b in PASSES:
                                    last = nc.tensor.matmul(bank[m % 2][:], w[a][:, n, k, P * m:P * (m + 1)],
                                                            xnT_parts[b][:, k, bass.ds(c * C, C)],
                                                            start=(k == 0 and a + b == 0), stop=(k == KD - 1 and a == 1))
                            last.then_inc(done, 1)
                    pe.wait_ge(y_added, ONE + it * TC)
                    for q in range(TC):
                        nc.tensor.matmul(b_y[q][:, 0:D], ones[:], b3[:, n, :], start=True, stop=False)
                    for m in range(KH):
                        pe.wait_ge(lo_ready, ONE + it * KH + m + 1)
                        for q in range(TC):
                            for a, b in PASSES:
                                last = nc.tensor.matmul(b_y[q][:, 0:D], glu[a][:, m, P * q:P * (q + 1)], w3[b][:, n, m, :],
                                                        start=False, stop=(m == KH - 1 and a == 1))
                            if m == KH - 1:
                                last.then_inc(y_done, 1)


def routed_blocks(nc, g, sorted_rows, sorted_out, block_e, block_f):
    ins = g.ins
    E, _, H = ins["L0_ffn_rw1"].shape
    KH, NB = H // P, block_e.shape[1]
    with phase(nc) as (e, semaphore, begin):
        sb = lambda n, shape, dt=F32: e.enter_context(nc.sbuf_tensor(f"rb_{n}", shape, dt))
        sem = lambda n: semaphore(f"rb_{n}")
        w1, w2 = sb("w1", [P, E, KD, H]), sb("w2", [P, E, KD, H])
        w3 = sb("w3", [P, E, KH, D])
        b_all = sb("b_all", [2 * E, 2 * H + D])
        b_hi = sb("b_hi", [2 * E, 2 * H + D], F32R)
        b_parts = sb("b_parts", [2 * E, 2 * H + D], F32R)
        rest = sb("rest", [2 * E, 1])
        row_e, row_at = sb("row_e", [2 * E, P]), sb("row_at", [2 * E, P])
        own = [sb(f"own{s}", [2 * E, P], F32R) for s in range(2)]
        own_out = sb("own_out", [2 * E, P], F32R)
        xb = [sb(f"xb{s}", [P, D]) for s in range(2)]
        xT = [sb(f"xT{s}", [P, KD, P]) for s in range(2)]
        silu = sb("silu", [P, H])
        glu, gluT = sb("glu", [P, H]), sb("gluT", [P, KH, P])
        yb = [sb(f"yb{s}", [P, D]) for s in range(2)]
        w_in, b_in, step, rest_set = sem("w_in"), sem("b_in"), sem("step"), sem("rest_set")
        xb_in, kept = [semaphore(f"rb_xb_in{s}", 0) for s in range(2)], [sem(f"kept{s}") for s in range(2)]
        xT_done, xT_ready, own_ready, p1_done, p2_done = [sem(n) for n in (
            "xT_done", "xT_ready", "own_ready", "p1_done", "p2_done")]
        silu_ready, glu_ready, gluT_done, gluT_ready, y_done, y_ready = [sem(n) for n in (
            "silu_ready", "glu_ready", "gluT_done", "gluT_ready", "y_done", "y_ready")]
        b_x, b_p1, b_p2, b_g, b_y = g.bank[0:5]
        block = begin()

        @block.sync
        def _(sp):
            for h in range(2):
                for at, b in ((0, ins["L0_ffn_rb1"]), (H, ins["L0_ffn_rb2"]), (2 * H, ins["L0_ffn_rb3"])):
                    sp.dma_start(b_all[E * h:E * (h + 1), at:at + b.shape[1]], b).then_inc(b_in, 16)
            dst = sorted_out.rearrange("(j p) d -> j p d", p=P)
            sp.dma_start(w1[:], ins["L0_ffn_rw1"].rearrange("e (k p) h -> p e k h", p=P)).then_inc(w_in, 16)
            sp.dma_start(w2[:], ins["L0_ffn_rw2"].rearrange("e (k p) h -> p e k h", p=P)).then_inc(w_in, 16)
            sp.dma_start(w3[:], ins["L0_ffn_rw3"].rearrange("e (k p) d -> p e k d", p=P)).then_inc(w_in, 16)
            with sp.Fori(0, NB // 2) as i:
                for s in range(2):
                    j = 2 * i + s
                    sp.wait_ge(y_ready, ONE + j + 1)
                    sp.dma_start(dst[bass.ds(j, 1), :, :].rearrange("j p d -> (j p) d"), yb[s][:]).then_inc(kept[s], 16)
            for s in range(2):
                sp.wait_ge(kept[s], ONE + 16 * (NB // 2))

        @block.gpsimd
        def _(pool):
            io = dict(allow_small_or_imprecise_dtypes=True)
            nc.gpsimd.iota(rest[:], pattern=[[0, 1]], base=0, channel_multiplier=1, **io)
            nc.gpsimd.iota(row_at[:], pattern=[[0, P]], base=0, channel_multiplier=1, **io).then_inc(rest_set, 1)
            src = sorted_rows.rearrange("(j p) d -> j p d", p=P)
            for s in range(2):
                pool.dma_start(xb[s][:], src[s]).then_inc(xb_in[s], 16)
            with pool.Fori(0, NB // 2 - 1) as i:
                for s in range(2):
                    j = 2 * i + s
                    pool.wait_ge(xT_done, ONE + j + 1)
                    pool.dma_start(xb[s][:], src[bass.ds(j + 2, 1), :, :].rearrange("j p d -> (j p) d")).then_inc(xb_in[s], 16)

        @block.vector
        def _(dve):
            link = Chain(dve, step)
            dve.wait_ge(rest_set, ONE + 1)
            link(nc.vector.tensor_scalar(rest[:], rest[:], float(E), -1.0, ALU.is_ge, ALU.mult))
            link(nc.vector.tensor_scalar(row_e[:], row_at[:], float(E), float(-E), ALU.is_ge, ALU.mult))
            link(nc.vector.tensor_tensor(row_e[:], row_e[:], row_at[:], ALU.add))
            dve.wait_ge(b_in, ONE + 16 * 6)
            link(nc.vector.tensor_copy(b_hi[:], b_all[:]))
            link(nc.vector.scalar_tensor_tensor(b_parts[:], b_hi[:].bitcast(F32), rest[:, 0:1], b_all[:], ALU.mult, ALU.add))

            def rows_in(s, j):
                dve.wait_ge(xT_done, ONE + j + 1)
                dve.wait_ge(p2_done, ONE + j - 1)
                nc.vector.tensor_copy(xT[s][:], b_x[:, 0:D].rearrange("p (k q) -> p k q", k=KD)).then_inc(xT_ready, 1)
                nc.vector.tensor_scalar(own[s][:], row_e[:], block_f[0:2 * E, bass.ds(j, 1)], None, ALU.is_equal).then_inc(own_ready, 1)

            def gated(j):
                dve.wait_ge(silu_ready, ONE + j + 1)
                dve.wait_ge(p2_done, ONE + j + 1)
                dve.wait_ge(gluT_done, ONE + j)
                nc.vector.tensor_tensor(glu[:], b_p2[:], silu[:], ALU.mult).then_inc(glu_ready, 1)

            def gated_T(j):
                dve.wait_ge(gluT_done, ONE + j + 1)
                dve.wait_ge(y_done, ONE + j)
                nc.vector.tensor_scalar(own_out[:], row_e[:], block_f[0:2 * E, bass.ds(j, 1)], None, ALU.is_equal)
                nc.vector.tensor_copy(gluT[:], b_g[:].rearrange("p (m q) -> p m q", m=KH)).then_inc(gluT_ready, 1)

            def out_rows(s, j, used):
                dve.wait_ge(y_done, ONE + j + 1)
                dve.wait_ge(kept[s], ONE + 16 * used)
                nc.vector.tensor_copy(yb[s][:], b_y[:, 0:D]).then_inc(y_ready, 1)

            rows_in(0, 0)
            rows_in(1, 1)
            gated(0)
            with dve.Fori(0, NB // 2 - 1) as i:
                for s in range(2):
                    j = 2 * i + s + 1
                    gated_T(j - 1)
                    rows_in(s, j + 1)
                    gated(j)
                    out_rows(s, j - 1, i)
            gated_T(NB - 2)
            gated(NB - 1)
            out_rows(0, NB - 2, NB // 2 - 1)
            gated_T(NB - 1)
            out_rows(1, NB - 1, NB // 2 - 1)

        @block.scalar
        def _(act):
            with act.Fori(0, NB) as j:
                act.wait_ge(p1_done, ONE + j + 1)
                act.wait_ge(glu_ready, ONE + j)
                nc.scalar.activation(silu[:], b_p1[:], ACT.Silu).then_inc(silu_ready, 1)

        @block.tensor
        def _(pe):
            pe.wait_ge(w_in, ONE + 48)

            def expert(j):
                return pe.value_load(block_e[0:1, bass.ds(j, 1)], min_val=0, max_val=E - 1)

            def rows_T(s, j, round_):
                pe.wait_ge(xb_in[s], 16 * (round_ + 1))
                pe.wait_ge(xT_ready, ONE + j)
                for k in range(KD):
                    last = nc.tensor.transpose(b_x[:, P * k:P * (k + 1)], xb[s][:, P * k:P * (k + 1)], g.ident[:])
                last.then_inc(xT_done, 1)

            def hidden(s, n, w, at, bank, done):
                flat = w[:].rearrange("p e k h -> p (e k) h")
                nc.tensor.matmul(bank[:], own[s][:], b_parts[:, H * at:H * (at + 1)], start=True, stop=False)
                for k in range(KD):
                    last = nc.tensor.matmul(bank[:], xT[s][:, k, :], flat[:, bass.ds(n * KD + k, 1), :].rearrange("p o h -> p (o h)"),
                                            start=False, stop=(k == KD - 1))
                last.then_inc(done, 1)

            def first(s, j, n):
                pe.wait_ge(own_ready, ONE + j + 1)
                pe.wait_ge(silu_ready, ONE + j)
                hidden(s, n, w1, 0, b_p1, p1_done)

            def second(s, j, n):
                pe.wait_ge(glu_ready, ONE + j)
                hidden(s, n, w2, 1, b_p2, p2_done)

            def gated_T(j):
                pe.wait_ge(glu_ready, ONE + j + 1)
                pe.wait_ge(gluT_ready, ONE + j)
                for m in range(KH):
                    last = nc.tensor.transpose(b_g[:, P * m:P * (m + 1)], glu[:, P * m:P * (m + 1)], g.ident[:])
                last.then_inc(gluT_done, 1)

            def down(j):
                n = expert(j)
                pe.wait_ge(gluT_ready, ONE + j + 1)
                pe.wait_ge(y_ready, ONE + j)
                flat = w3[:].rearrange("p e m d -> p (e m) d")
                nc.tensor.matmul(b_y[:, 0:D], own_out[:], b_parts[:, 2 * H:], start=True, stop=False)
                for m in range(KH):
                    last = nc.tensor.matmul(b_y[:, 0:D], gluT[:, m, :], flat[:, bass.ds(n * KH + m, 1), :].rearrange("p o d -> p (o d)"),
                                            start=False, stop=(m == KH - 1))
                last.then_inc(y_done, 1)

            rows_T(0, 0, 0)
            n = expert(0)
            first(0, 0, n)
            second(0, 0, n)
            rows_T(1, 1, 0)
            with pe.Fori(0, NB // 2 - 1) as i:
                for s in range(2):
                    j = 2 * i + s + 1
                    n = expert(j)
                    first(1 - s, j, n)
                    gated_T(j - 1)
                    second(1 - s, j, n)
                    rows_T(s, j + 1, i + 1)
                    down(j - 1)
            n = expert(NB - 1)
            first(1, NB - 1, n)
            gated_T(NB - 2)
            second(1, NB - 1, n)
            down(NB - 2)
            gated_T(NB - 1)
            down(NB - 1)


def routed_sum(nc, g, sorted_out, slot, weight):
    SL = 8
    with phase(nc) as (e, semaphore, begin):
        sem = lambda n: semaphore(f"rs_{n}")
        got = [e.enter_context(nc.sbuf_tensor(f"rs_got{s}", [P, D], F32)) for s in range(SL)]
        got_in = [semaphore(f"rs_got_in{s}", 0) for s in range(SL)]
        x_ready, stats_ready = sem("x_ready"), sem("stats_ready")
        block = begin()

        @block.gpsimd
        def _(pool):
            for n in range(2 * T):
                t, k = n // 2, n % 2
                if n >= SL:
                    pool.wait_ge(x_ready, ONE + n - SL + 1)
                nc.gpsimd.indirect_dma_start(out=got[n % SL][:], out_offset=None, in_=sorted_out,
                                             in_offset=bass.IndirectOffsetOnAxis(ap=slot[k][:, t:t + 1], axis=0)
                                             ).then_inc(got_in[n % SL], 16)

        @block.vector
        def _(dve):
            with dve.Fori(0, 2 * T // SL) as i:
                for s in range(SL):
                    t, k = i * (SL // 2) + s // 2, s % 2
                    xt = g.x[:, bass.ds(t, 1), :].rearrange("p o d -> p (o d)")
                    dve.wait_ge(got_in[s], 16 * i + 16)
                    dve.wait_ge(x_ready, ONE + SL * i + s)
                    nc.vector.scalar_tensor_tensor(xt, got[s][:], weight[k][:, bass.ds(t, 1)], xt,
                                                   ALU.mult, ALU.add).then_inc(x_ready, 1)
                    if k:
                        dve.wait_ge(x_ready, ONE + SL * i + s + 1)
                        nc.vector.bn_stats(g.stats[:, bass.ds(t, 1), :], g.x[:, bass.ds(t, 1), :]).then_inc(stats_ready, 1)


def mixture0(nc, g, sorted_rows):
    ins = g.ins
    E = ins["L0_ffn_rw1"].shape[0]
    NB = sorted_rows.shape[0] // P
    rows = nc.dram_tensor("normalised_rows", [N, D], F32, kind="Internal").ap()
    sorted_out = nc.dram_tensor("sorted_out", [NB * P, D], F32, kind="Internal").ap()
    with ExitStack() as e:
        sb = lambda n, shape, dt=F32: e.enter_context(nc.sbuf_tensor(f"m0_{n}", shape, dt))
        slot, weight = [sb(f"slot{k}", [P, T], U32) for k in range(2)], [sb(f"weight{k}", [P, T]) for k in range(2)]
        block_e, block_f = sb("block_e", [P, NB], I32), sb("block_f", [P, NB])
        with ExitStack() as e:
            xnT_parts = [sb(f"xnT_{part}", [P, KD, N], F32R) for part in ("rounded", "rest")]
            logits = sb("logits", [P, T, E])
            taken = [sb(f"taken{k}", [P, T, E]) for k in range(2)]
            normalised_tiles(nc, g, "np0", ins["L0_ffn_gate_w"], ins["L0_ffn_gate_b"], logits, rows, xnT_parts)
            top2_weights(nc, g, logits, taken, weight)
            block_slots(nc, g, taken, slot, block_e, block_f)
            shared_experts(nc, g, xnT_parts, rows, sorted_rows, slot)
        routed_blocks(nc, g, sorted_rows, sorted_out, block_e, block_f)
        routed_sum(nc, g, sorted_out, slot, weight)


GT = S * D // NH // D
NG = 2 * P // GT
PC = D // DH
L = GT * PC
A = P // GT
QT = L // P
BL = 32
ST = 3 * BL
NP = T // 2


def project_groups(nc, g, parts, values, x_kept, qs, ks, nmax, tile_rows):
    ins = g.ins
    with phase(nc) as (e, semaphore, begin):
        sb = lambda n, shape, dt=F32: e.enter_context(nc.sbuf_tensor(f"pg_{n}", shape, dt))
        sem = lambda n: semaphore(f"pg_{n}")
        wq, wk, wv = [sb(n, [P, KD, D]) for n in ("wq", "wk", "wv")]
        b_qk = sb("b_qk", [P, 2, KD])
        bv = sb("bv", [P, QT, DH])
        bo = sb("bo", [P, D])
        xn = [[sb(f"xn{s}{h}", [P, D]) for h in range(2)] for s in range(2)]
        xnT = [sb(f"xnT{s}", [P, KD, 2 * P]) for s in range(2)]
        hi = [[sb(f"hi{s}{n}", [P, KD, 2 * P], F32R) for n in range(2)] for s in range(2)]
        lo = [[sb(f"lo{s}{n}", [P, KD, 2 * P], F32R) for n in range(2)] for s in range(2)]
        v = [sb(f"v{s}", [P, NG, QT, BL]) for s in range(2)]
        w_in, b_in, v_zero, v_one, stack_zero, rows_set = [sem(n) for n in (
            "w_in", "b_in", "v_zero", "v_one", "stack_zero", "rows_set")]
        xn_ready, xnT_done, xnT_ready, qk_done, hi_ready, lo_ready, v_done, v_ready, xn_bo_ready = [sem(n) for n in (
            "xn_ready", "xnT_done", "xnT_ready", "qk_done", "hi_ready", "lo_ready", "v_done", "v_ready", "xn_bo_ready")]
        x_out, parts_out, v_out = [[sem(f"{n}{s}") for s in range(2)] for n in ("x_out", "parts_out", "v_out")]
        b_t, b_q, b_k, b_v = [g.bank[2 * n:2 * n + 2] for n in range(4)]
        block = begin()
        W_IN, B_IN, PARTS = 16 * 3, 16 * (2 * KD + A + 1), 16 * 4

        @block.sync
        def _(sp):
            for w, src in ((wq, ins["L1_attn_wq"]), (wk, ins["L1_attn_wk"]), (wv, ins["L1_attn_wv"])):
                sp.dma_start(w[:], src.rearrange("(k p) n -> p k n", p=P)).then_inc(w_in, 16)
            for n, src in enumerate((ins["L1_attn_bq"], ins["L1_attn_bk"])):
                for k in range(KD):
                    sp.dma_start(b_qk[:, n, k:k + 1], src[P * k:P * (k + 1)].rearrange("(p o) -> p o", o=1)).then_inc(b_in, 16)
            bv_parts = ins["L1_attn_bv"].rearrange("(o q a d) -> a o q d", o=1, a=A, d=DH)
            for a in range(A):
                sp.dma_start(bv[a * GT:(a + 1) * GT], bv_parts[a].broadcast_to([GT, QT, DH])).then_inc(b_in, 16)
            sp.dma_start(bo[:], ins["L1_attn_bo"].rearrange("(o n) -> o n", o=1).broadcast_to([P, D])).then_inc(b_in, 16)
            x_dst = x_kept.rearrange("(i s p) d -> i p s d", s=2, p=P)
            with sp.Fori(0, NP // 2) as r:
                for s in range(2):
                    i = 2 * r + s
                    sp.wait_ge(xn_bo_ready, ONE + 4 * r)
                    sp.dma_start(x_dst[bass.ds(i, 1)].rearrange("i p s d -> (i p) s d"), g.x[:, bass.ds(2 * i, 2), :]).then_inc(x_out[s], 16)
                for s in range(2):
                    i = 2 * r + s
                    for n in range(2):
                        for part, (tile, ready) in enumerate(((hi, hi_ready), (lo, lo_ready))):
                            sp.wait_ge(ready, ONE + 4 * i + 2 * n + 2)
                            dst = parts[n][part].rearrange("i (m p) t -> i p m t", m=KD)
                            sp.dma_start(dst[bass.ds(i, 1)].rearrange("i p m t -> (i p) m t"),
                                         tile[s][n][:].bitcast(F32)).then_inc(parts_out[s], 16)
                    sp.wait_ge(v_ready, ONE + i + 1)
                    sp.dma_start(values[bass.ds(i, 1)].rearrange("i p f -> (i p) f"),
                                 v[s][:].rearrange("p n q r -> p (n q r)")).then_inc(v_out[s], 16)
            for s in range(2):
                sp.wait_ge(x_out[s], ONE + 16 * (NP // 2))
                sp.wait_ge(parts_out[s], ONE + PARTS * (NP // 2))
                sp.wait_ge(v_out[s], ONE + 16 * (NP // 2))

        @block.gpsimd
        def _(pool):
            for s in range(2):
                nc.gpsimd.memset(v[s][:], 0.0).then_inc(v_zero, 1)
            pool.wait_ge(v_zero, ONE + 2)
            for s in range(2):
                nc.gpsimd.memset(v[s][:, :, :, DH:DH + 1], 1.0).then_inc(v_one, 1)
            nc.gpsimd.memset(nmax[:], 0.0)
            nc.gpsimd.memset(tile_rows[:], 0.0).then_inc(rows_set, 1)
            pool.wait_ge(rows_set, ONE + 1)
            pool.wait_ge(v_one, ONE + 2)
            nc.gpsimd.affine_select(out=tile_rows[ST:P], in_=tile_rows[ST:P], compare_op=ALU.not_equal, fill=1.0, base=0,
                                    pattern=[[-1, QT], [0, P]], channel_multiplier=1).then_inc(rows_set, 1)
            pool.wait_ge(rows_set, ONE + 2)
            pool.wait_ge(b_in, ONE + B_IN)
            with pool.Fori(0, NP // 2) as r:
                for s in range(2):
                    i = 2 * r + s
                    pool.wait_ge(x_out[s], ONE + 16 * r + 16)
                    for h in range(2):
                        pool.wait_ge(xn_ready, ONE + 2 * i + h + 1)
                        nc.gpsimd.tensor_tensor(g.x[:, bass.ds(2 * i + h, 1), :].rearrange("p o d -> p (o d)"),
                                                xn[s][h][:], bo[:], ALU.add).then_inc(xn_bo_ready, 1)
            for a in range(3):
                nc.gpsimd.memset(qs[a][0:ST].bitcast(F32), 0.0)
                nc.gpsimd.memset(ks[a][0:ST].bitcast(F32), 0.0).then_inc(stack_zero, 1)

        @block.vector
        def _(dve):
            for a in range(3):
                nc.vector.memset(ks[a][ST:P].bitcast(F32), 1.0)
            dve.wait_ge(b_in, ONE + B_IN)
            dve.wait_ge(v_one, ONE + 2)
            with dve.Fori(0, NP // 2) as r:
                for s in range(2):
                    i = 2 * r + s
                    for h in range(2):
                        t = 2 * i + h
                        dve.wait_ge(xnT_done, ONE + 2 * r)
                        dve.wait_ge(xn_bo_ready, ONE + 4 * r)
                        nc.vector.tensor_scalar(xn[s][h][:], g.x[:, bass.ds(t, 1), :].rearrange("p o d -> p (o d)"),
                                                g.mean[:, bass.ds(t, 1)], g.rstd[:, bass.ds(t, 1)],
                                                ALU.subtract, ALU.mult).then_inc(xn_ready, 1)
                for s in range(2):
                    i = 2 * r + s
                    for n in range(2):
                        for m in range(KD):
                            dve.wait_ge(hi_ready, ONE + 4 * i + 2 * n + 2)
                            dve.wait_ge(parts_out[s], ONE + PARTS * r)
                            nc.vector.scalar_tensor_tensor(lo[s][n][:, m], (b_q, b_k)[n][s][:, 2 * P * m:2 * P * (m + 1)],
                                                           b_qk[:, n, m:m + 1], hi[s][n][:, m].bitcast(F32),
                                                           ALU.add, ALU.subtract).then_inc(lo_ready, 1)
                    dve.wait_ge(v_done, ONE + i + 1)
                    dve.wait_ge(v_out[s], ONE + 16 * r)
                    nc.vector.tensor_tensor(v[s][:, :, :, 0:DH], b_v[s][:].rearrange("p (n q d) -> p n q d", n=NG, d=DH),
                                            bv[:].unsqueeze(1).broadcast_to([P, NG, QT, DH]), ALU.add).then_inc(v_ready, 1)

        @block.scalar
        def _(act):
            act.wait_ge(b_in, ONE + B_IN)
            with act.Fori(0, NP // 2) as r:
                for s in range(2):
                    i = 2 * r + s
                    act.wait_ge(xnT_done, ONE + i + 1)
                    act.wait_ge(v_done, ONE + 2 * r)
                    nc.scalar.activation(xnT[s][:].rearrange("p k (h q) -> p h k q", h=2),
                                         b_t[s][:].rearrange("p (h k q) -> p h k q", h=2, k=KD), ACT.Identity).then_inc(xnT_ready, 1)
                for s in range(2):
                    i = 2 * r + s
                    for n in range(2):
                        act.wait_ge(qk_done, ONE + 2 * i + n + 1)
                        act.wait_ge(parts_out[s], ONE + PARTS * r)
                        for m in range(KD):
                            nc.scalar.activation(hi[s][n][:, m], (b_q, b_k)[n][s][:, 2 * P * m:2 * P * (m + 1)], ACT.Identity,
                                                 bias=b_qk[:, n, m:m + 1]).then_inc(hi_ready, 1)

        @block.tensor
        def _(pe):
            pe.wait_ge(w_in, ONE + W_IN)
            with pe.Fori(0, NP // 2) as r:
                for s in range(2):
                    i = 2 * r + s
                    pe.wait_ge(xn_ready, ONE + 2 * i + 2)
                    pe.wait_ge(xnT_ready, ONE + 2 * r)
                    for h in range(2):
                        for k in range(KD):
                            last = nc.tensor.transpose(b_t[s][:, P * (KD * h + k):P * (KD * h + k + 1)],
                                                       xn[s][h][:, P * k:P * (k + 1)], g.ident[:])
                    last.then_inc(xnT_done, 1)
                for s in range(2):
                    i = 2 * r + s
                    pe.wait_ge(xnT_ready, ONE + i + 1)
                    pe.wait_ge(lo_ready, ONE + 8 * r)
                    for n, w in enumerate((wq, wk)):
                        for m in range(KD):
                            for k in range(KD):
                                last = nc.tensor.matmul((b_q, b_k)[n][s][:, 2 * P * m:2 * P * (m + 1)], w[:, k, P * m:P * (m + 1)],
                                                        xnT[s][:, k, :], start=(k == 0), stop=(k == KD - 1))
                        last.then_inc(qk_done, 1)
                    pe.wait_ge(v_ready, ONE + 2 * r)
                    for n in range(NG):
                        for a in range(A):
                            for k in range(KD):
                                cols = wv[:, k, :].rearrange("p (q a d) -> p a q d", a=A, d=DH)[:, a]
                                last = nc.tensor.matmul(b_v[s][GT * a:GT * (a + 1), P * n:P * (n + 1)],
                                                        xnT[s][:, k, GT * n:GT * (n + 1)], cols,
                                                        start=(k == 0), stop=(k == KD - 1))
                    last.then_inc(v_done, 1)


def group_attention(nc, g, parts, values, qs, ks, nmax, tile_rows):
    ins = g.ins
    HALF = 512
    LAG = 4
    U = NG * QT
    HU = 2 * U
    SETS = 3
    NS = HU // NG
    SLOTS = 3

    def step_uses(c):
        uses = []
        for u in range(0, U, 2):
            if u == 2 and 1 <= c <= NP:
                uses.append(("maxima", NG - 1, u))
            if u % QT == 2 and u > QT and c < NP:
                uses.append(("maxima", u // QT - 1, u))
            for at, use in ((LAG + 8, ("context", 0)), (LAG + 12, ("contextT", 0)),
                            (LAG + 16, ("project", 0)), (LAG + 20, ("project", 1))):
                if u == at and c >= 2:
                    uses.append((*use, u))
            if c < NP:
                uses += [("scores", u, u), ("scores", u + 1, u + 1)]
        return uses

    FULL = len(step_uses(2))
    FIRST = [0, len(step_uses(0)), len(step_uses(0)) + len(step_uses(1))]

    def uses_before(c):
        if c <= 2:
            return FIRST[c]
        return FIRST[2] + sum(len(step_uses(n)) for n in range(2, c))

    def use_at(c, kind, arg):
        return uses_before(c) + [(k, a) for k, a, _ in step_uses(c)].index((kind, arg))

    with phase(nc) as (e, semaphore, begin):
        sb = lambda n, shape, dt=F32: e.enter_context(nc.sbuf_tensor(f"ga_{n}", shape, dt))
        sem = lambda n: semaphore(f"ga_{n}")
        wo = sb("wo", [P, A, D])
        v = [sb(f"v{a}", [P, NG, QT, BL]) for a in range(SLOTS)]
        probT = [[sb(f"probT{k}{n}", [P, HALF]) for n in range(NG)] for k in range(SETS)]
        o = sb("o", [P, L])
        max_rows = sb("max_rows", [P, NG, P])
        rsum = sb("rsum", [P, QT, NG])
        ctxn = sb("ctxn", [P, NG, QT, DH])
        ctxT = sb("ctxT", [P, 2, A, P])
        w_in = sem("w_in")
        qk_in, v_in = [sem(f"qk_in{a}") for a in range(SLOTS)], [sem(f"v_in{a}") for a in range(SLOTS)]
        use_done, use_read, sT_done, exp_ready, pv_done, o_ready = [sem(n) for n in (
            "use_done", "use_read", "sT_done", "exp_ready", "pv_done", "o_ready")]
        fold_ready, rsum_ready, stats_ready = sem("fold_ready"), sem("rsum_ready"), sem("stats_ready")
        b_s, b_t, b_o = g.bank2[0:2], g.bank[4:6], g.bank2[3]
        block = begin()

        def steps(eng, step):
            for c in range(2):
                step(0, c)
            with eng.Fori(0, (NP - 2) // SLOTS) as r:
                for c in range(2, 2 + SLOTS):
                    step(r, c)
            for c in range(2 + (NP - 2) // SLOTS * SLOTS, NP + 2):
                step(0, c)

        def back_units(c):
            return [(U - LAG + u, c - 2) if u < LAG else (u - LAG, c - 1) for u in range(U)]

        @block.sync
        def _(sp):
            wo_rows = ins["L1_attn_wo"].rearrange("(q a d) n -> q d a n", a=A, d=DH)
            for q in range(QT):
                sp.dma_start(wo[q * DH:(q + 1) * DH], wo_rows[q]).then_inc(w_in, 16)

            def load(r, c):
                i, a = SLOTS * r + c, c % SLOTS
                if c >= SLOTS:
                    sp.wait_ge(sT_done, ONE + HU * (i - SLOTS + 1))
                    sp.wait_ge(pv_done, ONE + NS * (i - SLOTS + 1))
                for tile, n, blocks in ((qs, 0, (0, 0, 1)), (ks, 1, (0, 1, 0))):
                    for b, part in enumerate(blocks):
                        src = parts[n][part][bass.ds(i, 1)].rearrange("i (c d) (n t) -> (i d) n c t", d=DH, n=NG)
                        sp.dma_start(tile[a][BL * b:BL * b + DH].bitcast(F32).rearrange("p n (c t) -> p n c t", c=PC),
                                     src).then_inc(qk_in[a], 16)
                sp.dma_start(v[a][:].rearrange("p n q r -> p (n q r)"),
                             values[bass.ds(i, 1)].rearrange("i p f -> (i p) f")).then_inc(v_in[a], 16)

            for c in range(SLOTS):
                load(0, c)
            with sp.Fori(0, NP // SLOTS - 1) as r:
                for c in range(SLOTS, 2 * SLOTS):
                    load(r, c)
            for c in range(NP // SLOTS * SLOTS, NP):
                load(0, c)

        @block.vector
        def _(dve):
            def step(r, c):
                i = SLOTS * r + c
                before = FULL * SLOTS * r + uses_before(c)
                for n, (kind, arg, _) in enumerate(step_uses(c)):
                    use = before + n
                    slot = b_s[(uses_before(c) + n) % 2]
                    dve.wait_ge(use_done, ONE + use + 1)
                    if kind == "scores":
                        gr, q = arg // QT, arg % QT
                        nc.vector.tensor_reduce(nmax[:, gr, ST + q:ST + q + 1], slot[:], axis=AX.X, op=ALU.max,
                                                negate=True).then_inc(use_read, 1)
                    elif kind == "maxima":
                        of = c - 1 if arg == NG - 1 else c
                        if of > 0:
                            dve.wait_ge(fold_ready, ONE + NG * (SLOTS * r + of - 1) + arg + 1)
                        nc.vector.tensor_copy(max_rows[ST:P, arg], slot[ST:P, 0:P]).then_inc(use_read, 1)
                    elif kind == "context":
                        src = slot[:].rearrange("p (q n r) -> p q n r", n=NG, r=BL)
                        nc.vector.reciprocal(rsum[:], src[:, :, :, DH]).then_inc(rsum_ready, 1)
                        dve.wait_ge(rsum_ready, ONE + i - 1)
                        nc.vector.tensor_tensor(ctxn[:].rearrange("p n q d -> p q n d"), src[:, :, :, 0:DH],
                                                rsum[:].unsqueeze(3).broadcast_to([P, QT, NG, DH]), ALU.mult).then_inc(use_read, 1)
                    elif kind == "contextT":
                        for s in range(2):
                            last = nc.vector.tensor_copy(ctxT[:, s].rearrange("p a (n t) -> p n a t", t=GT),
                                                         slot[:, 2 * P * s:2 * P * (s + 1)].rearrange("p (n a t) -> p n a t", a=A, t=GT))
                        last.then_inc(use_read, 1)
                    else:
                        t = 2 * (i - 2) + arg
                        xt = g.x[:, bass.ds(t, 1), :].rearrange("p o d -> p (o d)")
                        nc.vector.tensor_tensor(xt, slot[:, 0:D], xt, ALU.add).then_inc(use_read, 1)
                        dve.wait_ge(use_read, ONE + use + 1)
                        nc.vector.bn_stats(g.stats[:, bass.ds(t, 1), :], xt).then_inc(stats_ready, 1)

            steps(dve, step)

        @block.gpsimd
        def _(pool):
            def fold(r, c, n):
                step_of = c + 1 if n == NG - 1 else c
                pool.wait_ge(use_read, ONE + FULL * SLOTS * r + use_at(step_of, "maxima", n) + 1)
                nc.gpsimd.tensor_tensor(qs[c % SLOTS][ST:P, n].rearrange("p (t q) -> p t q", t=QT),
                                        max_rows[ST:P, n].unsqueeze(1).broadcast_to([P - ST, QT, P]),
                                        tile_rows[ST:P], ALU.mult).then_inc(fold_ready, 1)

            def step(r, c):
                if 1 <= c <= NP:
                    fold(r, c - 1, NG - 1)
                if c < NP:
                    for n in range(NG - 1):
                        fold(r, c, n)

            steps(pool, step)

        @block.scalar
        def _(act):
            def step(r, c):
                for unit, pc in back_units(c):
                    pair = SLOTS * r + pc
                    if 0 <= pc < NP:
                        for h in (2 * unit, 2 * unit + 1):
                            k, n = h // NG, h % NG
                            act.wait_ge(sT_done, ONE + HU * pair + h + 1)
                            if n == 0 and NS * pc + k >= SETS:
                                act.wait_ge(pv_done, ONE + NS * pair + k - SETS + 1)
                            nc.scalar.activation(probT[(NS * pc + k) % SETS][n][:], b_t[h % 2][:], ACT.Exp,
                                                 scale=SCALE).then_inc(exp_ready, 1)
                    if unit == 0 and c >= 2:
                        i = SLOTS * r + c - 2
                        act.wait_ge(pv_done, ONE + NS * i + NS)
                        if c > 2:
                            act.wait_ge(use_read, ONE + FULL * SLOTS * r + use_at(c - 1, "context", 0) + 1)
                        nc.scalar.activation(o[:], b_o[:], ACT.Copy).then_inc(o_ready, 1)

            steps(act, step)

        @block.tensor
        def _(pe):
            def use(r, c, n, kind, arg):
                at = uses_before(c) + n
                before = FULL * SLOTS * r
                slot = b_s[at % 2]
                if at >= 2:
                    pe.wait_ge(use_read, ONE + before + at - 1)
                if kind == "scores":
                    a, gr, q = c % SLOTS, arg // QT, arg % QT
                    if arg == 0:
                        pe.wait_ge(qk_in[a], ONE + 16 * 6 * (r + c // SLOTS + 1))
                    for hf in range(L // HALF):
                        last = nc.tensor.matmul(slot[:, HALF * hf:HALF * (hf + 1)], qs[a][0:ST, gr, P * q:P * (q + 1)],
                                                ks[a][0:ST, gr, HALF * hf:HALF * (hf + 1)], start=True, stop=True)
                elif kind == "maxima":
                    of = c - 1 if arg == NG - 1 else c
                    pe.wait_ge(use_read, ONE + before + use_at(of, "scores", QT * (arg + 1) - 1) + 1)
                    last = nc.tensor.transpose(slot[:, 0:P], nmax[:, arg, :], g.ident[:])
                elif kind == "context":
                    pe.wait_ge(o_ready, ONE + SLOTS * r + c - 1)
                    for q in range(QT):
                        last = nc.tensor.transpose(slot[:, P * q:P * (q + 1)], o[:, P * q:P * (q + 1)], g.ident[:])
                elif kind == "contextT":
                    pe.wait_ge(use_read, ONE + before + use_at(c, "context", 0) + 1)
                    for gr in range(NG):
                        last = nc.tensor.transpose(slot[:, P * gr:P * (gr + 1)], ctxn[:, gr].rearrange("p q d -> p (q d)"), g.ident[:])
                else:
                    pe.wait_ge(use_read, ONE + before + use_at(c, "contextT", 0) + 1)
                    for a in range(A):
                        last = nc.tensor.matmul(slot[:, 0:D], ctxT[:, arg, a, :], wo[:, a, :],
                                                start=(a == 0), stop=(a == A - 1))
                last.then_inc(use_done, 1)

            def scores_T(r, c, unit):
                pair, a = SLOTS * r + c, c % SLOTS
                for h in (2 * unit, 2 * unit + 1):
                    k, hf, n = h // NG // 2, h // NG % 2, h % NG
                    if h < NG:
                        pe.wait_ge(fold_ready, ONE + NG * pair + n + 1)
                    if c > 0 or h >= 2:
                        pe.wait_ge(exp_ready, ONE + HU * pair + h - 1)
                    nc.tensor.matmul(b_t[h % 2][:], ks[a][:, n, P * k:P * (k + 1)], qs[a][:, n, HALF * hf:HALF * (hf + 1)],
                                     start=True, stop=True).then_inc(sT_done, 1)

            def weigh(r, c, k):
                pair, a = SLOTS * r + c, c % SLOTS
                kt, hf = k // 2, k % 2
                pe.wait_ge(exp_ready, ONE + HU * pair + NG * (k + 1))
                if k == 0:
                    pe.wait_ge(v_in[a], ONE + 16 * (r + c // SLOTS + 1))
                    if c > 0:
                        pe.wait_ge(o_ready, ONE + pair)
                for n in range(NG):
                    last = nc.tensor.matmul(b_o[BL * n:BL * (n + 1), HALF * hf:HALF * (hf + 1)], v[a][:, n, kt, :],
                                            probT[(NS * c + k) % SETS][n][:], start=(kt == 0), stop=(kt == QT - 1))
                last.then_inc(pv_done, 1)

            def step(r, c):
                uses, back = list(enumerate(step_uses(c))), back_units(c)
                for u in range(0, U, 2):
                    unit, pc = back[u]
                    if 0 <= pc < NP:
                        scores_T(r, pc, unit)
                    if unit:
                        if 0 <= pc < NP:
                            weigh(r, pc, unit // 2 - 1)
                    elif c >= 2:
                        weigh(r, c - 2, NS - 1)
                    for n, (kind, arg, at) in uses:
                        if at == u and kind != "scores":
                            use(r, c, n, kind, arg)
                    if 0 <= pc < NP:
                        scores_T(r, pc, unit + 1)
                    for n, (kind, arg, at) in uses:
                        if at in (u, u + 1) and kind == "scores":
                            use(r, c, n, kind, arg)

            pe.wait_ge(w_in, ONE + 16 * QT)
            steps(pe, step)


def norm_residual(nc, g, x_kept):
    C, SL = 4, 4
    with phase(nc) as (e, semaphore, begin):
        sb = lambda n, shape, dt=F32: e.enter_context(nc.sbuf_tensor(f"nr_{n}", shape, dt))
        sem = lambda n: semaphore(f"nr_{n}")
        gamma, beta = sb("gamma", [P, D]), sb("beta", [P, D])
        scaled = [sb(f"scaled{s}", [P, C, D]) for s in range(2)]
        xb = [sb(f"xb{s}", [P, C, D]) for s in range(SL)]
        w_in, xb_ready, scaled_ready, x_ready, stats_ready = [sem(n) for n in (
            "w_in", "xb_ready", "scaled_ready", "x_ready", "stats_ready")]
        xb_in = [sem(f"xb_in{s}") for s in range(SL)]
        block = begin()

        @block.sync
        def _(sp):
            for w, src in ((gamma, g.ins["L1_attn_gamma"]), (beta, g.ins["L1_attn_beta"])):
                sp.dma_start(w[:], src.rearrange("(o n) -> o n", o=1).broadcast_to([P, D])).then_inc(w_in, 16)
            src = x_kept.rearrange("(i c p) d -> i p c d", c=C, p=P)
            for n in range(T // C):
                if n >= SL:
                    sp.wait_ge(x_ready, ONE + C * (n - SL + 1))
                sp.dma_start(xb[n % SL][:], src[n]).then_inc(xb_in[n % SL], 16)

        @block.gpsimd
        def _(pool):
            pool.wait_ge(w_in, ONE + 32)
            for n in range(T // C):
                pool.wait_ge(xb_in[n % SL], ONE + 16 * (n // SL + 1))
                nc.gpsimd.tensor_tensor(xb[n % SL][:], xb[n % SL][:], beta[:].unsqueeze(1).broadcast_to([P, C, D]),
                                        ALU.add).then_inc(xb_ready, 1)

        @block.vector
        def _(dve):
            dve.wait_ge(w_in, ONE + 32)
            for n in range(T // C):
                for c in range(C):
                    t = C * n + c
                    nc.vector.scalar_tensor_tensor(scaled[n % 2][:, c, :], g.x[:, t, :], g.mean[:, t:t + 1], gamma[:],
                                                   ALU.subtract, ALU.mult).then_inc(scaled_ready, 1)
                dve.wait_ge(xb_ready, ONE + n + 1)
                for c in range(C):
                    t = C * n + c
                    dve.wait_ge(scaled_ready, ONE + t + 1)
                    nc.vector.scalar_tensor_tensor(g.x[:, t, :], scaled[n % 2][:, c, :], g.rstd[:, t:t + 1], xb[n % SL][:, c, :],
                                                   ALU.mult, ALU.add).then_inc(x_ready, 1)
                for c in range(C):
                    t = C * n + c
                    dve.wait_ge(x_ready, ONE + t + 1)
                    nc.vector.bn_stats(g.stats[:, t, :], g.x[:, t, :]).then_inc(stats_ready, 1)


def attention1(nc, g):
    dram = lambda n, shape: nc.dram_tensor(n, shape, F32, kind="Internal").ap()
    parts = [[dram(f"{n}_{part}", [NP, D, 2 * P]) for part in ("rounded", "rest")] for n in ("queries", "keys")]
    values, x_kept = dram("values", [NP, P, NG * QT * BL]), dram("x_kept", [N, D])
    with ExitStack() as e:
        sb = lambda n, shape, dt=F32: e.enter_context(nc.sbuf_tensor(f"a1_{n}", shape, dt))
        qs, ks = [[sb(f"{n}{a}", [P, NG, L], F32R) for a in range(3)] for n in ("qs", "ks")]
        nmax = sb("nmax", [P, NG, P])
        tile_rows = sb("tile_rows", [P, QT, P])
        project_groups(nc, g, parts, values, x_kept, qs, ks, nmax, tile_rows)
        group_attention(nc, g, parts, values, qs, ks, nmax, tile_rows)
    finish_stats(nc, g, "ln3")
    norm_residual(nc, g, x_kept)


SINKHORN_ITERS, CLIP = 8, 1e-6


def sinkhorn(nc, g, logits, gates):
    E = logits.shape[2]
    with phase(nc) as (e, semaphore, begin):
        sb = lambda n, shape, dt=F32: e.enter_context(nc.sbuf_tensor(f"sk_{n}", shape, dt))
        sem = lambda n: semaphore(f"sk_{n}")
        ones = sb("ones", [P, P])
        p = sb("p", [P, B, TB, E])
        token_sum, expert_sum = sb("token_sum", [P, B, E]), sb("expert_sum", [P, B, TB])
        ones_set, step, p_ready, sums_done = sem("ones_set"), sem("step"), sem("p_ready"), sem("sums_done")
        bank = g.bank[0]
        block = begin()

        @block.gpsimd
        def _(pool):
            nc.gpsimd.memset(ones[:], 1.0).then_inc(ones_set, 1)

        @block.tensor
        def _(pe):
            pe.wait_ge(ones_set, ONE + 1)
            for n in range(SINKHORN_ITERS):
                pe.wait_ge(p_ready, ONE + n + 1)
                nc.tensor.matmul(bank[:, 0:T * E], ones[:], p[:].rearrange("p b q e -> p (b q e)"),
                                 start=True, stop=True).then_inc(sums_done, 1)

        @block.vector
        def _(dve):
            link = Chain(dve, step)
            nc.vector.tensor_scalar(p[:].rearrange("p b q e -> p (b q) e"), logits[:], CLIP, None, ALU.max).then_inc(p_ready, 1)
            for n in range(SINKHORN_ITERS):
                dve.wait_ge(sums_done, ONE + n + 1)
                link(nc.vector.tensor_reduce(token_sum[:], bank[:, 0:T * E].rearrange("p (b q e) -> p b e q", b=B, q=TB),
                                             axis=AX.X, op=ALU.add))
                link(nc.vector.reciprocal(token_sum[:], token_sum[:]))
                link(nc.vector.tensor_tensor(p[:], p[:], token_sum[:].unsqueeze(2).broadcast_to([P, B, TB, E]), ALU.mult))
                link(nc.vector.tensor_reduce(expert_sum[:], p[:], axis=AX.X, op=ALU.add))
                link(nc.vector.reciprocal(expert_sum[:], expert_sum[:]))
                last = n == SINKHORN_ITERS - 1
                dst = gates[:].rearrange("p q b e -> p b q e") if last else p[:]
                nc.vector.tensor_tensor(dst, p[:], expert_sum[:].unsqueeze(3).broadcast_to([P, B, TB, E]),
                                        ALU.mult).then_inc(p_ready, 1)


def top_tokens(nc, g, gates, index, value, place):
    E = gates.shape[3]
    BE, M = B * E, S // E
    ROUNDS = M // 8
    with phase(nc) as (e, semaphore, begin):
        sb = lambda n, shape, dt=F32: e.enter_context(nc.sbuf_tensor(f"tt_{n}", shape, dt))
        sem = lambda n: semaphore(f"tt_{n}")
        left = [sb(f"left{k}", [BE, S]) for k in range(2)]
        top, top_at = sb("top", [BE, M]), sb("top_at", [BE, M], U32)
        top_at_f = sb("top_at_f", [BE, M])
        indexT = sb("indexT", [M, BE])
        batch_row = sb("batch_row", [M, B, E])
        token = sb("token", [M, S], F16)
        rank1 = sb("rank1", [M, 1], BF16)
        expert = sb("expert", [P, E])
        tile_base = sb("tile_base", [P, B, TB])
        is_token = [sb(f"is_token{k}", [M, S], BF16) for k in range(2)]
        key = sb("key", [P, B, E, TB])
        best, best_i = sb("best", [P, T]), sb("best_i", [P, T], I32)
        best_e, best_r = sb("best_e", [P, T], I32), sb("best_r", [P, T], I32)
        row, has = sb("row", [P, T]), sb("has", [P, T])
        consts, gT_done, step, top_ready, topT_done, topT_ready = [sem(n) for n in (
            "consts", "gT_done", "step", "top_ready", "topT_done", "topT_ready")]
        is_ready, rank_done = sem("is_ready"), sem("rank_done")
        b_g, b_t, b_r = g.bank2[0], g.bank[2], g.bank[3]
        block = begin()

        @block.gpsimd
        def _(pool):
            io = dict(allow_small_or_imprecise_dtypes=True)
            nc.gpsimd.iota(token[:], pattern=[[1, S]], base=0, channel_multiplier=0, **io)
            nc.gpsimd.iota(rank1[:], pattern=[[0, 1]], base=1, channel_multiplier=1, **io)
            nc.gpsimd.iota(expert[:], pattern=[[1, E]], base=0, channel_multiplier=0, **io)
            nc.gpsimd.iota(batch_row[:], pattern=[[S, B], [0, E]], base=0, channel_multiplier=0, **io)
            nc.gpsimd.iota(tile_base[:], pattern=[[E * M, B], [0, TB]], base=-1, channel_multiplier=0, **io).then_inc(consts, 1)

        @block.tensor
        def _(pe):
            for q in range(TB):
                last = nc.tensor.transpose(b_g[0:BE, P * q:P * (q + 1)], gates[:, q].rearrange("p b e -> p (b e)"), g.ident[:])
            last.then_inc(gT_done, 1)
            pe.wait_ge(top_ready, ONE + 1)
            nc.tensor.transpose(b_t[:, 0:BE], top[:], g.ident[0:BE, 0:BE])
            nc.tensor.transpose(b_t[:, BE:2 * BE], top_at_f[:], g.ident[0:BE, 0:BE]).then_inc(topT_done, 1)
            pe.wait_ge(consts, ONE + 1)
            for n in range(BE):
                pe.wait_ge(is_ready, ONE + n + 1)
                for q in range(TB):
                    last = nc.tensor.matmul(b_r[:, TB * n + q:TB * n + q + 1], is_token[n % 2][:, P * q:P * (q + 1)],
                                            rank1[:], start=True, stop=True)
                last.then_inc(rank_done, 1)

        @block.vector
        def _(dve):
            link = Chain(dve, step)
            dve.wait_ge(gT_done, ONE + 1)
            link(nc.vector.tensor_copy(left[0][:], b_g[0:BE, :]))
            for r in range(ROUNDS):
                eight = slice(8 * r, 8 * r + 8)
                link(nc.vector.max(out=top[:, eight], in_=left[r % 2][:]))
                link(nc.vector.max_index(out=top_at[:, eight], in_max=top[:, eight], in_values=left[r % 2][:]))
                if r < ROUNDS - 1:
                    link(nc.vector.match_replace(out=left[(r + 1) % 2][:], in_to_replace=top[:, eight],
                                                 in_values=left[r % 2][:], imm_value=-1.0))
            nc.vector.tensor_copy(top_at_f[:], top_at[:]).then_inc(top_ready, 1)
            dve.wait_ge(topT_done, ONE + 1)
            nc.vector.tensor_copy(value[:], b_t[:, 0:BE])
            link(nc.vector.tensor_copy(indexT[:], b_t[:, BE:2 * BE]))
            dve.wait_ge(consts, ONE + 1)
            nc.vector.tensor_tensor(index[:], indexT[:], batch_row[:].rearrange("p b e -> p (b e)"), ALU.add)
            for n in range(BE):
                if n >= 2:
                    dve.wait_ge(rank_done, ONE + n - 1)
                nc.vector.tensor_scalar(is_token[n % 2][:], token[:], indexT[:, n:n + 1], None, ALU.is_equal).then_inc(is_ready, 1)
            dve.wait_ge(rank_done, ONE + BE)
            link(nc.vector.tensor_scalar(key[:].rearrange("p b e q -> p (b e q)"), b_r[:, 0:BE * TB], float(E), None, ALU.mult))
            link(nc.vector.tensor_tensor(key[:], key[:], expert[:].unsqueeze(1).unsqueeze(3).broadcast_to([P, B, E, TB]), ALU.add))
            link(nc.vector.tensor_reduce(best[:].rearrange("p (b q) -> p b q", b=B), key[:].rearrange("p b e q -> p b q e"),
                                         axis=AX.X, op=ALU.max))
            link(nc.vector.tensor_copy(best_i[:], best[:]))
            link(nc.vector.tensor_scalar(best_e[:], best_i[:], E - 1, None, ALU.bitwise_and))
            link(nc.vector.tensor_scalar(best_r[:], best_i[:], E.bit_length() - 1, None, ALU.logical_shift_right))
            link(nc.vector.scalar_tensor_tensor(row[:], best_e[:], float(M), best_r[:], ALU.mult, ALU.add))
            link(nc.vector.tensor_tensor(row[:], row[:], tile_base[:].rearrange("p b q -> p (b q)"), ALU.add))
            link(nc.vector.tensor_scalar(has[:], best_r[:], 0.0, None, ALU.is_gt))
            link(nc.vector.scalar_tensor_tensor(row[:], row[:], float(-N), has[:], ALU.add, ALU.mult))
            link(nc.vector.tensor_scalar(place[:], row[:], float(N), None, ALU.add))


def routed_experts(nc, g, rows, outputs, index, value, place, out):
    E = g.ins["L1_ffn_experts"].shape[0]
    BE, M = B * E, S // E
    SL = 4
    with phase(nc) as (e, semaphore, begin):
        sb = lambda n, shape, dt=F32: e.enter_context(nc.sbuf_tensor(f"re_{n}", shape, dt))
        sem = lambda n: semaphore(f"re_{n}")
        w = sb("w", [P, E, KD, D])
        taken = [sb(f"taken{s}", [M, D]) for s in range(SL)]
        takenT = [sb(f"takenT{s}", [P, KD, M]) for s in range(SL)]
        y = [sb(f"y{s}", [M, D]) for s in range(SL)]
        zero = sb("zero", [P, D])
        w_in, zero_set, zero_kept = sem("w_in"), sem("zero_set"), sem("zero_kept")
        taken_in = [semaphore(f"re_taken_in{s}", 0) for s in range(SL)]
        kept = [sem(f"kept{s}") for s in range(SL)]
        t_done, t_ready, y_done, y_ready = [sem(n) for n in ("t_done", "t_ready", "y_done", "y_ready")]
        b_t, b_y = g.bank[0:SL], g.bank[SL:2 * SL]
        block = begin()

        @block.sync
        def _(sp):
            sp.dma_start(w[:], g.ins["L1_ffn_experts"].rearrange("e (k p) n -> p e k n", p=P)).then_inc(w_in, 16)
            sp.wait_ge(zero_set, ONE + 1)
            sp.dma_start(outputs[N:N + P, :], zero[:]).then_inc(zero_kept, 16)
            dst = outputs[0:N, :].rearrange("(b e m) d -> b e m d", b=B, e=E)
            with sp.Fori(0, B) as b:
                for n in range(E):
                    sp.wait_ge(y_ready, ONE + b * E + n + 1)
                    sp.dma_start(dst[bass.ds(b, 1), n, :, :].rearrange("b m d -> (b m) d"), y[n % SL][:]).then_inc(kept[n % SL], 16)
            sp.wait_ge(zero_kept, ONE + 16)
            for s in range(SL):
                sp.wait_ge(kept[s], ONE + 16 * BE // SL)

        @block.gpsimd
        def _(pool):
            nc.gpsimd.memset(zero[:], 0.0).then_inc(zero_set, 1)
            for n in range(BE):
                if n >= SL:
                    pool.wait_ge(t_done, ONE + n - SL + 1)
                nc.gpsimd.indirect_dma_start(out=taken[n % SL][:], out_offset=None, in_=rows,
                                             in_offset=bass.IndirectOffsetOnAxis(ap=index[:, n:n + 1], axis=0)
                                             ).then_inc(taken_in[n % SL], 16)

        @block.tensor
        def _(pe):
            pe.wait_ge(w_in, ONE + 16)
            with pe.Fori(0, B) as b:
                for n in range(E):
                    s, at = n % SL, b * E + n
                    pe.wait_ge(taken_in[s], 16 * (E // SL) * b + 16 * (n // SL + 1))
                    if n >= SL:
                        pe.wait_ge(t_ready, ONE + at - SL + 1)
                    else:
                        pe.wait_ge(t_ready, ONE + b * E)
                    for k in range(KD):
                        last = nc.tensor.transpose(b_t[s][:, M * k:M * (k + 1)], taken[s][:, P * k:P * (k + 1)], g.ident[:])
                    last.then_inc(t_done, 1)
                    pe.wait_ge(t_ready, ONE + at + 1)
                    if n >= SL:
                        pe.wait_ge(y_ready, ONE + at - SL + 1)
                    else:
                        pe.wait_ge(y_ready, ONE + b * E)
                    for k in range(KD):
                        last = nc.tensor.matmul(b_y[s][:, 0:D], takenT[s][:, k, :], w[:, n, k, :],
                                                start=(k == 0), stop=(k == KD - 1))
                    last.then_inc(y_done, 1)

        @block.scalar
        def _(act):
            with act.Fori(0, B) as b:
                for n in range(E):
                    s, at = n % SL, b * E + n
                    act.wait_ge(t_done, ONE + at + 1)
                    if n >= SL:
                        act.wait_ge(y_done, ONE + at - SL + 1)
                    else:
                        act.wait_ge(y_done, ONE + b * E)
                    nc.scalar.activation(takenT[s][:], b_t[s][:, 0:KD * M].rearrange("p (k m) -> p k m", k=KD),
                                         ACT.Copy).then_inc(t_ready, 1)

        @block.vector
        def _(dve):
            with dve.Fori(0, B) as b:
                for n in range(E):
                    s, at = n % SL, b * E + n
                    dve.wait_ge(y_done, ONE + at + 1)
                    if n >= SL:
                        dve.wait_ge(kept[s], ONE + 16 * (E // SL) * b + 16 * (n // SL))
                    else:
                        dve.wait_ge(kept[s], ONE + 16 * (E // SL) * b)
                    nc.vector.tensor_scalar(y[s][:], b_y[s][:, 0:D], value[:, bass.ds(at, 1)], None, ALU.mult).then_inc(y_ready, 1)
    with phase(nc) as (e, semaphore, begin):
        sem = lambda n: semaphore(f"rb_{n}")
        got = [e.enter_context(nc.sbuf_tensor(f"rb_got{s}", [P, D], F32)) for s in range(SL)]
        got_in = [semaphore(f"rb_got_in{s}", 0) for s in range(SL)]
        x_ready, out_done = sem("x_ready"), sem("out_done")
        block = begin()

        @block.gpsimd
        def _(pool):
            for t in range(T):
                if t >= SL:
                    pool.wait_ge(x_ready, ONE + t - SL + 1)
                nc.gpsimd.indirect_dma_start(out=got[t % SL][:], out_offset=None, in_=outputs,
                                             in_offset=bass.IndirectOffsetOnAxis(ap=place[:, t:t + 1], axis=0)
                                             ).then_inc(got_in[t % SL], 16)

        @block.vector
        def _(dve):
            with dve.Fori(0, T // SL) as i:
                for s in range(SL):
                    xt = g.x[:, bass.ds(SL * i + s, 1), :].rearrange("p o d -> p (o d)")
                    dve.wait_ge(got_in[s], 16 * i + 16)
                    nc.vector.tensor_tensor(xt, got[s][:], xt, ALU.add).then_inc(x_ready, 1)

        @block.sync
        def _(sp):
            dst = out.rearrange("b (t p) d -> (b t) p d", p=P)
            with sp.Fori(0, T) as t:
                sp.wait_ge(x_ready, ONE + t + 1)
                sp.dma_start(dst[bass.ds(t, 1), :, :].rearrange("t p d -> (t p) d"),
                             g.x[:, bass.ds(t, 1), :].rearrange("p o d -> p (o d)")).then_inc(out_done, 16)
            sp.wait_ge(out_done, ONE + 16 * T)


def mixture1(nc, g, out):
    E = g.ins["L1_ffn_gate_w"].shape[1]
    BE, M = B * E, S // E
    rows = nc.dram_tensor("routed_rows", [N, D], F32, kind="Internal").ap()
    outputs = nc.dram_tensor("routed_outputs", [N + P, D], F32, kind="Internal").ap()
    with ExitStack() as e:
        sb = lambda n, shape, dt=F32: e.enter_context(nc.sbuf_tensor(f"m1_{n}", shape, dt))
        logits = sb("logits", [P, T, E])
        gates = sb("gates", [P, TB, B, E])
        index, value, place = sb("index", [M, BE], U32), sb("value", [M, BE]), sb("place", [P, T], U32)
        normalised_tiles(nc, g, "np1", g.ins["L1_ffn_gate_w"], None, logits, rows)
        sinkhorn(nc, g, logits, gates)
        top_tokens(nc, g, gates, index, value, place)
        routed_experts(nc, g, rows, outputs, index, value, place, out)


def program(nc, g, out, stop=""):
    setup(nc, g)
    finish_stats(nc, g, "ln0")
    E = g.ins["L0_ffn_rw1"].shape[0]
    sorted_rows = nc.dram_tensor("sorted_rows", [(2 * T + E) * P, D], F32, kind="Internal").ap()
    window_attention(nc, g, sorted_rows)
    if stop == "A":
        return
    finish_stats(nc, g, "ln1")
    mixture0(nc, g, sorted_rows)
    if stop == "B":
        return
    finish_stats(nc, g, "ln2")
    attention1(nc, g)
    if stop == "C":
        return
    finish_stats(nc, g, "ln4")
    mixture1(nc, g, out)


_INS = ['L0_attn_x', 'L0_attn_W_qkv', 'L0_attn_W_out', 'L0_ffn_gate_w', 'L0_ffn_gate_b', 'L0_ffn_rw1', 'L0_ffn_rb1',
        'L0_ffn_rw2', 'L0_ffn_rb2', 'L0_ffn_rw3', 'L0_ffn_rb3', 'L0_ffn_sw1', 'L0_ffn_sb1', 'L0_ffn_sw2', 'L0_ffn_sb2',
        'L0_ffn_sw3', 'L0_ffn_sb3', 'L1_attn_wq', 'L1_attn_bq', 'L1_attn_wk', 'L1_attn_bk', 'L1_attn_wv', 'L1_attn_bv',
        'L1_attn_wo', 'L1_attn_bo', 'L1_attn_gamma', 'L1_attn_beta', 'L1_ffn_gate_w', 'L1_ffn_experts']


def kernel(**inputs):
    import numpy as _np
    import concourse.bacc as _bacc
    from concourse import mybir as _mybir
    from concourse.bass_utils import run_bass_kernel_spmd as _run

    nc = _bacc.Bacc("TRN2", target_bir_lowering=False, num_devices=1)
    arrays, aps = {}, {}
    for name in _INS:
        a = _np.ascontiguousarray(inputs[name])
        arrays[f"in_{name}_dram"] = a
        aps[name] = nc.dram_tensor(f"in_{name}_dram", a.shape, _mybir.dt.from_np(a.dtype), kind="ExternalInput").ap()
    out = nc.dram_tensor("out_0_dram", (B, S, D), F32, kind="ExternalOutput").ap()
    with ExitStack() as ctx:
        program(nc, Shared(ctx, aps), out)
    r = _run(nc, [arrays], core_ids=[0])
    return r.results[0]["out_0_dram"]
```
